# Optimizing a Trainium2 kernel written in Bass

```python
import numpy as np
import jax
import jax.numpy as jnp

def _softmax(x, axis=-1):
    return jax.nn.softmax(x, axis=axis)

def _gelu(x):
    return jax.nn.gelu(x, approximate=True)

def _silu(x):
    return jax.nn.silu(x)

def _sigmoid(x):
    return jax.nn.sigmoid(x)

def _layernorm(x, axis=-1, eps=1e-05):
    m = jnp.mean(x, axis=axis, keepdims=True)
    v = jnp.var(x, axis=axis, keepdims=True)
    return (x - m) / jnp.sqrt(v + eps)

def _scatter_add(tgt, idx, src, axis=0):
    return tgt.at[idx].add(src)

def _segment_sum(src, seg, n):
    return jax.ops.segment_sum(src, seg, n)
kernel_name = 'mk_gnn_preln_d2_gnn_r8_8e5467'

def setup_inputs(seed: int=0):
    np.random.seed(seed)
    _w = jnp.asarray

    def _rec_inputs():
        import jax
        import jax.numpy as jnp
        _gk = jax.random.key(seed)
        x = 8.953e-05 + 1 * jax.random.normal(jax.random.fold_in(_gk, 1), (12500, 16), jnp.float32)
        src = jax.random.randint(jax.random.fold_in(_gk, 2), (400000,), 0, 12500, jnp.int32)
        dst = jnp.minimum((12500 * jax.random.uniform(jax.random.fold_in(_gk, 3), (400000,)) ** 2.0).astype(jnp.int32), 99999)
        _o = jnp.argsort(dst, stable=True)
        src = src[_o]
        dst = dst[_o]
        edge_attr_3 = -1.09012e-05 + 0.99985 * jax.random.normal(jax.random.fold_in(_gk, 11), (400000, 3), jnp.float32)
        edge_attr_48 = -3.69585e-06 + 0.999911 * jax.random.normal(jax.random.fold_in(_gk, 12), (400000, 48), jnp.float32)
        edge_attr_8 = -5.3897e-05 + 0.999841 * jax.random.normal(jax.random.fold_in(_gk, 13), (400000, 8), jnp.float32)
        node_vec1 = -0.00472126 + 0.997171 * jax.random.normal(jax.random.fold_in(_gk, 15), (12500, 1), jnp.float32)
        return (x, src, dst, edge_attr_3, edge_attr_48, edge_attr_8, node_vec1)
    x, src, dst, edge_attr_3, edge_attr_48, edge_attr_8, node_vec1 = _rec_inputs()

    def _L0_gnn_setup():
        import jax, jax.numpy as jnp
        import numpy as np
        NS, NV = (16, 4)
        EPS = 1e-05
        N_NODES, N_EDGES = (5000, 50000)

        def _bn_scalar(x, g, b):
            m = x.mean(0)
            v = ((x - m) ** 2).mean(0)
            return (x - m) / jnp.sqrt(v + EPS) * g + b

        def _seg_mean(x, idx, n):
            s = jax.ops.segment_sum(x, idx, num_segments=n)
            c = jax.ops.segment_sum(jnp.ones((idx.shape[0],), x.dtype), idx, num_segments=n)
            return s / jnp.maximum(c, 1.0)[:, None]

        def _edge_weights(edge_attr, w1, b1, w2, b2):
            h = jax.nn.relu(edge_attr @ w1 + b1)
            return h @ w2 + b2

        def _forward(node_attr, edge_attr, edge_vec, fc0_w1, fc0_b1, fc0_w2, fc0_b2, fc1_w1, fc1_b1, fc1_w2, fc1_b2, bn0_gs, bn0_bs, bn0_gv, bn1_gs, bn1_bs, edge_index):
            N = node_attr.shape[0]
            E = edge_attr.shape[0]
            src, dst = (edge_index[0], edge_index[1])
            rhat = edge_vec / (jnp.linalg.norm(edge_vec, axis=-1, keepdims=True) + 1e-12)
            sh1 = rhat * float(np.sqrt(3.0))
            w = _edge_weights(edge_attr, fc0_w1, fc0_b1, fc0_w2, fc0_b2)
            wa = w[:, :NS * NS].reshape(E, NS, NS)
            wb = w[:, NS * NS:].reshape(E, NS, NV)
            x = node_attr[dst]
            inv = float(1.0 / np.sqrt(NS))
            msg_s = jnp.einsum('ei,eij->ej', x, wa) * inv
            msg_v = jnp.einsum('ei,eij,ec->ejc', x, wb, sh1) * inv
            msg = jnp.concatenate([msg_s, msg_v.reshape(E, NV * 3)], axis=-1)
            out = _seg_mean(msg, src, N)
            s0 = _bn_scalar(out[:, :NS], bn0_gs, bn0_bs)
            v0 = out[:, NS:].reshape(N, NV, 3)
            vn = jnp.sqrt((v0 ** 2).mean(axis=(0, 2)) + EPS)
            v0 = v0 / vn[None, :, None] * bn0_gv[None, :, None]
            w = _edge_weights(edge_attr, fc1_w1, fc1_b1, fc1_w2, fc1_b2)
            wa = w[:, :NS * NS].reshape(E, NS, NS)
            wb = w[:, NS * NS:].reshape(E, NV, NS)
            s = s0[dst]
            v = v0[dst]
            path_a = jnp.einsum('ei,eij->ej', s, wa)
            path_b = jnp.einsum('eic,ec,eij->ej', v, sh1, wb) * float(1.0 / np.sqrt(3.0))
            msg = (path_a + path_b) * float(1.0 / np.sqrt(NS + NV))
            node1 = _seg_mean(msg, src, N)
            return _bn_scalar(node1, bn1_gs, bn1_bs)
        key = jax.random.key(seed)
        ks = jax.random.split(key, 8)
        d = 3 * NS
        wn = NS * NS + NS * NV
        g = lambda k, shape, sc: jax.random.normal(k, shape, jnp.float32) * sc
        return {'node_attr': g(ks[0], (N_NODES, NS), 1.0), 'edge_attr': g(ks[1], (N_EDGES, d), 1.0), 'edge_vec': g(ks[2], (N_EDGES, 3), 1.0), 'fc0_w1': g(ks[3], (d, d), d ** (-0.5)), 'fc0_b1': jnp.zeros((d,), jnp.float32), 'fc0_w2': g(ks[4], (d, wn), d ** (-0.5)), 'fc0_b2': jnp.zeros((wn,), jnp.float32), 'fc1_w1': g(ks[5], (d, d), d ** (-0.5)), 'fc1_b1': jnp.zeros((d,), jnp.float32), 'fc1_w2': g(ks[6], (d, wn), d ** (-0.5)), 'fc1_b2': jnp.zeros((wn,), jnp.float32), 'bn0_gs': jnp.ones((NS,), jnp.float32), 'bn0_bs': jnp.zeros((NS,), jnp.float32), 'bn0_gv': jnp.ones((NV,), jnp.float32), 'bn1_gs': jnp.ones((NS,), jnp.float32), 'bn1_bs': jnp.zeros((NS,), jnp.float32), 'edge_index': jax.random.randint(ks[7], (2, N_EDGES), 0, N_NODES)}
    _L0_gnn_all = _L0_gnn_setup()
    _L0_gnn_in = {k: v for k, v in _L0_gnn_all.items() if k in ('fc0_w1', 'fc0_b1', 'fc0_w2', 'fc0_b2', 'fc1_w1', 'fc1_b1', 'fc1_w2', 'fc1_b2', 'bn0_gs', 'bn0_bs', 'bn0_gv', 'bn1_gs', 'bn1_bs')}
    del _L0_gnn_all

    def _L1_gnn_setup():
        import jax, jax.numpy as jnp
        import numpy as np
        N_NODES = 12500
        N_EDGES = 400000
        D_NODE = 16
        D_EDGE = 8
        D_HIDDEN = 16
        key = jax.random.key(seed)
        ks = jax.random.split(key, 8)
        node_features = jax.random.normal(ks[0], (N_NODES, D_NODE), dtype=jnp.float32)
        edge_attr_e3nn = jax.random.normal(ks[1], (N_EDGES, D_EDGE), dtype=jnp.float32)
        node_attr_scalar_raw = jax.random.normal(ks[2], (N_NODES, 1), dtype=jnp.float32)
        W_msg_tp = jax.random.normal(ks[3], (D_NODE, D_EDGE, D_HIDDEN), dtype=jnp.float32)
        W_msg_lin = jax.random.normal(ks[4], (D_HIDDEN, D_HIDDEN), dtype=jnp.float32)
        W_upd_tp = jax.random.normal(ks[5], (D_NODE, D_HIDDEN, D_HIDDEN), dtype=jnp.float32)
        W_upd_lin = jax.random.normal(ks[6], (D_HIDDEN, D_NODE), dtype=jnp.float32)
        edge_index = jax.random.randint(ks[7], (2, N_EDGES), 0, N_NODES, dtype=jnp.int64)
        return {'node_features': node_features, 'edge_attr_e3nn': edge_attr_e3nn, 'node_attr_scalar_raw': node_attr_scalar_raw, 'W_msg_tp': W_msg_tp, 'W_msg_lin': W_msg_lin, 'W_upd_tp': W_upd_tp, 'W_upd_lin': W_upd_lin, 'edge_index': edge_index}
    _L1_gnn_all = _L1_gnn_setup()
    _L1_gnn_in = {k: v for k, v in _L1_gnn_all.items() if k in ('W_msg_tp', 'W_msg_lin', 'W_upd_tp', 'W_upd_lin')}
    del _L1_gnn_all
    return {'x': x, 'src': src, 'dst': dst, 'edge_attr_3': edge_attr_3, 'edge_attr_48': edge_attr_48, 'edge_attr_8': edge_attr_8, 'node_vec1': node_vec1, 'L0_gnn_fc0_w1': _L0_gnn_in['fc0_w1'], 'L0_gnn_fc0_b1': _L0_gnn_in['fc0_b1'], 'L0_gnn_fc0_w2': _L0_gnn_in['fc0_w2'], 'L0_gnn_fc0_b2': _L0_gnn_in['fc0_b2'], 'L0_gnn_fc1_w1': _L0_gnn_in['fc1_w1'], 'L0_gnn_fc1_b1': _L0_gnn_in['fc1_b1'], 'L0_gnn_fc1_w2': _L0_gnn_in['fc1_w2'], 'L0_gnn_fc1_b2': _L0_gnn_in['fc1_b2'], 'L0_gnn_bn0_gs': _L0_gnn_in['bn0_gs'], 'L0_gnn_bn0_bs': _L0_gnn_in['bn0_bs'], 'L0_gnn_bn0_gv': _L0_gnn_in['bn0_gv'], 'L0_gnn_bn1_gs': _L0_gnn_in['bn1_gs'], 'L0_gnn_bn1_bs': _L0_gnn_in['bn1_bs'], 'L1_gnn_W_msg_tp': _L1_gnn_in['W_msg_tp'], 'L1_gnn_W_msg_lin': _L1_gnn_in['W_msg_lin'], 'L1_gnn_W_upd_tp': _L1_gnn_in['W_upd_tp'], 'L1_gnn_W_upd_lin': _L1_gnn_in['W_upd_lin']}

def reference(x, src, dst, edge_attr_3, edge_attr_48, edge_attr_8, node_vec1, L0_gnn_fc0_w1, L0_gnn_fc0_b1, L0_gnn_fc0_w2, L0_gnn_fc0_b2, L0_gnn_fc1_w1, L0_gnn_fc1_b1, L0_gnn_fc1_w2, L0_gnn_fc1_b2, L0_gnn_bn0_gs, L0_gnn_bn0_bs, L0_gnn_bn0_gv, L0_gnn_bn1_gs, L0_gnn_bn1_bs, L1_gnn_W_msg_tp, L1_gnn_W_msg_lin, L1_gnn_W_upd_tp, L1_gnn_W_upd_lin):
    import jax
    import jax.numpy as jnp

    def _L0_gnn_ref(node_attr, edge_attr, edge_vec, fc0_w1, fc0_b1, fc0_w2, fc0_b2, fc1_w1, fc1_b1, fc1_w2, fc1_b2, bn0_gs, bn0_bs, bn0_gv, bn1_gs, bn1_bs, edge_index):
        import jax, jax.numpy as jnp
        import numpy as np
        NS, NV = (16, 4)
        EPS = 1e-05
        N_NODES, N_EDGES = (5000, 50000)

        def _bn_scalar(x, g, b):
            m = x.mean(0)
            v = ((x - m) ** 2).mean(0)
            return (x - m) / jnp.sqrt(v + EPS) * g + b

        def _seg_mean(x, idx, n):
            s = jax.ops.segment_sum(x, idx, num_segments=n)
            c = jax.ops.segment_sum(jnp.ones((idx.shape[0],), x.dtype), idx, num_segments=n)
            return s / jnp.maximum(c, 1.0)[:, None]

        def _edge_weights(edge_attr, w1, b1, w2, b2):
            h = jax.nn.relu(edge_attr @ w1 + b1)
            return h @ w2 + b2

        def _forward(node_attr, edge_attr, edge_vec, fc0_w1, fc0_b1, fc0_w2, fc0_b2, fc1_w1, fc1_b1, fc1_w2, fc1_b2, bn0_gs, bn0_bs, bn0_gv, bn1_gs, bn1_bs, edge_index):
            N = node_attr.shape[0]
            E = edge_attr.shape[0]
            src, dst = (edge_index[0], edge_index[1])
            rhat = edge_vec / (jnp.linalg.norm(edge_vec, axis=-1, keepdims=True) + 1e-12)
            sh1 = rhat * float(np.sqrt(3.0))
            w = _edge_weights(edge_attr, fc0_w1, fc0_b1, fc0_w2, fc0_b2)
            wa = w[:, :NS * NS].reshape(E, NS, NS)
            wb = w[:, NS * NS:].reshape(E, NS, NV)
            x = node_attr[dst]
            inv = float(1.0 / np.sqrt(NS))
            msg_s = jnp.einsum('ei,eij->ej', x, wa) * inv
            msg_v = jnp.einsum('ei,eij,ec->ejc', x, wb, sh1) * inv
            msg = jnp.concatenate([msg_s, msg_v.reshape(E, NV * 3)], axis=-1)
            out = _seg_mean(msg, src, N)
            s0 = _bn_scalar(out[:, :NS], bn0_gs, bn0_bs)
            v0 = out[:, NS:].reshape(N, NV, 3)
            vn = jnp.sqrt((v0 ** 2).mean(axis=(0, 2)) + EPS)
            v0 = v0 / vn[None, :, None] * bn0_gv[None, :, None]
            w = _edge_weights(edge_attr, fc1_w1, fc1_b1, fc1_w2, fc1_b2)
            wa = w[:, :NS * NS].reshape(E, NS, NS)
            wb = w[:, NS * NS:].reshape(E, NV, NS)
            s = s0[dst]
            v = v0[dst]
            path_a = jnp.einsum('ei,eij->ej', s, wa)
            path_b = jnp.einsum('eic,ec,eij->ej', v, sh1, wb) * float(1.0 / np.sqrt(3.0))
            msg = (path_a + path_b) * float(1.0 / np.sqrt(NS + NV))
            node1 = _seg_mean(msg, src, N)
            return _bn_scalar(node1, bn1_gs, bn1_bs)
        return _forward(node_attr, edge_attr, edge_vec, fc0_w1, fc0_b1, fc0_w2, fc0_b2, fc1_w1, fc1_b1, fc1_w2, fc1_b2, bn0_gs, bn0_bs, bn0_gv, bn1_gs, bn1_bs, edge_index)

    def _L1_gnn_ref(node_features, edge_attr_e3nn, node_attr_scalar_raw, W_msg_tp, W_msg_lin, W_upd_tp, W_upd_lin, edge_index):
        import jax, jax.numpy as jnp
        import numpy as np
        N_NODES = 12500
        N_EDGES = 400000
        D_NODE = 16
        D_EDGE = 8
        D_HIDDEN = 16
        n_nodes = node_features.shape[0]
        row = edge_index[0]
        col = edge_index[1]
        norm_msg_tp = 1.0 / np.float32(np.sqrt(D_NODE * D_EDGE))
        norm_upd_tp = 1.0 / np.float32(np.sqrt(D_NODE * D_HIDDEN))
        norm_lin = 1.0 / np.float32(np.sqrt(D_HIDDEN))
        x_j = node_features[col]
        m = jnp.einsum('ei,ej,ijh->eh', x_j, edge_attr_e3nn, W_msg_tp) * norm_msg_tp
        m = jax.nn.silu(m)
        m = m @ W_msg_lin * norm_lin
        agg = jax.ops.segment_sum(m, row, num_segments=n_nodes)
        u = jnp.einsum('ni,nh,ihk->nk', node_features, agg, W_upd_tp) * norm_upd_tp
        u = jax.nn.silu(u)
        u = u @ W_upd_lin * norm_lin
        return node_features + u
    edge_index = jnp.stack([src, dst])
    h = jnp.maximum(_layernorm(x, axis=-1), 0.0)
    x = x + _L0_gnn_ref(h, edge_attr_48, edge_attr_3, L0_gnn_fc0_w1, L0_gnn_fc0_b1, L0_gnn_fc0_w2, L0_gnn_fc0_b2, L0_gnn_fc1_w1, L0_gnn_fc1_b1, L0_gnn_fc1_w2, L0_gnn_fc1_b2, L0_gnn_bn0_gs, L0_gnn_bn0_bs, L0_gnn_bn0_gv, L0_gnn_bn1_gs, L0_gnn_bn1_bs, edge_index)
    h = jnp.maximum(_layernorm(x, axis=-1), 0.0)
    x = x + _L1_gnn_ref(h, edge_attr_8, node_vec1, L1_gnn_W_msg_tp, L1_gnn_W_msg_lin, L1_gnn_W_upd_tp, L1_gnn_W_upd_lin, edge_index)
    return x

_drawn_inputs = setup_inputs


def setup_inputs(seed=0):
    import zlib

    import numpy as np

    out = dict(_drawn_inputs(seed))
    spreads = {'L0_gnn_fc0_b1': (0.0, 0.1),
     'L0_gnn_fc0_b2': (0.0, 0.1),
     'L0_gnn_fc1_b1': (0.0, 0.1),
     'L0_gnn_fc1_b2': (0.0, 0.1),
     'L0_gnn_bn0_gs': (1.0, 0.2),
     'L0_gnn_bn0_bs': (0.0, 0.1),
     'L0_gnn_bn0_gv': (1.0, 0.2),
     'L0_gnn_bn1_gs': (1.0, 0.2),
     'L0_gnn_bn1_bs': (0.0, 0.1)}
    factors = {}
    for name, (base, spread) in spreads.items():
        noise = np.random.default_rng([zlib.crc32(name.encode()), seed]).standard_normal(out[name].shape)
        drawn = base * np.exp(spread * noise) if base else spread * noise
        out[name] = jnp.asarray(drawn.astype(out[name].dtype))
    for name, factor in factors.items():
        out[name] = (out[name] * factor).astype(out[name].dtype)
    return out
```

```python
import numpy as np
import concourse.bass as bass
from concourse import mybir
from contextlib import ExitStack

F32 = mybir.dt.float32
BF16 = mybir.dt.bfloat16
FP16 = mybir.dt.float16
I32 = mybir.dt.int32
U32 = mybir.dt.uint32
U16 = mybir.dt.uint16
ALU = mybir.AluOpType
ACT = mybir.ActivationFunctionType
AX = mybir.AxisListType

P = 128
LOCAL = 125
UNIT = 2
GROUP = 4
GU = GROUP // UNIT
RING = 4
REC = 64
EPS = 1e-5

ATTR, EA8, RHAT, LO, DST = 0, 48, 56, 59, 60
CMP = 13
C_EA8, C_RHAT, C_LO, C_DST = 0, 8, 11, 12

NS, NV, HID = 16, 4, 48
F0 = NS + 3 * NV + 1
T0 = NS + 3 * NV



def moved(n, by):
    body, slot = n
    return body + (slot + by) // RING, (slot + by) % RING


def exists(n, by, groups):
    body, slot = moved(n, by)
    return not isinstance(body, int) or 0 <= body * RING + slot < groups


def index(n, by=0):
    body, slot = moved(n, by)
    return body * RING + slot


def count(n, by=0, per=1, start=0):
    return index(n, by) * per + per + start


def used(n, by=0, each=16):
    return moved(n, by)[0] * each + each


def walk(eng, step, groups):
    bodies = groups // RING
    for g in range(-2 * RING, 2 * RING):
        step((g // RING, g % RING))
    with eng.Fori(2, bodies - 2) as body:
        for slot in range(RING):
            step((body, slot))
    for g in range((bodies - 2) * RING, (bodies + 2) * RING):
        step((g // RING, g % RING))


class Kept:
    pass


def gnn(nc, x, src, dst, ea3, ea48, ea8, w1, b1, w2_0, w2_1, rows, w_msg, w_lin_t, w_upd, w_out, out):
    N, E = x.shape[0], src.shape[0]
    B = N // LOCAL
    C = E // P
    assert N == B * LOCAL and E == C * P and B <= 100
    units = E // (P * UNIT) + B
    G = -(-units // (GU * RING)) * RING
    K = max(k for k in range(1, P + 1) if G % k == 0)
    CH = G // K
    STEP = 25
    assert C % STEP == 0
    chunks = [min(500, C - c) for c in range(0, C, 500)]

    rec_d = nc.dram_tensor("rec_sorted", (G, GU, P, UNIT * REC), F32, kind="Internal").ap()
    cmp_d = nc.dram_tensor("cmp_sorted", (G, P, GROUP * CMP), F32, kind="Internal").ap()
    hid_d = nc.dram_tensor("hidden1", (G, HID, GROUP * P), F32, kind="Internal").ap()
    sum0_d = nc.dram_tensor("sums0", (G, P, GU * F0), F32, kind="Internal").ap()
    sum1_d = nc.dram_tensor("sums1", (G, P, GU * NS), F32, kind="Internal").ap()
    sum2_d = nc.dram_tensor("sums2", (G, P, GU * NS), F32, kind="Internal").ap()
    tab0_d = nc.dram_tensor("table0", (N, NS), F32, kind="Internal").ap()
    tab1_d = nc.dram_tensor("table1", (N, T0), F32, kind="Internal").ap()
    tab2_d = nc.dram_tensor("table2", (N, NS * 8), F32, kind="Internal").ap()

    whole = ExitStack()
    with whole:
        spent = []

        def alloc(scope):
            def semaphore(name, by_pool_dma=False):
                s = nc.alloc_semaphore(name)
                if not by_pool_dma:
                    spent.append(s)
                return s
            return lambda name, shape, dt: scope.enter_context(nc.sbuf_tensor(name, shape, dt)), semaphore

        def clear_spent():
            nc.clear_and_free_semaphores(list(spent))
            spent.clear()
            nc.all_engine_barrier()
        sb, sem = alloc(whole)
        ps = whole.enter_context(nc.psum_tensor("ps", [P, 8, 512], F32))

        x_sb = sb("x_sb", [B, LOCAL, NS], F32)
        h_sb = sb("h_sb", [B, LOCAL, NS], F32)
        rcount = sb("rcount", [B, LOCAL], F32)
        owner = sb("owner", [K, CH * GU, B], F32)
        ident = sb("ident", [P, P], F32)
        ones = sb("ones", [P, P], F32)
        rows_sb = sb("rows_sb", [B, rows.shape[1]], F32)
        iota_p = sb("iota_p", [P, P], F32)

        def layernorm_relu(dve, link, xin, hout, var, tmp, sq_ready, rt_ready, turn):
            bc = lambda a: a[:, :].unsqueeze(2).to_broadcast([B, LOCAL, NS])
            link(nc.vector.tensor_reduce(var[:, :], xin[:, :, :], AX.X, ALU.add))
            link(nc.vector.tensor_scalar(var[:, :], var[:, :], 1.0 / NS, None, ALU.mult))
            link(nc.vector.tensor_tensor(hout[:, :, :], xin[:, :, :], bc(var), ALU.subtract))
            link(nc.vector.tensor_tensor(tmp[:, :, 0:NS], hout[:, :, :], hout[:, :, :], ALU.mult))
            link(nc.vector.tensor_reduce(var[:, :], tmp[:, :, 0:NS], AX.X, ALU.add))
            nc.vector.tensor_scalar(var[:, :], var[:, :], 1.0 / NS, EPS, ALU.mult, ALU.add).then_inc(sq_ready, 1)
            dve.wait_ge(rt_ready, turn)
            link(nc.vector.reciprocal(var[:, :], var[:, :]))
            link(nc.vector.tensor_tensor(hout[:, :, :], hout[:, :, :], bc(var), ALU.mult))
            link(nc.vector.tensor_scalar(hout[:, :, :], hout[:, :, :], 0.0, None, ALU.max))

        sort = ExitStack()
        with sort:
            sbs, _ = alloc(sort)
            loc = sbs("loc", [P, C], F32)
            rhat = sbs("rhat", [P, C, 3], F32)
            bucket = sbs("bucket", [P, C], BF16)
            base_hi = sbs("base_hi", [B, C], BF16)
            base_lo = sbs("base_lo", [B, C], FP16)
            iota_b = sbs("iota_b", [P, P], F32)

            prep = ExitStack()
            with prep:
                sbp, semp = alloc(prep)
                srci = sbp("srci", [P, C], I32)
                f0 = sbp("f0", [P, C], F32)
                f1 = sbp("f1", [P, C], F32)
                f2 = sbp("f2", [P, C], F32)
                lnv = sbp("lnv", [B, LOCAL], F32)
                lnt = sbp("lnt", [B, LOCAL, NS], F32)
                rows1 = sbp("rows1", [1, rows.shape[1]], F32)
                eq = sbp("eq", [P, 2, C], BF16)
                pick = sbp("pick", [P, 2 * P], BF16)
                zb = sbp("zb", [P, 512], BF16)
                tri = sbp("tri", [P, P], F32)
                tri_in = sbp("tri_in", [P, P], F32)
                fill = sbp("fill", [P, 8, REC], F32)
                nb = sbp("nb", [B, 4], F32)
                nbi = sbp("nbi", [B, 1], I32)
                unit_no = sbp("unit_no", [K, CH * GU], F32)
                span = sbp("span", [K, 2 * P], F32)
                src_in, x_in, v_in, rows_in = semp("src_in"), semp("x_in"), semp("v_in"), semp("rows_in")
                fill_ready, fill_out, tab_out = semp("fill_ready"), semp("fill_out"), semp("tab_out")
                const_ready, link_s, sq_ready, rt_ready = semp("const_ready"), semp("link_s"), semp("sq_ready"), semp("rt_ready")
                eq_ready, eq_used, counted = semp("eq_ready"), semp("eq_used"), semp("counted")
                pe_turn = semp("pe_turn")
                n_ready, starts_ready, rows_bc, h_ready = semp("n_ready"), semp("starts_ready"), semp("rows_bc"), semp("h_ready")
                pool_link = semp("pool_link")
                count_cols = [(c, min(448, C - c)) for c in range(0, C, 448)]

                block = prep.enter_context(nc.Block())

                @block.sync
                def _(sp):
                    sp.dma_start(srci[:, :], src.rearrange("(p c) -> p c", p=P)).then_inc(src_in, 16)
                    sp.dma_start(rhat[:, :, :], ea3.rearrange("(p c) f -> p c f", p=P)).then_inc(v_in, 16)
                    sp.dma_start(x_sb[:, :, :], x.rearrange("(b l) f -> b l f", l=LOCAL)).then_inc(x_in, 16)
                    sp.dma_start(rows1[:, :], rows).then_inc(rows_in, 16)
                    sp.wait_ge(fill_ready, 2)
                    rec_f = rec_d.rearrange("g u p x -> (g u p x)").rearrange("(p r x) -> p r x", p=P, x=8 * REC)
                    per_p = rec_f.shape[1]
                    cuts = [per_p * i // 8 for i in range(9)]
                    for a, b in zip(cuts, cuts[1:]):
                        if b > a:
                            sp.dma_start(rec_f[:, a:b, :], fill[:, :, :].rearrange("p a x -> p (a x)").unsqueeze(1)
                                         .to_broadcast([P, b - a, 8 * REC])).then_inc(fill_out, 16)
                    sp.wait_ge(h_ready, 1)
                    sp.dma_start(tab0_d.rearrange("(b l) f -> b l f", l=LOCAL), h_sb[:, :, :]).then_inc(tab_out, 16)
                    sp.wait_ge(tab_out, 16)
                    sp.wait_ge(fill_out, 16 * sum(b > a for a, b in zip(cuts, cuts[1:])))

                @block.gpsimd
                def _(pool):
                    nc.gpsimd.memset(fill[:, :, :], 0.0).then_inc(fill_ready, 1)
                    pool.wait_ge(fill_ready, 1)
                    nc.gpsimd.memset(fill[:, :, LO:LO + 1], -1.0).then_inc(fill_ready, 1)
                    nc.gpsimd.iota(iota_p[:, :], pattern=[[1, P]], base=0, channel_multiplier=0,
                                   allow_small_or_imprecise_dtypes=True)
                    nc.gpsimd.iota(iota_b[:, :], pattern=[[1, P]], base=0, channel_multiplier=0,
                                   allow_small_or_imprecise_dtypes=True)
                    nc.gpsimd.iota(unit_no[:, :], pattern=[[GU * K, CH], [1, GU]], base=0, channel_multiplier=GU,
                                   allow_small_or_imprecise_dtypes=True)
                    nc.gpsimd.memset(ones[:, :], 1.0)
                    nc.gpsimd.memset(ident[:, :], 0.0)
                    nc.gpsimd.memset(zb[:, :], 0.0)
                    nc.gpsimd.memset(pick[:, :], 0.0).then_inc(pool_link, 1)
                    pool.wait_ge(pool_link, 1)
                    nc.gpsimd.memset(pick[:, P:P + 1], 1.0)
                    nc.gpsimd.affine_select(out=ident[:, :], in_=ident[:, :], compare_op=ALU.not_equal, fill=1.0,
                                            base=0, pattern=[[-1, P]], channel_multiplier=1)
                    nc.gpsimd.affine_select(out=tri[:, :], in_=ones[:, :], compare_op=ALU.is_gt, fill=0.0,
                                            base=0, pattern=[[1, P]], channel_multiplier=-1)
                    nc.gpsimd.affine_select(out=tri_in[:, :], in_=ones[:, :], compare_op=ALU.is_ge, fill=0.0,
                                            base=0, pattern=[[1, P]], channel_multiplier=-1).then_inc(const_ready, 1)

                @block.scalar
                def _(act):
                    act.wait_ge(sq_ready, 1)
                    nc.scalar.activation(lnv[:, :], lnv[:, :], ACT.Sqrt).then_inc(rt_ready, 1)
                    act.wait_ge(sq_ready, 2)
                    nc.scalar.activation(f1[:, :], f0[:, :], ACT.Sqrt).then_inc(rt_ready, 1)

                @block.tensor
                def _(pe):
                    pe.wait_ge(rows_in, 16)
                    pe.wait_ge(const_ready, 1)
                    nc.tensor.matmul(ps[0:B, 7, 0:rows.shape[1]], ones[0:1, 0:B], rows1[:, :], start=True,
                                     stop=True).then_inc(rows_bc, 1)
                    for j, (c, w) in enumerate(count_cols):
                        nc.tensor.matmul(ps[0:B, j, 0:w], zb[:, 0:B], zb[:, 0:w], start=True, stop=False)
                    with pe.Fori(0, B // 2) as i:
                        for s in range(2):
                            pe.wait_ge(eq_ready, 2 * i + s + 1)
                            pe.sem_inc(pe_turn, 1)
                            for j, (c, w) in enumerate(count_cols):
                                last = nc.tensor.matmul(ps[0:B, j, 0:w], pick[:, bass.ds(P - s - 2 * i, B)],
                                                        eq[:, s, c:c + w], start=False, stop=False)
                            last.then_inc(eq_used, 1)
                    for j, (c, w) in enumerate(count_cols):
                        last = nc.tensor.matmul(ps[0:B, j, 0:w], zb[:, 0:B], zb[:, 0:w], start=False, stop=True)
                    last.then_inc(counted, 1)
                    pe.wait_ge(n_ready, 1)
                    nc.tensor.matmul(ps[0:B, 7, 64:65], tri[0:B, 0:B], nb[:, 3:4], start=True, stop=True)
                    units_bc = nb[:, 3:4].to_broadcast([B, K])
                    nc.tensor.matmul(ps[0:K, 7, 128:128 + B], units_bc, tri[0:B, 0:B], start=True, stop=True)
                    nc.tensor.matmul(ps[0:K, 7, 256:256 + B], units_bc, tri_in[0:B, 0:B], start=True,
                                     stop=True).then_inc(starts_ready, 1)

                @block.vector
                def _(dve):
                    linked = [0]

                    def link(ins):
                        linked[0] += 1
                        ins.then_inc(link_s, 1)
                        dve.wait_ge(link_s, linked[0])

                    def floor_of(out, value, whole_i, more):
                        link(nc.vector.tensor_copy(whole_i, value))
                        link(nc.vector.tensor_copy(out, whole_i))
                        link(nc.vector.tensor_tensor(more, out, value, ALU.is_gt))
                        link(nc.vector.tensor_tensor(out, out, more, ALU.subtract))

                    dve.wait_ge(src_in, 16)
                    link(nc.vector.tensor_copy(f0[:, :], srci[:, :]))
                    link(nc.vector.tensor_scalar(f1[:, :], f0[:, :], 1.0 / LOCAL, None, ALU.mult))
                    floor_of(f2[:, :], f1[:, :], srci[:, :], loc[:, :])
                    link(nc.vector.scalar_tensor_tensor(out=loc[:, :], in0=f2[:, :], scalar=-float(LOCAL), in1=f0[:, :],
                                                        op0=ALU.mult, op1=ALU.add))
                    link(nc.vector.tensor_scalar(f1[:, :], loc[:, :], 0.0, None, ALU.is_lt))
                    link(nc.vector.tensor_scalar(f0[:, :], loc[:, :], float(LOCAL), None, ALU.is_ge))
                    link(nc.vector.tensor_tensor(f0[:, :], f0[:, :], f1[:, :], ALU.subtract))
                    link(nc.vector.tensor_tensor(bucket[:, :], f2[:, :], f0[:, :], ALU.add))
                    link(nc.vector.scalar_tensor_tensor(out=loc[:, :], in0=f0[:, :], scalar=-float(LOCAL), in1=loc[:, :],
                                                        op0=ALU.mult, op1=ALU.add))
                    dve.wait_ge(x_in, 16)
                    dve.wait_ge(rows_bc, 1)
                    nc.vector.tensor_copy(rows_sb[:, :], ps[0:B, 7, 0:rows.shape[1]])
                    layernorm_relu(dve, link, x_sb, h_sb, lnv, lnt, sq_ready, rt_ready, 1)
                    dve.engine_nop().then_inc(h_ready, 1)
                    dve.wait_ge(v_in, 16)
                    link(nc.vector.tensor_tensor(f0[:, :], rhat[:, :, 0], rhat[:, :, 0], ALU.mult))
                    for c in (1, 2):
                        link(nc.vector.tensor_tensor(f1[:, :], rhat[:, :, c], rhat[:, :, c], ALU.mult))
                        link(nc.vector.tensor_tensor(f0[:, :], f0[:, :], f1[:, :], ALU.add))
                    dve.engine_nop().then_inc(sq_ready, 1)
                    dve.wait_ge(const_ready, 1)
                    for s in range(2):
                        nc.vector.tensor_scalar(eq[:, s, :], bucket[:, :], iota_b[:, s:s + 1], None,
                                                ALU.is_equal).then_inc(eq_ready, 1)
                    with dve.Fori(1, B // 2) as i:
                        for s in range(2):
                            dve.wait_ge(eq_used, 2 * i + s - 1)
                            nc.vector.tensor_scalar(eq[:, s, :], bucket[:, :], iota_b[:, bass.ds(2 * i + s, 1)], None,
                                                    ALU.is_equal).then_inc(eq_ready, 1)
                    dve.wait_ge(rt_ready, 2)
                    link(nc.vector.tensor_scalar(f1[:, :], f1[:, :], 1e-12, None, ALU.add))
                    link(nc.vector.reciprocal(f0[:, :], f1[:, :]))
                    link(nc.vector.tensor_tensor(rhat[:, :, :], rhat[:, :, :], f0[:, :].unsqueeze(2)
                                                 .to_broadcast([P, C, 3]), ALU.mult))
                    dve.wait_ge(counted, 1)
                    for j, (c, w) in enumerate(count_cols):
                        last = nc.vector.tensor_copy(f0[0:B, c:c + w], ps[0:B, j, 0:w])
                    link(last)
                    link(nc.vector.tensor_tensor_scan(f1[0:B, :], ones[0:B, 0:1].to_broadcast([B, C]), f0[0:B, :], 0.0,
                                                      ALU.mult, ALU.add))
                    link(nc.vector.tensor_tensor(f1[0:B, :], f1[0:B, :], f0[0:B, :], ALU.subtract))
                    link(nc.vector.tensor_tensor(nb[:, 0:1], f1[0:B, C - 1:C], f0[0:B, C - 1:C], ALU.add))
                    link(nc.vector.tensor_scalar(nb[:, 1:2], nb[:, 0:1], float(UNIT * P - 1), 1.0 / (UNIT * P),
                                                 ALU.add, ALU.mult))
                    link(nc.vector.tensor_copy(nbi[:, :], nb[:, 1:2]))
                    link(nc.vector.tensor_copy(nb[:, 3:4], nbi[:, :]))
                    link(nc.vector.tensor_tensor(nb[:, 2:3], nb[:, 3:4], nb[:, 1:2], ALU.is_gt))
                    link(nc.vector.tensor_tensor(nb[:, 3:4], nb[:, 3:4], nb[:, 2:3], ALU.subtract))
                    dve.engine_nop().then_inc(n_ready, 1)
                    dve.wait_ge(starts_ready, 1)
                    link(nc.vector.tensor_scalar(nb[:, 0:1], ps[0:B, 7, 64:65], float(UNIT * P), None, ALU.mult))
                    link(nc.vector.tensor_copy(span[:, 0:B], ps[0:K, 7, 128:128 + B]))
                    link(nc.vector.tensor_copy(span[:, P:P + B], ps[0:K, 7, 256:256 + B]))
                    link(nc.vector.tensor_scalar(f1[0:B, :], f1[0:B, :], nb[:, 0:1], None, ALU.add))
                    link(nc.vector.tensor_scalar(f0[0:B, :], f1[0:B, :], 1.0 / 2048, None, ALU.mult))
                    link(nc.vector.tensor_copy(srci[0:B, :], f0[0:B, :]))
                    link(nc.vector.tensor_copy(f2[0:B, :], srci[0:B, :]))
                    link(nc.vector.tensor_tensor(f0[0:B, :], f2[0:B, :], f0[0:B, :], ALU.is_gt))
                    link(nc.vector.tensor_tensor(f2[0:B, :], f2[0:B, :], f0[0:B, :], ALU.subtract))
                    link(nc.vector.tensor_scalar(base_hi[:, :], f2[0:B, :], 2048.0, None, ALU.mult))
                    link(nc.vector.scalar_tensor_tensor(out=base_lo[:, :], in0=f2[0:B, :], scalar=-2048.0,
                                                        in1=f1[0:B, :], op0=ALU.mult, op1=ALU.add))
                    for q in range(CH * GU):
                        link(nc.vector.tensor_scalar(owner[:, q, :], span[:, 0:B], unit_no[:, q:q + 1], None, ALU.is_le))
                        link(nc.vector.scalar_tensor_tensor(out=owner[:, q, :], in0=span[:, P:P + B],
                                                            scalar=unit_no[:, q:q + 1], in1=owner[:, q, :],
                                                            op0=ALU.is_gt, op1=ALU.mult))

            place = ExitStack()
            with place:
                sbp, semp = alloc(place)
                spread = sbp("spread", [B, B, P], BF16)
                tri_b = sbp("tri_b", [P, P], BF16)
                ones_b = sbp("ones_b", [P, P], BF16)
                eq = sbp("eq2", [P, 4, 512], BF16)
                pos = sbp("pos", [P, C], F32)
                rec = sbp("rec", [P, 2, STEP, REC], F32)
                in48 = sbp("in48", [P, 2, STEP, HID], F32)
                in8 = sbp("in8", [P, 2, STEP, 8], F32)
                ind = sbp("ind", [P, 2, STEP], I32)
                to = sbp("to", [P, 2, STEP], U32)
                consts, eq_ready, table_ready, copied = semp("consts2"), semp("eq_ready2"), semp("table_ready"), semp("copied")
                plink = semp("plink2")
                in_sem = [semp(f"edges_in{s}") for s in range(2)]
                rec_ready, rec_zero = semp("rec_ready"), semp("rec_zero")
                scattered = [semp(f"scattered{s}", True) for s in range(2)]
                pool_turn, dve_turn, pe_turn = semp("pool_turn"), semp("dve_turn"), semp("pe_turn2")
                steps = C // STEP
                block = place.enter_context(nc.Block())

                ea48_v = ea48.rearrange("(p c) f -> p c f", p=P)
                ea8_v = ea8.rearrange("(p c) f -> p c f", p=P)
                dst_v = dst.rearrange("(p c) -> p c", p=P)

                def edge_steps(eng, step):
                    pairs = steps // 2
                    for s in range(2):
                        step(0, s)
                    if pairs > 1:
                        with eng.Fori(1, pairs) as pair:
                            for s in range(2):
                                step(pair, s)
                    if steps % 2:
                        step(pairs, 0)

                @block.sync
                def _(sp):
                    def step(pair, s):
                        st = 2 * pair + s
                        if not (isinstance(pair, int) and pair == 0):
                            sp.wait_ge(rec_ready, st - 1)
                        cols = bass.ds(st * STEP, STEP)
                        sp.dma_start(in48[:, s], ea48_v[:, cols, :]).then_inc(in_sem[s], 16)
                        sp.dma_start(in8[:, s], ea8_v[:, cols, :]).then_inc(in_sem[s], 16)
                        sp.dma_start(ind[:, s], dst_v[:, cols]).then_inc(in_sem[s], 16)
                    edge_steps(sp, step)

                @block.scalar
                def _(act):
                    act.wait_ge(rec_zero, 1)

                    def step(pair, s, need):
                        st = 2 * pair + s
                        act.wait_ge(in_sem[s], 48 * (pair + 1))
                        if not (isinstance(pair, int) and pair == 0):
                            act.wait_ge(scattered[s], 16 * STEP * pair)
                        if need:
                            act.wait_ge(copied, need)
                        cols = bass.ds(st * STEP, STEP)
                        nc.scalar.activation(rec[:, s, :, ATTR:ATTR + HID], in48[:, s], ACT.Copy)
                        nc.scalar.activation(rec[:, s, :, EA8:EA8 + 8], in8[:, s], ACT.Copy)
                        nc.scalar.activation(rec[:, s, :, RHAT:RHAT + 3], rhat[:, cols, :], ACT.Copy)
                        nc.scalar.activation(rec[:, s, :, LO], loc[:, cols], ACT.Copy)
                        nc.scalar.activation(rec[:, s, :, DST], ind[:, s], ACT.Copy)
                        nc.scalar.activation(to[:, s], pos[:, cols], ACT.Copy).then_inc(rec_ready, 1)
                    done = 0
                    for n, width in enumerate(chunks):
                        k = width // STEP
                        pair0, pairs = done // 2, k // 2
                        for s in range(min(2, k)):
                            step(pair0, s, B * (n + 1) if s == 0 else 0)
                        if pairs > 1:
                            with act.Fori(pair0 + 1, pair0 + pairs) as pair:
                                for s in range(2):
                                    step(pair, s, 0)
                        if k % 2 and k > 1:
                            step(pair0 + pairs, 0, 0)
                        done += k

                @block.gpsimd
                def _(pool):
                    nc.gpsimd.memset(rec[:, :, :, DST + 1:REC], 0.0).then_inc(rec_zero, 1)
                    nc.gpsimd.memset(ones_b[:, :], 1.0).then_inc(plink, 1)
                    pool.wait_ge(plink, 1)
                    nc.gpsimd.affine_select(out=tri_b[:, :], in_=ones_b[:, :], compare_op=ALU.is_gt, fill=0.0,
                                            base=0, pattern=[[1, P]], channel_multiplier=-1)
                    nc.gpsimd.affine_select(out=spread[:, :, :], in_=ones_b[0:B, 0:1].unsqueeze(2).to_broadcast([B, B, P]),
                                            compare_op=ALU.is_equal, fill=0.0, base=0, pattern=[[1, B], [0, P]],
                                            channel_multiplier=-1).then_inc(consts, 1)
                    rec_rows = rec_d.rearrange("g u p (j f) -> (g u p j) f", f=REC)

                    def step(pair, s):
                        pool.wait_ge(rec_ready, 2 * pair + s + 1)
                        pool.sem_inc(pool_turn, 1)
                        for k in range(STEP):
                            nc.gpsimd.indirect_dma_start(
                                out=rec_rows, out_offset=bass.IndirectOffsetOnAxis(ap=to[:, s, k:k + 1], axis=0),
                                in_=rec[:, s, k, :], in_offset=None).then_inc(scattered[s], 16)
                    edge_steps(pool, step)
                    pool.wait_ge(scattered[0], 16 * STEP * ((steps + 1) // 2))
                    pool.wait_ge(scattered[1], 16 * STEP * (steps // 2))
                    pool.sem_inc(pool_turn, 1)

                @block.tensor
                def _(pe):
                    pe.wait_ge(consts, 1)
                    c = 0
                    for n, w in enumerate(chunks):
                        with pe.Fori(0, B // 2) as i:
                            for s in range(2):
                                b = 2 * i + s
                                pe.wait_ge(eq_ready, b + 1 + n * (B + 1))
                                pe.sem_inc(pe_turn, 1)
                                nc.tensor.matmul(ps[:, s, 0:w], tri_b[:, :], eq[:, s, 0:w], start=True, stop=False)
                                sel = spread[:, bass.ds(b, 1), :].rearrange("k o p -> k (o p)")
                                nc.tensor.matmul(ps[:, s, 0:w], sel, base_hi[:, c:c + w], start=False, stop=False)
                                nc.tensor.matmul(ps[:, s, 0:w], sel, base_lo[:, c:c + w], start=False,
                                                 stop=True).then_inc(table_ready, 1)
                        c += w

                @block.vector
                def _(dve):
                    c = 0
                    for n, w in enumerate(chunks):
                        cols = slice(c, c + w)
                        cmp = lambda b, s: nc.vector.tensor_scalar(
                            eq[:, s, 0:w], bucket[:, cols], iota_b[:, bass.ds(b, 1)], None, ALU.is_equal)
                        if n:
                            dve.wait_ge(copied, n * B)
                        cmp(0, 0).then_inc(eq_ready, 1)
                        with dve.Fori(0, B // 2) as i:
                            for s in range(2):
                                b = 2 * i + s
                                dve.wait_ge(copied, b + n * B)
                                cmp(b + 1, 1 - s).then_inc(eq_ready, 1)
                                dve.wait_ge(table_ready, b + 1 + n * B)
                                dve.sem_inc(dve_turn, 1)
                                nc.vector.copy_predicated(pos[:, cols], eq[:, s, 0:w].bitcast(U16),
                                                          ps[:, s, 0:w]).then_inc(copied, 1)
                        c += w
        p0 = ExitStack()
        with p0:
            sbp, semp = alloc(p0)
            recs = sbp("recs", [P, RING, GU, UNIT * REC], F32)
            comp = sbp("comp", [P, RING, GROUP, CMP], F32)
            at = sbp("at0", [P, RING, GROUP], I32)
            xs = sbp("xs0", [P, RING, GROUP, NS], F32)
            attr_t = sbp("attr_t", [HID, 2, GROUP * P], F32)
            hid = sbp("hid", [112, RING, GROUP * P], F32)
            w1c = sbp("w1c", [HID, 112], F32)
            b1c = sbp("b1c", [112, 1], F32)
            w2s = sbp("w2s0", [HID + 1, 320], F32)
            prod = sbp("prod0", [P, 2, 2, 20, NS], F32)
            msg = sbp("msg0", [P, 2, GROUP, 4 + F0], F32)
            owns = sbp("owns0", [P, 2, GROUP, P], F32)
            sums = sbp("sums0_sb", [P, RING, GU, F0], F32)

            rec_in = [semp(f"rec_in{k}") for k in range(RING)]
            xs_in = [semp(f"xs_in{k}", True) for k in range(RING)]
            comp_out = [semp(f"comp_out{k}") for k in range(RING)]
            hid_out = [semp(f"hid_out{k}") for k in range(RING)]
            sums_out = [semp(f"sums_out{k}") for k in range(RING)]
            w_in, w_zero, msg_one = semp("w_in0"), semp("w_zero"), semp("msg_one")
            attr_on_pe, attr_ready, hid_on_pe, hid_ready = semp("attr_on_pe"), semp("attr_ready"), semp("hid_on_pe"), semp("hid_ready")
            comp_ready, at_ready = semp("comp_ready"), semp("at_ready0")
            weights_ready, prod_ready, reduced = semp("weights_ready0"), semp("prod_ready0"), semp("reduced0")
            owns_ready, msg_ready, summed, sums_ready = semp("owns_ready0"), semp("msg_ready0"), semp("summed0"), semp("sums_ready0")
            turn, pe_turn = semp("pool_turn0"), semp("pe_turn0")
            block = p0.enter_context(nc.Block())

            @block.sync
            def _(sp):
                sp.dma_start(w2s[:, :], w2_0).then_inc(w_in, 16)
                sp.wait_ge(w_zero, 2)
                for k, at_col in ((0, 0), (1, 64)):
                    sp.dma_start(w1c[:, at_col:at_col + HID], w1[k]).then_inc(w_in, 16)
                    sp.dma_start(b1c[at_col:at_col + HID, :], b1[k]).then_inc(w_in, 16)

                def step(n):
                    if exists(n, 5, G):
                        slot = moved(n, 5)[1]
                        if exists(n, 1, G):
                            sp.wait_ge(attr_on_pe, count(n, 1))
                            sp.wait_ge(at_ready, count(n, 1))
                        sp.dma_start(recs[:, slot], rec_d[bass.ds(index(n, 5), 1)].rearrange("o u p x -> p (o u) x"))\
                          .then_inc(rec_in[slot], 16)
                    if exists(n, 2, G):
                        slot = moved(n, 2)[1]
                        sp.wait_ge(comp_ready, count(n, 2))
                        sp.dma_start(cmp_d[bass.ds(index(n, 2), 1)].rearrange("o p x -> p (o x)"),
                                     comp[:, slot].rearrange("p t f -> p (t f)")).then_inc(comp_out[slot], 16)
                    if exists(n, 0, G):
                        sp.wait_ge(hid_ready, count(n))
                        sp.dma_start(hid_d[bass.ds(index(n), 1)].rearrange("o k e -> k (o e)"),
                                     hid[64:64 + HID, n[1], :]).then_inc(hid_out[n[1]], 16)
                    if exists(n, -3, G):
                        slot = moved(n, -3)[1]
                        sp.wait_ge(sums_ready, count(n, -3))
                        sp.dma_start(sum0_d[bass.ds(index(n, -3), 1)].rearrange("o p x -> p (o x)"),
                                     sums[:, slot].rearrange("p u f -> p (u f)")).then_inc(sums_out[slot], 16)
                walk(sp, step, G)
                for k in range(RING):
                    for stored in (comp_out, hid_out, sums_out):
                        sp.wait_ge(stored[k], 16 * (G // RING))

            @block.gpsimd
            def _(pool):
                nc.gpsimd.memset(w1c[:, :], 0.0).then_inc(w_zero, 1)
                nc.gpsimd.memset(b1c[:, :], 1.0).then_inc(w_zero, 1)

                def step(n):
                    if exists(n, 3, G):
                        slot = moved(n, 3)[1]
                        pool.wait_ge(at_ready, count(n, 3))
                        if exists(n, -1, G):
                            pool.wait_ge(prod_ready, count(n, -1, 2))
                        pool.sem_inc(turn, 1)
                        for t in range(GROUP):
                            nc.gpsimd.indirect_dma_start(
                                out=xs[:, slot, t, :], out_offset=None, in_=tab0_d,
                                in_offset=bass.IndirectOffsetOnAxis(ap=at[:, slot, t:t + 1], axis=0))\
                              .then_inc(xs_in[slot], 16)
                walk(pool, step, G)

            @block.scalar
            def _(act):
                act.wait_ge(w_in, 80)

                def step(n):
                    if exists(n, 3, G):
                        slot = moved(n, 3)[1]
                        act.wait_ge(rec_in[slot], used(n, 3))
                        if exists(n, -1, G):
                            act.wait_ge(msg_ready, count(n, -1))
                            act.wait_ge(comp_out[slot], used(n, -1))
                        fields = recs[:, slot].rearrange("p u (j f) -> p (u j) f", f=REC)
                        nc.scalar.activation(comp[:, slot], fields[:, :, EA8:EA8 + CMP], ACT.Copy).then_inc(comp_ready, 1)
                        if exists(n, -1, G):
                            act.wait_ge(xs_in[slot], used(n, -1, 16 * GROUP))
                        nc.scalar.activation(at[:, slot], fields[:, :, DST], ACT.Copy).then_inc(at_ready, 1)
                    if exists(n, 2, G):
                        act.wait_ge(attr_on_pe, count(n, 2))
                        if exists(n, 0, G):
                            act.wait_ge(hid_on_pe, count(n))
                        nc.scalar.activation(attr_t[:, n[1] % 2, :], ps[0:HID, 0, :], ACT.Copy).then_inc(attr_ready, 1)
                    if exists(n, 1, G):
                        slot = moved(n, 1)[1]
                        act.wait_ge(hid_on_pe, count(n, 1))
                        if exists(n, -3, G):
                            act.wait_ge(weights_ready, count(n, -3, 2))
                            act.wait_ge(hid_out[slot], used(n, -3))
                        nc.scalar.activation(hid[:, slot, :], ps[0:112, 1, :], ACT.Relu, bias=b1c[:, 0:1])\
                          .then_inc(hid_ready, 1)
                    if exists(n, -2, G):
                        slot = moved(n, -2)[1]
                        act.wait_ge(summed, count(n, -2))
                        if exists(n, -6, G):
                            act.wait_ge(sums_out[slot], used(n, -6))
                        nc.scalar.activation(sums[:, slot], ps[:, 6 + slot % 2, 0:GU * F0]
                                             .rearrange("p (u f) -> p u f", f=F0), ACT.Copy).then_inc(sums_ready, 1)
                walk(act, step, G)

            @block.tensor
            def _(pe):
                pe.wait_ge(w_in, 80)

                def step(n):
                    if exists(n, 2, G):
                        slot = moved(n, 2)[1]
                        pe.wait_ge(rec_in[slot], used(n, 2))
                        if exists(n, 1, G):
                            pe.wait_ge(attr_ready, count(n, 1))
                        pe.sem_inc(pe_turn, 1)
                        for t in range(GROUP):
                            u, j = t // UNIT, t % UNIT
                            last = nc.tensor.transpose(ps[0:HID, 0, t * P:(t + 1) * P],
                                                       recs[:, slot, u, j * REC:j * REC + HID], ident[:, :])
                        last.then_inc(attr_on_pe, 1)
                    if exists(n, 1, G):
                        pe.wait_ge(attr_ready, count(n, 1))
                        if exists(n, 0, G):
                            pe.wait_ge(hid_ready, count(n))
                        nc.tensor.matmul(ps[0:112, 1, :], w1c[:, :], attr_t[:, (n[1] + 1) % 2, :], start=True,
                                         stop=True).then_inc(hid_on_pe, 1)
                    if exists(n, 0, G):
                        pe.wait_ge(hid_ready, count(n))
                        for q in range(2):
                            if exists(n, -1, G):
                                pe.wait_ge(prod_ready, count(n, -1, 2) - 1 + q)
                            for t in (2 * q, 2 * q + 1):
                                last = nc.tensor.matmul(ps[:, 2 + t, 0:320], hid[0:HID + 1, n[1], t * P:(t + 1) * P],
                                                        w2s[:, :], start=True, stop=True)
                            last.then_inc(weights_ready, 1)
                    if exists(n, -1, G):
                        half = (n[1] + 1) % 2
                        pe.wait_ge(msg_ready, count(n, -1))
                        pe.wait_ge(owns_ready, count(n, -1))
                        if exists(n, -3, G):
                            pe.wait_ge(sums_ready, count(n, -3))
                        for u in range(GU):
                            for j in range(UNIT):
                                t = u * UNIT + j
                                last = nc.tensor.matmul(ps[:, 6 + half, u * F0:(u + 1) * F0], owns[:, half, t, :],
                                                        msg[:, half, t, 4:], start=(j == 0), stop=(j == UNIT - 1))
                        last.then_inc(summed, 1)
                walk(pe, step, G)

            @block.vector
            def _(dve):
                nc.vector.memset(msg[:, :, :, :], 1.0).then_inc(msg_one, 1)
                dve.wait_ge(msg_one, 1)

                def step(n):
                    if not exists(n, 0, G):
                        return
                    slot, half = n[1], n[1] % 2
                    for q in range(2):
                        if q == 0:
                            dve.wait_ge(xs_in[slot], used(n, 0, 16 * GROUP))
                        dve.wait_ge(weights_ready, count(n, 0, 2) - 1 + q)
                        nc.vector.tensor_tensor(
                            prod[:, q], ps[:, 2 + 2 * q:4 + 2 * q, 0:320].rearrange("p t (j i) -> p t j i", i=NS),
                            xs[:, slot, 2 * q:2 * q + 2, :].unsqueeze(2).to_broadcast([P, 2, 20, NS]),
                            ALU.mult).then_inc(prod_ready, 1)
                    if exists(n, -2, G):
                        dve.wait_ge(summed, count(n, -2))
                    for q in range(2):
                        dve.wait_ge(prod_ready, count(n, 0, 2) - 1 + q)
                        nc.vector.tensor_reduce(msg[:, half, 2 * q:2 * q + 2, 0:20], prod[:, q], AX.X, ALU.add)\
                          .then_inc(reduced, 1)
                    dve.wait_ge(comp_ready, count(n))
                    for t in range(GROUP):
                        last = nc.vector.tensor_scalar(owns[:, half, t, :], iota_p[:, :], comp[:, slot, t, C_LO:C_LO + 1],
                                                       None, ALU.is_equal)
                    last.then_inc(owns_ready, 1)
                    dve.wait_ge(reduced, count(n, 0, 2))
                    nc.vector.tensor_tensor(
                        msg[:, half, :, 20:32].rearrange("p t (j c) -> p t j c", c=3),
                        msg[:, half, :, 0:4].unsqueeze(3).to_broadcast([P, GROUP, 4, 3]),
                        comp[:, slot, :, C_RHAT:C_RHAT + 3].unsqueeze(2).to_broadcast([P, GROUP, 4, 3]),
                        ALU.mult).then_inc(msg_ready, 1)
                walk(dve, step, G)

        clear_spent()

        sh = Kept()
        sh.N, sh.B, sh.G, sh.K, sh.CH, sh.alloc, sh.ps, sh.owner = N, B, G, K, CH, alloc, ps, owner
        sh.ones, sh.ident, sh.iota_p, sh.rcount, sh.rows_sb = ones, ident, iota_p, rcount, rows_sb
        sh.x_sb, sh.h_sb, sh.layernorm_relu, sh.cmp_d, sh.hid_d = x_sb, h_sb, layernorm_relu, cmp_d, hid_d
        nodes_0(nc, sh, sum0_d, tab1_d)
        pass_1(nc, sh, w2_1, tab1_d, sum1_d)
        nodes_1(nc, sh, sum1_d, w_msg, tab2_d)
        pass_2(nc, sh, tab2_d, sum2_d)
        nodes_2(nc, sh, sum2_d, w_lin_t, w_upd, w_out, out)


def reduce_units(nc, sh, sum_d, F, tot, tag, sbp, semp):
    K, CH, B, ps = sh.K, sh.CH, sh.B, sh.ps
    lc = 1 << ((512 // F).bit_length() - 1)
    banks = P // lc
    part = sbp(f"part{tag}", [K, 2, P, GU, F], F32)
    part_in = [semp(f"part_in{tag}{s}") for s in range(2)]
    part_used, tot_ready = semp(f"part_used{tag}"), semp(f"tot_ready{tag}")

    def sync(sp):
        for c in range(CH):
            if c >= 2:
                sp.wait_ge(part_used, c - 1)
            sp.dma_start(part[:, c % 2].rearrange("k l u f -> k (l u f)"),
                         sum_d[c * K:(c + 1) * K].rearrange("k l x -> k (l x)"), max_dma_last_dim=16384)\
              .then_inc(part_in[c % 2], 16)

    def tensor(pe):
        for c in range(CH):
            pe.wait_ge(part_in[c % 2], 16 * (c // 2 + 1))
            for u in range(GU):
                for j in range(banks):
                    last = nc.tensor.matmul(ps[0:B, j, 0:lc * F], sh.owner[:, c * GU + u, :],
                                            part[:, c % 2, j * lc:(j + 1) * lc, u, :],
                                            start=(c == 0 and u == 0), stop=(c == CH - 1 and u == GU - 1))
            last.then_inc(part_used, 1)
        pe.wait_ge(tot_ready, 1)

    def scalar(act):
        act.wait_ge(part_used, CH)
        for j in range(banks):
            last = nc.scalar.activation(tot[:, j * lc:(j + 1) * lc, :], ps[0:B, j, 0:lc * F]
                                        .rearrange("b (l f) -> b l f", f=F), ACT.Copy)
        last.then_inc(tot_ready, 1)
    return sync, tensor, scalar, tot_ready


class Linker:

    def __init__(self, dve, sem):
        self.dve, self.sem, self.n = dve, sem, 0

    def __call__(self, ins):
        self.n += 1
        ins.then_inc(self.sem, 1)
        self.dve.wait_ge(self.sem, self.n)


def nodes_0(nc, sh, sum_d, tab_d):
    B, N, ps, ones, rows = sh.B, sh.N, sh.ps, sh.ones, sh.rows_sb
    L = LOCAL
    scope = ExitStack()
    with scope:
        sbp, semp = sh.alloc(scope)
        tot = sbp("tot0", [B, P, F0], F32)
        val = sbp("val0", [B, L, T0], F32)
        sq = sbp("sq0", [B, L, T0], F32)
        m = sbp("m0", [B, 8, NS], F32)
        sync, tensor, scalar, tot_ready = reduce_units(nc, sh, sum_d, F0, tot, 0, sbp, semp)
        link_s, asked, answered = semp("nlink0"), semp("asked0"), semp("answered0")
        root_asked, root_ready, val_ready, tab_out = semp("root_asked0"), semp("root_ready0"), semp("val_ready0"), semp("tab_out0")
        block = scope.enter_context(nc.Block())

        @block.sync
        def _(sp):
            sync(sp)
            sp.wait_ge(val_ready, 1)
            sp.dma_start(tab_d.rearrange("(b l) f -> b l f", l=L), val[:, :, :]).then_inc(tab_out, 16)
            sp.wait_ge(tab_out, 16)

        @block.tensor
        def _(pe):
            tensor(pe)
            for k, row in enumerate((0, 1, 2)):
                pe.wait_ge(asked, k + 1)
                nc.tensor.matmul(ps[0:B, 0, k * NS:(k + 1) * NS], ones[0:B, 0:B], m[:, row, :], start=True,
                                 stop=True).then_inc(answered, 1)

        @block.scalar
        def _(act):
            scalar(act)
            for k in range(2):
                act.wait_ge(root_asked, k + 1)
                nc.scalar.activation(m[:, 4 + k, :], m[:, 4 + k, :], ACT.Sqrt).then_inc(root_ready, 1)

        @block.vector
        def _(dve):
            link = Linker(dve, link_s)
            over_l = lambda a: a.rearrange("b l f -> b f l")
            bc = lambda row, w=NS: m[:, row, 0:w].unsqueeze(1).to_broadcast([B, L, w])
            dve.wait_ge(tot_ready, 1)
            link(nc.vector.tensor_scalar(sh.rcount[:, :], tot[:, 0:L, F0 - 1], 1.0, None, ALU.max))
            link(nc.vector.reciprocal(sh.rcount[:, :], sh.rcount[:, :]))
            link(nc.vector.tensor_tensor(val[:, :, :], tot[:, 0:L, 0:T0],
                                         sh.rcount[:, :].unsqueeze(2).to_broadcast([B, L, T0]), ALU.mult))
            link(nc.vector.tensor_scalar(val[:, :, 0:NS], val[:, :, 0:NS], float(NS) ** -0.5, None, ALU.mult))
            link(nc.vector.tensor_scalar(val[:, :, NS:T0], val[:, :, NS:T0], (3.0 / NS) ** 0.5, None, ALU.mult))
            link(nc.vector.tensor_reduce(m[:, 0, :], over_l(val[:, :, 0:NS]), AX.X, ALU.add))
            dve.engine_nop().then_inc(asked, 1)
            link(nc.vector.tensor_tensor(sq[:, :, NS:T0], val[:, :, NS:T0], val[:, :, NS:T0], ALU.mult))
            link(nc.vector.memset(m[:, 2, :], 0.0))
            link(nc.vector.tensor_reduce(m[:, 7, 0:12], over_l(sq[:, :, NS:T0]), AX.X, ALU.add))
            link(nc.vector.tensor_reduce(m[:, 2, 0:NV], m[:, 7, 0:12].rearrange("b (j c) -> b j c", c=3), AX.X, ALU.add))
            dve.wait_ge(answered, 1)
            link(nc.vector.tensor_scalar(m[:, 3, :], ps[0:B, 0, 0:NS], 1.0 / N, None, ALU.mult))
            link(nc.vector.tensor_tensor(val[:, :, 0:NS], val[:, :, 0:NS], bc(3), ALU.subtract))
            link(nc.vector.tensor_tensor(sq[:, :, 0:NS], val[:, :, 0:NS], val[:, :, 0:NS], ALU.mult))
            link(nc.vector.tensor_reduce(m[:, 1, :], over_l(sq[:, :, 0:NS]), AX.X, ALU.add))
            dve.engine_nop().then_inc(asked, 2)
            dve.wait_ge(answered, 3)
            link(nc.vector.tensor_scalar(m[:, 4, :], ps[0:B, 0, NS:2 * NS], 1.0 / N, EPS, ALU.mult, ALU.add))
            link(nc.vector.tensor_scalar(m[:, 5, :], ps[0:B, 0, 2 * NS:3 * NS], 1.0 / (3 * N), EPS, ALU.mult, ALU.add))
            dve.engine_nop().then_inc(root_asked, 2)
            dve.wait_ge(root_ready, 2)
            link(nc.vector.reciprocal(m[:, 4:6, :], m[:, 4:6, :]))
            link(nc.vector.tensor_tensor(m[:, 4, :], m[:, 4, :], rows[:, 0:NS], ALU.mult))
            link(nc.vector.tensor_tensor(m[:, 5, 0:NV], m[:, 5, 0:NV], rows[:, 2 * NS:2 * NS + NV], ALU.mult))
            link(nc.vector.tensor_copy(m[:, 6, 0:12].rearrange("b (j c) -> b j c", c=3),
                                       m[:, 5, 0:NV].unsqueeze(2).to_broadcast([B, NV, 3])))
            link(nc.vector.tensor_tensor(val[:, :, 0:NS], val[:, :, 0:NS], bc(4), ALU.mult))
            link(nc.vector.tensor_tensor(val[:, :, 0:NS], val[:, :, 0:NS],
                                         rows[:, NS:2 * NS].unsqueeze(1).to_broadcast([B, L, NS]), ALU.add))
            link(nc.vector.tensor_tensor(val[:, :, NS:T0], val[:, :, NS:T0], bc(6, 12), ALU.mult))
            dve.engine_nop().then_inc(val_ready, 1)


def pass_1(nc, sh, w2_1, tab_d, sum_d):
    G, ps = sh.G, sh.ps
    scope = ExitStack()
    with scope:
        sbp, semp = sh.alloc(scope)
        comp = sbp("comp1", [P, RING, GROUP, CMP], F32)
        at = sbp("at1", [P, RING, GROUP], I32)
        xs = sbp("xs1", [P, RING, GROUP, T0], F32)
        hid = sbp("hid1", [HID + 1, RING, GROUP * P], F32)
        w2s = sbp("w2s1", [HID + 1, 320], F32)
        vr = sbp("vr", [P, GROUP, NV, 3], F32)
        xin = sbp("xin1", [P, 2, GROUP, 20], F32)
        prod = sbp("prod1", [P, 2, 2, NS, 20], F32)
        msg = sbp("msg1", [P, 2, GROUP, NS], F32)
        owns = sbp("owns1", [P, 2, GROUP, P], F32)
        sums = sbp("sums1_sb", [P, RING, GU, NS], F32)
        comp_in = [semp(f"comp_in{k}") for k in range(RING)]
        hid_in = [semp(f"hid_in{k}") for k in range(RING)]
        xs_in = [semp(f"xs_in1{k}", True) for k in range(RING)]
        sums_out = [semp(f"sums_out1{k}") for k in range(RING)]
        w_in, hid_one, at_ready = semp("w_in1"), semp("hid_one"), semp("at_ready1")
        weights_ready, prod_ready, msg_ready = semp("weights_ready1"), semp("prod_ready1"), semp("msg_ready1")
        owns_ready, summed, sums_ready = semp("owns_ready1"), semp("summed1"), semp("sums_ready1")
        vr_ready, xin_ready = semp("vr_ready"), semp("xin_ready")
        turn = semp("pool_turn1")
        block = scope.enter_context(nc.Block())

        @block.sync
        def _(sp):
            sp.dma_start(w2s[:, :], w2_1).then_inc(w_in, 16)
            sp.wait_ge(hid_one, 1)

            def step(n):
                if exists(n, 5, G):
                    slot = moved(n, 5)[1]
                    if exists(n, 1, G):
                        sp.wait_ge(at_ready, count(n, 1))
                        sp.wait_ge(owns_ready, count(n, 1))
                        sp.wait_ge(xin_ready, count(n, 1))
                    sp.dma_start(comp[:, slot].rearrange("p t f -> p (t f)"),
                                 sh.cmp_d[bass.ds(index(n, 5), 1)].rearrange("o p x -> p (o x)"))\
                      .then_inc(comp_in[slot], 16)
                if exists(n, 4, G):
                    slot = moved(n, 4)[1]
                    if exists(n, 0, G):
                        sp.wait_ge(weights_ready, count(n, 0, 2))
                    sp.dma_start(hid[0:HID, slot, :], sh.hid_d[bass.ds(index(n, 4), 1)].rearrange("o k e -> k (o e)"))\
                      .then_inc(hid_in[slot], 16)
                if exists(n, -1, G):
                    slot = moved(n, -1)[1]
                    sp.wait_ge(sums_ready, count(n, -1))
                    sp.dma_start(sum_d[bass.ds(index(n, -1), 1)].rearrange("o p x -> p (o x)"),
                                 sums[:, slot].rearrange("p u f -> p (u f)")).then_inc(sums_out[slot], 16)
            walk(sp, step, G)
            for k in range(RING):
                sp.wait_ge(sums_out[k], 16 * (G // RING))

        @block.gpsimd
        def _(pool):
            def step(n):
                if exists(n, 3, G):
                    slot = moved(n, 3)[1]
                    pool.wait_ge(at_ready, count(n, 3))
                    if exists(n, -1, G):
                        pool.wait_ge(xin_ready, count(n, -1))
                    pool.sem_inc(turn, 1)
                    for t in range(GROUP):
                        nc.gpsimd.indirect_dma_start(
                            out=xs[:, slot, t, :], out_offset=None, in_=tab_d,
                            in_offset=bass.IndirectOffsetOnAxis(ap=at[:, slot, t:t + 1], axis=0))\
                          .then_inc(xs_in[slot], 16)
            walk(pool, step, G)

        @block.scalar
        def _(act):
            def step(n):
                if exists(n, 3, G):
                    slot = moved(n, 3)[1]
                    act.wait_ge(comp_in[slot], used(n, 3))
                    if exists(n, -1, G):
                        act.wait_ge(xs_in[slot], used(n, -1, 16 * GROUP))
                    nc.scalar.activation(at[:, slot], comp[:, slot, :, C_DST], ACT.Copy).then_inc(at_ready, 1)
                if exists(n, -2, G):
                    slot = moved(n, -2)[1]
                    act.wait_ge(summed, count(n, -2))
                    if exists(n, -6, G):
                        act.wait_ge(sums_out[slot], used(n, -6))
                    nc.scalar.activation(sums[:, slot], ps[:, 6 + slot % 2, 0:GU * NS]
                                         .rearrange("p (u f) -> p u f", f=NS), ACT.Copy).then_inc(sums_ready, 1)
            walk(act, step, G)

        @block.tensor
        def _(pe):
            pe.wait_ge(w_in, 16)

            def step(n):
                if exists(n, 0, G):
                    pe.wait_ge(hid_in[n[1]], used(n))
                    for q in range(2):
                        if exists(n, -1, G):
                            pe.wait_ge(prod_ready, count(n, -1, 2) - 1 + q)
                        for t in (2 * q, 2 * q + 1):
                            last = nc.tensor.matmul(ps[:, 2 + t, 0:320], hid[:, n[1], t * P:(t + 1) * P],
                                                    w2s[:, :], start=True, stop=True)
                        last.then_inc(weights_ready, 1)
                if exists(n, -1, G):
                    half = (n[1] + 1) % 2
                    pe.wait_ge(msg_ready, count(n, -1, 2))
                    pe.wait_ge(owns_ready, count(n, -1))
                    if exists(n, -3, G):
                        pe.wait_ge(sums_ready, count(n, -3))
                    for u in range(GU):
                        for j in range(UNIT):
                            t = u * UNIT + j
                            last = nc.tensor.matmul(ps[:, 6 + half, u * NS:(u + 1) * NS], owns[:, half, t, :],
                                                    msg[:, half, t, :], start=(j == 0), stop=(j == UNIT - 1))
                    last.then_inc(summed, 1)
            walk(pe, step, G)

        @block.vector
        def _(dve):
            nc.vector.memset(hid[:, :, :], 1.0).then_inc(hid_one, 1)

            def inputs(n, by):
                slot, half = moved(n, by)[1], moved(n, by)[1] % 2
                dve.wait_ge(xs_in[slot], used(n, by, 16 * GROUP))
                dve.wait_ge(comp_in[slot], used(n, by))
                nc.vector.tensor_tensor(
                    vr[:, :, :, :], xs[:, slot, :, NS:T0].rearrange("p t (i c) -> p t i c", c=3),
                    comp[:, slot, :, C_RHAT:C_RHAT + 3].unsqueeze(2).to_broadcast([P, GROUP, NV, 3]),
                    ALU.mult).then_inc(vr_ready, 1)
                nc.vector.tensor_copy(xin[:, half, :, 0:NS], xs[:, slot, :, 0:NS])
                for t in range(GROUP):
                    last = nc.vector.tensor_scalar(owns[:, half, t, :], iota_p[:, :], comp[:, slot, t, C_LO:C_LO + 1],
                                                   None, ALU.is_equal)
                last.then_inc(owns_ready, 1)
                dve.wait_ge(vr_ready, count(n, by))
                nc.vector.tensor_reduce(xin[:, half, :, NS:20], vr[:, :, :, :], AX.X, ALU.add).then_inc(xin_ready, 1)
            iota_p = sh.iota_p

            def step(n):
                if not exists(n, 0, G):
                    return
                half = n[1] % 2
                if exists(n, -2, G):
                    dve.wait_ge(summed, count(n, -2))
                inputs(n, 0)
                dve.wait_ge(xin_ready, count(n))
                for q in range(2):
                    dve.wait_ge(weights_ready, count(n, 0, 2) - 1 + q)
                    nc.vector.tensor_tensor(
                        prod[:, q], ps[:, 2 + 2 * q:4 + 2 * q, 0:320].rearrange("p t (j i) -> p t j i", i=20),
                        xin[:, half, 2 * q:2 * q + 2, :].unsqueeze(2).to_broadcast([P, 2, NS, 20]),
                        ALU.mult).then_inc(prod_ready, 1)
                for q in range(2):
                    dve.wait_ge(prod_ready, count(n, 0, 2) - 1 + q)
                    nc.vector.tensor_reduce(msg[:, half, 2 * q:2 * q + 2, :], prod[:, q], AX.X, ALU.add)\
                      .then_inc(msg_ready, 1)
            walk(dve, step, G)


def block_diagonal(sp, dst, src, blocks, width, done):
    for k in range(blocks):
        sp.dma_start(dst[k * NS:(k + 1) * NS, k * width:(k + 1) * width], src).then_inc(done, 16)


NB = 5


def nodes_1(nc, sh, sum_d, w_msg, tab_d):
    B, N, ps, ones, rows = sh.B, sh.N, sh.ps, sh.ones, sh.rows_sb
    L = LOCAL
    steps = L // NB
    scope = ExitStack()
    with scope:
        sbp, semp = sh.alloc(scope)
        tot = sbp("tot1", [B, P, NS], F32)
        val = sbp("val1", [B, L, NS], F32)
        sq = sbp("sq1", [B, L, NS], F32)
        m = sbp("m1", [B, 8, NS], F32)
        lnv = sbp("lnv1", [B, L], F32)
        wd = sbp("wd", [NB * NS, NB * P], F32)
        h_t = sbp("h_t", [NB * NS, 2, B], F32)
        tab = sbp("tab", [B, 4, NB * P], F32)
        sync, tensor, scalar, tot_ready = reduce_units(nc, sh, sum_d, NS, tot, 1, sbp, semp)
        link_s, asked, answered = semp("nlink1"), semp("asked1"), semp("answered1")
        root_asked, root_ready, h_ready = semp("root_asked1"), semp("root_ready1"), semp("h_ready1")
        wd_zero, wd_in, h_on_pe, h_t_ready = semp("wd_zero"), semp("wd_in"), semp("h_on_pe"), semp("h_t_ready")
        rows_on_pe, tab_ready = semp("rows_on_pe"), semp("tab_ready")
        tab_out = [semp(f"tab_out1{s}") for s in range(4)]
        block = scope.enter_context(nc.Block())

        @block.gpsimd
        def _(pool):
            nc.gpsimd.memset(wd[:, :], 0.0).then_inc(wd_zero, 1)

        @block.sync
        def _(sp):
            sync(sp)
            sp.wait_ge(wd_zero, 1)
            block_diagonal(sp, wd, w_msg, NB, P, wd_in)
            tab_v = tab_d.rearrange("(b l) f -> b l f", l=L)
            for k in range(steps):
                sp.wait_ge(tab_ready, k + 1)
                sp.dma_start(tab_v[:, k * NB:(k + 1) * NB, :].rearrange("b l f -> b (l f)"), tab[:, k % 4, :])\
                  .then_inc(tab_out[k % 4], 16)
            for s in range(4):
                sp.wait_ge(tab_out[s], 16 * len(range(s, steps, 4)))

        @block.tensor
        def _(pe):
            tensor(pe)
            for k in range(2):
                pe.wait_ge(asked, k + 1)
                nc.tensor.matmul(ps[0:B, 0, k * NS:(k + 1) * NS], ones[0:B, 0:B], m[:, k, :], start=True,
                                 stop=True).then_inc(answered, 1)
            pe.wait_ge(h_ready, 1)
            pe.wait_ge(wd_in, 16 * NB)

            def turn(k):
                if k >= 2:
                    pe.wait_ge(h_t_ready, k - 1)
                nc.tensor.transpose(ps[0:NB * NS, 1 + k % 2, 0:B],
                                    sh.h_sb[:, k * NB:(k + 1) * NB, :].rearrange("b l f -> b (l f)"),
                                    sh.ident[0:B, 0:B]).then_inc(h_on_pe, 1)
            turn(0)
            for k in range(steps):
                if k + 1 < steps:
                    turn(k + 1)
                pe.wait_ge(h_t_ready, k + 1)
                if k >= 2:
                    pe.wait_ge(tab_ready, k - 1)
                for s in range(2):
                    half = NB * P // 2
                    last = nc.tensor.matmul(ps[0:B, 4 + 2 * (k % 2) + s, 0:half], h_t[:, k % 2, :],
                                            wd[:, s * half:(s + 1) * half], start=True, stop=True)
                last.then_inc(rows_on_pe, 1)

        @block.scalar
        def _(act):
            scalar(act)
            act.wait_ge(root_asked, 1)
            nc.scalar.activation(m[:, 4, :], m[:, 4, :], ACT.Sqrt).then_inc(root_ready, 1)
            act.wait_ge(root_asked, 2)
            nc.scalar.activation(lnv[:, :], lnv[:, :], ACT.Sqrt).then_inc(root_ready, 1)
            for k in range(steps):
                act.wait_ge(rows_on_pe, k + 1)
                if k >= 4:
                    act.wait_ge(tab_out[k % 4], 16 * (k // 4))
                half = NB * P // 2
                nc.scalar.activation(tab[:, k % 4, :].rearrange("b (s x) -> b s x", s=2),
                                     ps[0:B, 4 + 2 * (k % 2):6 + 2 * (k % 2), 0:half], ACT.Copy).then_inc(tab_ready, 1)

        @block.vector
        def _(dve):
            link = Linker(dve, link_s)
            over_l = lambda a: a.rearrange("b l f -> b f l")
            bc = lambda row: m[:, row, :].unsqueeze(1).to_broadcast([B, L, NS])
            dve.wait_ge(tot_ready, 1)
            link(nc.vector.tensor_tensor(val[:, :, :], tot[:, 0:L, :],
                                         sh.rcount[:, :].unsqueeze(2).to_broadcast([B, L, NS]), ALU.mult))
            link(nc.vector.tensor_scalar(val[:, :, :], val[:, :, :], float(NS + NV) ** -0.5, None, ALU.mult))
            link(nc.vector.tensor_reduce(m[:, 0, :], over_l(val[:, :, :]), AX.X, ALU.add))
            dve.engine_nop().then_inc(asked, 1)
            dve.wait_ge(answered, 1)
            link(nc.vector.tensor_scalar(m[:, 3, :], ps[0:B, 0, 0:NS], 1.0 / N, None, ALU.mult))
            link(nc.vector.tensor_tensor(val[:, :, :], val[:, :, :], bc(3), ALU.subtract))
            link(nc.vector.tensor_tensor(sq[:, :, :], val[:, :, :], val[:, :, :], ALU.mult))
            link(nc.vector.tensor_reduce(m[:, 1, :], over_l(sq[:, :, :]), AX.X, ALU.add))
            dve.engine_nop().then_inc(asked, 1)
            dve.wait_ge(answered, 2)
            link(nc.vector.tensor_scalar(m[:, 4, :], ps[0:B, 0, NS:2 * NS], 1.0 / N, EPS, ALU.mult, ALU.add))
            dve.engine_nop().then_inc(root_asked, 1)
            dve.wait_ge(root_ready, 1)
            link(nc.vector.reciprocal(m[:, 4, :], m[:, 4, :]))
            g0 = 2 * NS + NV
            link(nc.vector.tensor_tensor(m[:, 4, :], m[:, 4, :], rows[:, g0:g0 + NS], ALU.mult))
            link(nc.vector.tensor_tensor(val[:, :, :], val[:, :, :], bc(4), ALU.mult))
            link(nc.vector.tensor_tensor(val[:, :, :], val[:, :, :],
                                         rows[:, g0 + NS:g0 + 2 * NS].unsqueeze(1).to_broadcast([B, L, NS]), ALU.add))
            link(nc.vector.tensor_tensor(sh.x_sb[:, :, :], sh.x_sb[:, :, :], val[:, :, :], ALU.add))
            sh.layernorm_relu(dve, link, sh.x_sb, sh.h_sb, lnv, sq, root_asked, root_ready, 2)
            dve.engine_nop().then_inc(h_ready, 1)
            for k in range(steps):
                dve.wait_ge(h_on_pe, k + 1)
                if k >= 2:
                    dve.wait_ge(rows_on_pe, k - 1)
                nc.vector.tensor_copy(h_t[:, k % 2, :], ps[0:NB * NS, 1 + k % 2, 0:B]).then_inc(h_t_ready, 1)


def pass_2(nc, sh, tab_d, sum_d):
    G, ps = sh.G, sh.ps
    scope = ExitStack()
    with scope:
        sbp, semp = sh.alloc(scope)
        comp = sbp("comp2", [P, RING, GROUP, CMP], F32)
        at = sbp("at2", [P, RING, GROUP], I32)
        ys = sbp("ys", [P, RING, GROUP, NS * 8], F32)
        prod = sbp("prod2", [P, 2, GROUP, NS, 8], F32)
        pre = sbp("pre2", [P, 2, GROUP, NS], F32)
        msg = sbp("msg2", [P, 2, GROUP, NS], F32)
        owns = sbp("owns2", [P, 2, GROUP, P], F32)
        sums = sbp("sums2_sb", [P, RING, GU, NS], F32)
        comp_in = [semp(f"comp_in2{k}") for k in range(RING)]
        ys_in = [semp(f"ys_in{k}", True) for k in range(RING)]
        sums_out = [semp(f"sums_out2{k}") for k in range(RING)]
        at_ready, prod_ready, pre_ready, msg_ready = semp("at_ready2"), semp("prod_ready2"), semp("pre_ready2"), semp("msg_ready2")
        owns_ready, summed, sums_ready, turn = semp("owns_ready2"), semp("summed2"), semp("sums_ready2"), semp("pool_turn2")
        block = scope.enter_context(nc.Block())

        @block.sync
        def _(sp):
            def step(n):
                if exists(n, 5, G):
                    slot = moved(n, 5)[1]
                    if exists(n, 1, G):
                        sp.wait_ge(at_ready, count(n, 1))
                        sp.wait_ge(owns_ready, count(n, 1))
                    sp.dma_start(comp[:, slot].rearrange("p t f -> p (t f)"),
                                 sh.cmp_d[bass.ds(index(n, 5), 1)].rearrange("o p x -> p (o x)"))\
                      .then_inc(comp_in[slot], 16)
                if exists(n, -1, G):
                    slot = moved(n, -1)[1]
                    sp.wait_ge(sums_ready, count(n, -1))
                    sp.dma_start(sum_d[bass.ds(index(n, -1), 1)].rearrange("o p x -> p (o x)"),
                                 sums[:, slot].rearrange("p u f -> p (u f)")).then_inc(sums_out[slot], 16)
            walk(sp, step, G)
            for k in range(RING):
                sp.wait_ge(sums_out[k], 16 * (G // RING))

        @block.gpsimd
        def _(pool):
            def step(n):
                if exists(n, 3, G):
                    slot = moved(n, 3)[1]
                    pool.wait_ge(at_ready, count(n, 3))
                    if exists(n, -1, G):
                        pool.wait_ge(prod_ready, count(n, -1))
                    pool.sem_inc(turn, 1)
                    for t in range(GROUP):
                        nc.gpsimd.indirect_dma_start(
                            out=ys[:, slot, t, :], out_offset=None, in_=tab_d,
                            in_offset=bass.IndirectOffsetOnAxis(ap=at[:, slot, t:t + 1], axis=0))\
                          .then_inc(ys_in[slot], 16)
            walk(pool, step, G)

        @block.scalar
        def _(act):
            def step(n):
                if exists(n, 3, G):
                    slot = moved(n, 3)[1]
                    act.wait_ge(comp_in[slot], used(n, 3))
                    if exists(n, -1, G):
                        act.wait_ge(ys_in[slot], used(n, -1, 16 * GROUP))
                    nc.scalar.activation(at[:, slot], comp[:, slot, :, C_DST], ACT.Copy).then_inc(at_ready, 1)
                if exists(n, -1, G):
                    half = (n[1] + 1) % 2
                    act.wait_ge(pre_ready, count(n, -1))
                    if exists(n, -3, G):
                        act.wait_ge(summed, count(n, -3))
                    nc.scalar.activation(msg[:, half], pre[:, half], ACT.Silu, scale=float(NS * 8) ** -0.5)\
                      .then_inc(msg_ready, 1)
                if exists(n, -3, G):
                    slot = moved(n, -3)[1]
                    act.wait_ge(summed, count(n, -3))
                    if exists(n, -7, G):
                        act.wait_ge(sums_out[slot], used(n, -7))
                    nc.scalar.activation(sums[:, slot], ps[:, 6 + slot % 2, 0:GU * NS]
                                         .rearrange("p (u f) -> p u f", f=NS), ACT.Copy).then_inc(sums_ready, 1)
            walk(act, step, G)

        @block.tensor
        def _(pe):
            def step(n):
                if exists(n, -1, G):
                    half = (n[1] + 1) % 2
                    pe.wait_ge(msg_ready, count(n, -1))
                    pe.wait_ge(owns_ready, count(n, -1))
                    if exists(n, -3, G):
                        pe.wait_ge(sums_ready, count(n, -3))
                    for u in range(GU):
                        for j in range(UNIT):
                            t = u * UNIT + j
                            last = nc.tensor.matmul(ps[:, 6 + half, u * NS:(u + 1) * NS], owns[:, half, t, :],
                                                    msg[:, half, t, :], start=(j == 0), stop=(j == UNIT - 1))
                    last.then_inc(summed, 1)
            walk(pe, step, G)

        @block.vector
        def _(dve):
            def step(n):
                if not exists(n, 0, G):
                    return
                slot, half = n[1], n[1] % 2
                dve.wait_ge(ys_in[slot], used(n, 0, 16 * GROUP))
                dve.wait_ge(comp_in[slot], used(n))
                nc.vector.tensor_tensor(prod[:, half], ys[:, slot].rearrange("p t (h j) -> p t h j", j=8),
                                        comp[:, slot, :, C_EA8:C_EA8 + 8].unsqueeze(2).to_broadcast([P, GROUP, NS, 8]),
                                        ALU.mult).then_inc(prod_ready, 1)
                if exists(n, -2, G):
                    dve.wait_ge(summed, count(n, -2))
                for t in range(GROUP):
                    last = nc.vector.tensor_scalar(owns[:, half, t, :], sh.iota_p[:, :], comp[:, slot, t, C_LO:C_LO + 1],
                                                   None, ALU.is_equal)
                last.then_inc(owns_ready, 1)
                dve.wait_ge(prod_ready, count(n))
                nc.vector.tensor_reduce(pre[:, half], prod[:, half], AX.X, ALU.add).then_inc(pre_ready, 1)
            walk(dve, step, G)


def nodes_2(nc, sh, sum_d, w_lin_t, w_upd, w_out, out):
    B, ps = sh.B, sh.ps
    L = LOCAL
    steps = L // NB
    W = NB * NS
    scope = ExitStack()
    with scope:
        sbp, semp = sh.alloc(scope)
        tot = sbp("tot2", [B, P, NS], F32)
        lin_d = sbp("lin_d", [W, W], F32)
        upd_d = sbp("upd_d", [W, NB * 256], F32)
        both_d = sbp("both_d", [W, NB * 256], F32)
        out_d = sbp("out_d", [W, W], F32)
        a_t = sbp("a_t", [W, 2, B], F32)
        hv = sbp("hv", [B, 2, NB * 256], F32)
        u = sbp("u", [B, L, NS], F32)
        su = sbp("su", [B, L, NS], F32)
        sync, tensor, scalar, tot_ready = reduce_units(nc, sh, sum_d, NS, tot, 2, sbp, semp)
        zero, w_in, both_on_pe, both_ready = semp("zero2"), semp("w_in2"), semp("both_on_pe"), semp("both_ready")
        a_on_pe, a_t_ready, v_on_pe, hv_ready = semp("a_on_pe"), semp("a_t_ready"), semp("v_on_pe"), semp("hv_ready")
        u_ready, su_ready, s_on_pe, s_t_ready = semp("u_ready"), semp("su_ready"), semp("s_on_pe"), semp("s_t_ready")
        o_on_pe, x_ready, out_done, xh_ready = semp("o_on_pe"), semp("x_ready"), semp("out_done"), semp("xh_ready")
        block = scope.enter_context(nc.Block())
        v_cuts = [(0, 2), (2, 4), (4, 5)]

        @block.gpsimd
        def _(pool):
            for t in (lin_d, upd_d, out_d):
                nc.gpsimd.memset(t[:, :], 0.0).then_inc(zero, 1)

        @block.sync
        def _(sp):
            sync(sp)
            sp.wait_ge(zero, 3)
            block_diagonal(sp, lin_d, w_lin_t, NB, NS, w_in)
            block_diagonal(sp, upd_d, w_upd, NB, 256, w_in)
            block_diagonal(sp, out_d, w_out, NB, NS, w_in)
            sp.wait_ge(x_ready, steps)
            sp.dma_start(out.rearrange("(b l) f -> b l f", l=L), sh.x_sb[:, :, :]).then_inc(out_done, 16)
            sp.wait_ge(out_done, 16)

        @block.tensor
        def _(pe):
            tensor(pe)
            pe.wait_ge(w_in, 16 * 3 * NB)
            for c, (a, b) in enumerate(v_cuts):
                last = nc.tensor.matmul(ps[0:W, c, 0:(b - a) * 256], lin_d[:, :], upd_d[:, a * 256:b * 256],
                                        start=True, stop=True)
            last.then_inc(both_on_pe, 1)
            pe.wait_ge(both_ready, 1)
            for k in range(steps):
                l0 = slice(k * NB, (k + 1) * NB)
                if k >= 1:
                    pe.wait_ge(a_t_ready, k)
                nc.tensor.transpose(ps[0:W, 7, 0:B], tot[:, l0, :].rearrange("b l f -> b (l f)"),
                                    sh.ident[0:B, 0:B]).then_inc(a_on_pe, 1)
                pe.wait_ge(a_t_ready, k + 1)
                if k >= 2:
                    pe.wait_ge(hv_ready, k - 1)
                for c, (a, b) in enumerate(v_cuts):
                    last = nc.tensor.matmul(ps[0:B, 3 * (k % 2) + c, 0:(b - a) * 256], a_t[:, k % 2, :],
                                            both_d[:, a * 256:b * 256], start=True, stop=True)
                last.then_inc(v_on_pe, 1)
            pe.wait_ge(su_ready, 1)
            for k in range(steps):
                l0 = slice(k * NB, (k + 1) * NB)
                if k >= 2:
                    pe.wait_ge(s_t_ready, k - 1)
                nc.tensor.transpose(ps[0:W, k % 2, 0:B], su[:, l0, :].rearrange("b l f -> b (l f)"),
                                    sh.ident[0:B, 0:B]).then_inc(s_on_pe, 1)
                pe.wait_ge(s_t_ready, k + 1)
                if k >= 2:
                    pe.wait_ge(x_ready, k - 1)
                nc.tensor.matmul(ps[0:B, 2 + k % 2, 0:W], a_t[:, k % 2, :], out_d[:, :], start=True,
                                 stop=True).then_inc(o_on_pe, 1)

        @block.scalar
        def _(act):
            scalar(act)
            act.wait_ge(both_on_pe, 1)
            for c, (a, b) in enumerate(v_cuts):
                last = nc.scalar.activation(both_d[:, a * 256:b * 256], ps[0:W, c, 0:(b - a) * 256], ACT.Copy)
            last.then_inc(both_ready, 1)
            for k in range(steps):
                act.wait_ge(a_on_pe, k + 1)
                if k >= 2:
                    act.wait_ge(v_on_pe, k - 1)
                nc.scalar.activation(a_t[:, k % 2, :], ps[0:W, 7, 0:B], ACT.Copy).then_inc(a_t_ready, 1)
            act.wait_ge(u_ready, steps)
            nc.scalar.activation(su[:, :, :], u[:, :, :], ACT.Silu, scale=(NS * NS * NS) ** -0.5).then_inc(su_ready, 1)
            for k in range(steps):
                act.wait_ge(s_on_pe, k + 1)
                if k >= 2:
                    act.wait_ge(o_on_pe, k - 1)
                nc.scalar.activation(a_t[:, k % 2, :], ps[0:W, k % 2, 0:B], ACT.Copy).then_inc(s_t_ready, 1)

        @block.vector
        def _(dve):
            nc.vector.tensor_tensor(sh.x_sb[:, :, :], sh.x_sb[:, :, :], sh.h_sb[:, :, :], ALU.add).then_inc(xh_ready, 1)
            for k in range(steps):
                dve.wait_ge(v_on_pe, k + 1)
                for c, (a, b) in enumerate(v_cuts):
                    h_of = sh.h_sb[:, k * NB + a:k * NB + b, :].unsqueeze(2).to_broadcast([B, b - a, NS, NS])
                    last = nc.vector.tensor_tensor(
                        hv[:, k % 2, a * 256:b * 256].rearrange("b (l k i) -> b l k i", k=NS, i=NS),
                        ps[0:B, 3 * (k % 2) + c, 0:(b - a) * 256].rearrange("b (l k i) -> b l k i", k=NS, i=NS),
                        h_of, ALU.mult)
                last.then_inc(hv_ready, 1)
                dve.wait_ge(hv_ready, k + 1)
                nc.vector.tensor_reduce(u[:, k * NB:(k + 1) * NB, :], hv[:, k % 2, :]
                                        .rearrange("b (l k i) -> b l k i", k=NS, i=NS), AX.X, ALU.add).then_inc(u_ready, 1)
            dve.wait_ge(xh_ready, 1)
            for k in range(steps):
                dve.wait_ge(o_on_pe, k + 1)
                x_of = sh.x_sb[:, k * NB:(k + 1) * NB, :].rearrange("b l f -> b (l f)")
                nc.vector.scalar_tensor_tensor(out=x_of, in0=ps[0:B, 2 + k % 2, 0:W], scalar=float(NS) ** -0.5,
                                               in1=x_of, op0=ALU.mult, op1=ALU.add).then_inc(x_ready, 1)


_INS = ["x", "src", "dst", "ea3", "ea48", "ea8", "w1", "b1", "w2_0", "w2_1", "rows", "w_msg", "w_lin_t", "w_upd", "w_out"]


def lay_out(i):
    f = lambda n: np.ascontiguousarray(i[n])
    g = "L0_gnn_"

    def second(k):
        w, b = f(f"{g}fc{k}_w2"), f(f"{g}fc{k}_b2")
        w = np.concatenate([w, b[None, :]], 0)
        a, v = w[:, :NS * NS].reshape(-1, NS, NS), w[:, NS * NS:]
        if k == 0:
            v = v.reshape(-1, NS, NV)
            return np.ascontiguousarray(np.concatenate([v.transpose(0, 2, 1), a.transpose(0, 2, 1)], 1).reshape(-1, 320))
        v = v.reshape(-1, NV, NS)
        return np.ascontiguousarray(np.concatenate([a.transpose(0, 2, 1), v.transpose(0, 2, 1)], 2).reshape(-1, 320))

    rows = np.concatenate([f(g + n) for n in ("bn0_gs", "bn0_bs", "bn0_gv", "bn1_gs", "bn1_bs")])[None, :]
    return {
        "x": f("x"), "src": f("src"), "dst": f("dst"), "ea3": f("edge_attr_3"), "ea48": f("edge_attr_48"),
        "ea8": f("edge_attr_8"),
        "w1": np.stack([f(g + "fc0_w1"), f(g + "fc1_w1")]), "b1": np.stack([f(g + "fc0_b1"), f(g + "fc1_b1")])[:, :, None],
        "w2_0": second(0), "w2_1": second(1), "rows": np.ascontiguousarray(rows),
        "w_msg": np.ascontiguousarray(f("L1_gnn_W_msg_tp").transpose(0, 2, 1).reshape(NS, 128)),
        "w_lin_t": np.ascontiguousarray(f("L1_gnn_W_msg_lin").T),
        "w_upd": np.ascontiguousarray(f("L1_gnn_W_upd_tp").transpose(1, 2, 0).reshape(NS, 256)),
        "w_out": f("L1_gnn_W_upd_lin"),
    }


def kernel(**inputs):
    import numpy as _np
    import concourse.bacc as _bacc
    from concourse import mybir as _mybir
    from concourse.bass_utils import run_bass_kernel_spmd as _run

    nc = _bacc.Bacc("TRN2", target_bir_lowering=False, num_devices=1)
    given = lay_out({n: _np.asarray(a) for n, a in inputs.items()})
    arrays, args = {}, []
    for name in _INS:
        a = given[name]
        arrays[f"in_{name}"] = a
        args.append(nc.dram_tensor(f"in_{name}", a.shape, _mybir.dt.from_np(a.dtype), kind="ExternalInput").ap())
    out = nc.dram_tensor("out_0", given["x"].shape, _mybir.dt.float32, kind="ExternalOutput").ap()
    gnn(nc, *args, out)
    r = _run(nc, [arrays], core_ids=[0])
    return r.results[0]["out_0"]
```

```python
import numpy as np
import concourse.bass as bass
from concourse import mybir
from contextlib import ExitStack

F32 = mybir.dt.float32
BF16 = mybir.dt.bfloat16
FP16 = mybir.dt.float16
I32 = mybir.dt.int32
U32 = mybir.dt.uint32
U16 = mybir.dt.uint16
ALU = mybir.AluOpType
ACT = mybir.ActivationFunctionType
AX = mybir.AxisListType

P = 128
LOCAL = 125
UNIT = 2
GROUP = 4
GU = GROUP // UNIT
RING = 4
EPS = 1e-5

SMALL = 72
CMP = 13
C_EA8, C_RHAT, C_NLO, C_DST = 0, 8, 11, 12
PART0 = (0, 2 * (SMALL + CMP))

NS, NV, HID = 16, 4, 48
REC = 2 * SMALL + CMP
F0 = NS + 3 * NV + 1
T0 = NS + 3 * NV



def moved(n, by):
    body, slot = n
    return body + (slot + by) // RING, (slot + by) % RING


def exists(n, by, groups):
    body, slot = moved(n, by)
    return not isinstance(body, int) or 0 <= body * RING + slot < groups


def index(n, by=0):
    body, slot = moved(n, by)
    return body * RING + slot


def count(n, by=0, per=1, start=0):
    return index(n, by) * per + per + start


def used(n, by=0, each=16):
    return moved(n, by)[0] * each + each


def walk(eng, step, groups):
    bodies = groups // RING
    for g in range(-2 * RING, 2 * RING):
        step((g // RING, g % RING))
    with eng.Fori(2, bodies - 2) as body:
        for slot in range(RING):
            step((body, slot))
    for g in range((bodies - 2) * RING, (bodies + 2) * RING):
        step((g // RING, g % RING))


class Kept:
    pass


def gnn(nc, x, src, dst, ea3, ea48, ea8, w1, b1, w2_0, w2_1, rows, w_msg, w_lin_t, w_upd, w_out, out):
    N, E = x.shape[0], src.shape[0]
    B = N // LOCAL
    C = E // P
    assert N == B * LOCAL and E == C * P and B <= 100
    units = E // (P * UNIT) + B
    G = -(-units // (GU * RING)) * RING
    K = max(k for k in range(1, P + 1) if G % k == 0)
    CH = G // K
    STEP, BATCH = 25, 5
    assert C % STEP == 0
    chunks = [min(500, C - c) for c in range(0, C, 500)]

    rec_d = nc.dram_tensor("rec_sorted", (G, GU, P, UNIT * REC), F32, kind="Internal").ap()
    cmp_d = nc.dram_tensor("cmp_sorted", (G, P, GROUP * CMP), F32, kind="Internal").ap()
    sum0_d = nc.dram_tensor("sums0", (G, P, GU * F0), F32, kind="Internal").ap()
    sum1_d = nc.dram_tensor("sums1", (G, P, GU * NS), F32, kind="Internal").ap()
    sum2_d = nc.dram_tensor("sums2", (G, P, GU * NS), F32, kind="Internal").ap()
    tab0_d = nc.dram_tensor("table0", (N, NS), F32, kind="Internal").ap()
    tab1_d = nc.dram_tensor("table1", (N, T0), F32, kind="Internal").ap()
    tab2_d = nc.dram_tensor("table2", (N, NS * 8), F32, kind="Internal").ap()

    whole = ExitStack()
    with whole:
        spent = []

        def alloc(scope):
            def semaphore(name, by_pool_dma=False):
                s = nc.alloc_semaphore(name)
                if not by_pool_dma:
                    spent.append(s)
                return s
            return lambda name, shape, dt: scope.enter_context(nc.sbuf_tensor(name, shape, dt)), semaphore

        def clear_spent():
            nc.clear_and_free_semaphores(list(spent))
            spent.clear()
            nc.all_engine_barrier()
        sb, sem = alloc(whole)
        ps = whole.enter_context(nc.psum_tensor("ps", [P, 8, 512], F32))

        x_sb = sb("x_sb", [B, LOCAL, NS], F32)
        h_sb = sb("h_sb", [B, LOCAL, NS], F32)
        rcount = sb("rcount", [B, LOCAL], F32)
        owner = sb("owner", [K, CH * GU, B], F32)
        ident = sb("ident", [P, P], F32)
        ident_b = sb("ident_b", [P, P], BF16)
        ones = sb("ones", [P, P], F32)
        rows_sb = sb("rows_sb", [B, rows.shape[1]], F32)
        iota_p = sb("iota_p", [P, P], F32)

        def layernorm_relu(dve, link, xin, hout, var, tmp, sq_ready, rt_ready, turn):
            bc = lambda a: a[:, :].unsqueeze(2).to_broadcast([B, LOCAL, NS])
            link(nc.vector.tensor_reduce(var[:, :], xin[:, :, :], AX.X, ALU.add))
            link(nc.vector.tensor_scalar(var[:, :], var[:, :], 1.0 / NS, None, ALU.mult))
            link(nc.vector.tensor_tensor(hout[:, :, :], xin[:, :, :], bc(var), ALU.subtract))
            link(nc.vector.tensor_tensor(tmp[:, :, 0:NS], hout[:, :, :], hout[:, :, :], ALU.mult))
            link(nc.vector.tensor_reduce(var[:, :], tmp[:, :, 0:NS], AX.X, ALU.add))
            nc.vector.tensor_scalar(var[:, :], var[:, :], 1.0 / NS, EPS, ALU.mult, ALU.add).then_inc(sq_ready, 1)
            dve.wait_ge(rt_ready, turn)
            link(nc.vector.reciprocal(var[:, :], var[:, :]))
            link(nc.vector.tensor_tensor(hout[:, :, :], hout[:, :, :], bc(var), ALU.mult))
            link(nc.vector.tensor_scalar(hout[:, :, :], hout[:, :, :], 0.0, None, ALU.max))

        sort = ExitStack()
        with sort:
            sbs, sems = alloc(sort)
            fill_out = sems("fill_out")
            loc = sbs("loc", [P, C], F32)
            rhat = sbs("rhat", [P, C, 3], F32)
            bucket = sbs("bucket", [P, C], BF16)
            base_hi = sbs("base_hi", [B, C], BF16)
            base_lo = sbs("base_lo", [B, C], FP16)
            iota_b = sbs("iota_b", [P, P], F32)
            fill = sbs("fill", [P, 8, REC], F32)

            fill_rows = G * GU * UNIT // 8
            fill_cuts = [(fill_rows * i // 8, fill_rows * (i + 1) // 8) for i in range(8)]

            prep = ExitStack()
            with prep:
                sbp, semp = alloc(prep)
                srci = sbp("srci", [P, C], I32)
                f0 = sbp("f0", [P, C], F32)
                f1 = sbp("f1", [P, C], F32)
                f2 = sbp("f2", [P, C], F32)
                lnv = sbp("lnv", [B, LOCAL], F32)
                lnt = sbp("lnt", [B, LOCAL, NS], F32)
                rows1 = sbp("rows1", [1, rows.shape[1]], F32)
                eq = sbp("eq", [P, 2, C], BF16)
                pick = sbp("pick", [P, 2 * P], BF16)
                zb = sbp("zb", [P, 512], BF16)
                tri = sbp("tri", [P, P], F32)
                tri_in = sbp("tri_in", [P, P], F32)
                nb = sbp("nb", [B, 4], F32)
                nbi = sbp("nbi", [B, 1], I32)
                unit_no = sbp("unit_no", [K, CH * GU], F32)
                span = sbp("span", [K, 2 * P], F32)
                src_in, x_in, v_in, rows_in = semp("src_in"), semp("x_in"), semp("v_in"), semp("rows_in")
                fill_ready, tab_out = semp("fill_ready"), semp("tab_out")
                const_ready, link_s, sq_ready, rt_ready = semp("const_ready"), semp("link_s"), semp("sq_ready"), semp("rt_ready")
                eq_ready, eq_used, counted = semp("eq_ready"), semp("eq_used"), semp("counted")
                pe_turn = semp("pe_turn")
                n_ready, starts_ready, rows_bc, h_ready = semp("n_ready"), semp("starts_ready"), semp("rows_bc"), semp("h_ready")
                pool_link = semp("pool_link")
                count_cols = [(c, min(448, C - c)) for c in range(0, C, 448)]

                block = prep.enter_context(nc.Block())

                @block.sync
                def _(sp):
                    sp.dma_start(srci[:, :], src.rearrange("(p c) -> p c", p=P)).then_inc(src_in, 16)
                    sp.dma_start(rhat[:, :, :], ea3.rearrange("(p c) f -> p c f", p=P)).then_inc(v_in, 16)
                    sp.dma_start(x_sb[:, :, :], x.rearrange("(b l) f -> b l f", l=LOCAL)).then_inc(x_in, 16)
                    sp.dma_start(rows1[:, :], rows).then_inc(rows_in, 16)
                    sp.wait_ge(fill_ready, 2)
                    rec_f = rec_d.rearrange("g u p x -> (g u p x)").rearrange("(p r x) -> p r x", p=P, x=8 * REC)
                    for a, b in fill_cuts:
                            sp.dma_start(rec_f[:, a:b, :], fill[:, :, :].rearrange("p a x -> p (a x)").unsqueeze(1)
                                         .to_broadcast([P, b - a, 8 * REC])).then_inc(fill_out, 16)
                    sp.wait_ge(h_ready, 1)
                    sp.dma_start(tab0_d.rearrange("(b l) f -> b l f", l=LOCAL), h_sb[:, :, :]).then_inc(tab_out, 16)
                    sp.wait_ge(tab_out, 16)

                @block.gpsimd
                def _(pool):
                    nc.gpsimd.memset(fill[:, :, :], 0.0).then_inc(fill_ready, 1)
                    pool.wait_ge(fill_ready, 1)
                    nc.gpsimd.memset(fill[:, :, SMALL + C_NLO:SMALL + C_NLO + 1], 1.0).then_inc(fill_ready, 1)
                    nc.gpsimd.iota(iota_p[:, :], pattern=[[1, P]], base=0, channel_multiplier=0,
                                   allow_small_or_imprecise_dtypes=True)
                    nc.gpsimd.iota(iota_b[:, :], pattern=[[1, P]], base=0, channel_multiplier=0,
                                   allow_small_or_imprecise_dtypes=True)
                    nc.gpsimd.iota(unit_no[:, :], pattern=[[GU * K, CH], [1, GU]], base=0, channel_multiplier=GU,
                                   allow_small_or_imprecise_dtypes=True)
                    nc.gpsimd.memset(ones[:, :], 1.0)
                    nc.gpsimd.memset(ident[:, :], 0.0)
                    nc.gpsimd.memset(zb[:, :], 0.0)
                    nc.gpsimd.memset(pick[:, :], 0.0).then_inc(pool_link, 1)
                    pool.wait_ge(pool_link, 1)
                    nc.gpsimd.memset(pick[:, P:P + 1], 1.0)
                    nc.gpsimd.affine_select(out=ident[:, :], in_=ident[:, :], compare_op=ALU.not_equal, fill=1.0,
                                            base=0, pattern=[[-1, P]], channel_multiplier=1)
                    nc.gpsimd.affine_select(out=tri[:, :], in_=ones[:, :], compare_op=ALU.is_gt, fill=0.0,
                                            base=0, pattern=[[1, P]], channel_multiplier=-1)
                    nc.gpsimd.affine_select(out=tri_in[:, :], in_=ones[:, :], compare_op=ALU.is_ge, fill=0.0,
                                            base=0, pattern=[[1, P]], channel_multiplier=-1).then_inc(const_ready, 1)

                @block.scalar
                def _(act):
                    act.wait_ge(sq_ready, 1)
                    nc.scalar.activation(lnv[:, :], lnv[:, :], ACT.Sqrt).then_inc(rt_ready, 1)
                    act.wait_ge(sq_ready, 2)
                    nc.scalar.activation(f1[:, :], f0[:, :], ACT.Sqrt).then_inc(rt_ready, 1)

                @block.tensor
                def _(pe):
                    pe.wait_ge(rows_in, 16)
                    pe.wait_ge(const_ready, 1)
                    nc.tensor.matmul(ps[0:B, 7, 0:rows.shape[1]], ones[0:1, 0:B], rows1[:, :], start=True,
                                     stop=True).then_inc(rows_bc, 1)
                    for j, (c, w) in enumerate(count_cols):
                        nc.tensor.matmul(ps[0:B, j, 0:w], zb[:, 0:B], zb[:, 0:w], start=True, stop=False)
                    with pe.Fori(0, B // 2) as i:
                        for s in range(2):
                            pe.wait_ge(eq_ready, 2 * i + s + 1)
                            pe.sem_inc(pe_turn, 1)
                            for j, (c, w) in enumerate(count_cols):
                                last = nc.tensor.matmul(ps[0:B, j, 0:w], pick[:, bass.ds(P - s - 2 * i, B)],
                                                        eq[:, s, c:c + w], start=False, stop=False)
                            last.then_inc(eq_used, 1)
                    for j, (c, w) in enumerate(count_cols):
                        last = nc.tensor.matmul(ps[0:B, j, 0:w], zb[:, 0:B], zb[:, 0:w], start=False, stop=True)
                    last.then_inc(counted, 1)
                    pe.wait_ge(n_ready, 1)
                    nc.tensor.matmul(ps[0:B, 7, 64:65], tri[0:B, 0:B], nb[:, 3:4], start=True, stop=True)
                    units_bc = nb[:, 3:4].to_broadcast([B, K])
                    nc.tensor.matmul(ps[0:K, 7, 128:128 + B], units_bc, tri[0:B, 0:B], start=True, stop=True)
                    nc.tensor.matmul(ps[0:K, 7, 256:256 + B], units_bc, tri_in[0:B, 0:B], start=True,
                                     stop=True).then_inc(starts_ready, 1)

                @block.vector
                def _(dve):
                    linked = [0]

                    def link(ins):
                        linked[0] += 1
                        ins.then_inc(link_s, 1)
                        dve.wait_ge(link_s, linked[0])

                    def floor_of(out, value, whole_i, more):
                        link(nc.vector.tensor_copy(whole_i, value))
                        link(nc.vector.tensor_copy(out, whole_i))
                        link(nc.vector.tensor_tensor(more, out, value, ALU.is_gt))
                        link(nc.vector.tensor_tensor(out, out, more, ALU.subtract))

                    dve.wait_ge(src_in, 16)
                    link(nc.vector.tensor_copy(f0[:, :], srci[:, :]))
                    link(nc.vector.tensor_scalar(f1[:, :], f0[:, :], 1.0 / LOCAL, None, ALU.mult))
                    floor_of(f2[:, :], f1[:, :], srci[:, :], loc[:, :])
                    link(nc.vector.scalar_tensor_tensor(out=loc[:, :], in0=f2[:, :], scalar=-float(LOCAL), in1=f0[:, :],
                                                        op0=ALU.mult, op1=ALU.add))
                    link(nc.vector.tensor_scalar(f1[:, :], loc[:, :], 0.0, None, ALU.is_lt))
                    link(nc.vector.tensor_scalar(f0[:, :], loc[:, :], float(LOCAL), None, ALU.is_ge))
                    link(nc.vector.tensor_tensor(f0[:, :], f0[:, :], f1[:, :], ALU.subtract))
                    link(nc.vector.tensor_tensor(bucket[:, :], f2[:, :], f0[:, :], ALU.add))
                    link(nc.vector.scalar_tensor_tensor(out=loc[:, :], in0=f0[:, :], scalar=-float(LOCAL), in1=loc[:, :],
                                                        op0=ALU.mult, op1=ALU.add))
                    dve.wait_ge(const_ready, 1)
                    nc.vector.tensor_copy(ident_b[:, :], ident[:, :])
                    dve.wait_ge(x_in, 16)
                    dve.wait_ge(rows_bc, 1)
                    nc.vector.tensor_copy(rows_sb[:, :], ps[0:B, 7, 0:rows.shape[1]])
                    layernorm_relu(dve, link, x_sb, h_sb, lnv, lnt, sq_ready, rt_ready, 1)
                    dve.engine_nop().then_inc(h_ready, 1)
                    dve.wait_ge(v_in, 16)
                    link(nc.vector.tensor_tensor(f0[:, :], rhat[:, :, 0], rhat[:, :, 0], ALU.mult))
                    for c in (1, 2):
                        link(nc.vector.tensor_tensor(f1[:, :], rhat[:, :, c], rhat[:, :, c], ALU.mult))
                        link(nc.vector.tensor_tensor(f0[:, :], f0[:, :], f1[:, :], ALU.add))
                    dve.engine_nop().then_inc(sq_ready, 1)
                    dve.wait_ge(const_ready, 1)
                    for s in range(2):
                        nc.vector.tensor_scalar(eq[:, s, :], bucket[:, :], iota_b[:, s:s + 1], None,
                                                ALU.is_equal).then_inc(eq_ready, 1)
                    with dve.Fori(1, B // 2) as i:
                        for s in range(2):
                            dve.wait_ge(eq_used, 2 * i + s - 1)
                            nc.vector.tensor_scalar(eq[:, s, :], bucket[:, :], iota_b[:, bass.ds(2 * i + s, 1)], None,
                                                    ALU.is_equal).then_inc(eq_ready, 1)
                    dve.wait_ge(rt_ready, 2)
                    link(nc.vector.tensor_scalar(f1[:, :], f1[:, :], 1e-12, None, ALU.add))
                    link(nc.vector.reciprocal(f0[:, :], f1[:, :]))
                    link(nc.vector.tensor_tensor(rhat[:, :, :], rhat[:, :, :], f0[:, :].unsqueeze(2)
                                                 .to_broadcast([P, C, 3]), ALU.mult))
                    dve.wait_ge(counted, 1)
                    for j, (c, w) in enumerate(count_cols):
                        last = nc.vector.tensor_copy(f0[0:B, c:c + w], ps[0:B, j, 0:w])
                    link(last)
                    link(nc.vector.tensor_tensor_scan(f1[0:B, :], ones[0:B, 0:1].to_broadcast([B, C]), f0[0:B, :], 0.0,
                                                      ALU.mult, ALU.add))
                    link(nc.vector.tensor_tensor(f1[0:B, :], f1[0:B, :], f0[0:B, :], ALU.subtract))
                    link(nc.vector.tensor_tensor(nb[:, 0:1], f1[0:B, C - 1:C], f0[0:B, C - 1:C], ALU.add))
                    link(nc.vector.tensor_scalar(nb[:, 1:2], nb[:, 0:1], float(UNIT * P - 1), 1.0 / (UNIT * P),
                                                 ALU.add, ALU.mult))
                    link(nc.vector.tensor_copy(nbi[:, :], nb[:, 1:2]))
                    link(nc.vector.tensor_copy(nb[:, 3:4], nbi[:, :]))
                    link(nc.vector.tensor_tensor(nb[:, 2:3], nb[:, 3:4], nb[:, 1:2], ALU.is_gt))
                    link(nc.vector.tensor_tensor(nb[:, 3:4], nb[:, 3:4], nb[:, 2:3], ALU.subtract))
                    dve.engine_nop().then_inc(n_ready, 1)
                    dve.wait_ge(starts_ready, 1)
                    link(nc.vector.tensor_scalar(nb[:, 0:1], ps[0:B, 7, 64:65], float(UNIT * P), None, ALU.mult))
                    link(nc.vector.tensor_copy(span[:, 0:B], ps[0:K, 7, 128:128 + B]))
                    link(nc.vector.tensor_copy(span[:, P:P + B], ps[0:K, 7, 256:256 + B]))
                    link(nc.vector.tensor_scalar(f1[0:B, :], f1[0:B, :], nb[:, 0:1], None, ALU.add))
                    link(nc.vector.tensor_scalar(f0[0:B, :], f1[0:B, :], 1.0 / 2048, None, ALU.mult))
                    link(nc.vector.tensor_copy(srci[0:B, :], f0[0:B, :]))
                    link(nc.vector.tensor_copy(f2[0:B, :], srci[0:B, :]))
                    link(nc.vector.tensor_tensor(f0[0:B, :], f2[0:B, :], f0[0:B, :], ALU.is_gt))
                    link(nc.vector.tensor_tensor(f2[0:B, :], f2[0:B, :], f0[0:B, :], ALU.subtract))
                    link(nc.vector.tensor_scalar(base_hi[:, :], f2[0:B, :], 2048.0, None, ALU.mult))
                    link(nc.vector.scalar_tensor_tensor(out=base_lo[:, :], in0=f2[0:B, :], scalar=-2048.0,
                                                        in1=f1[0:B, :], op0=ALU.mult, op1=ALU.add))
                    for q in range(CH * GU):
                        link(nc.vector.tensor_scalar(owner[:, q, :], span[:, 0:B], unit_no[:, q:q + 1], None, ALU.is_le))
                        link(nc.vector.scalar_tensor_tensor(out=owner[:, q, :], in0=span[:, P:P + B],
                                                            scalar=unit_no[:, q:q + 1], in1=owner[:, q, :],
                                                            op0=ALU.is_gt, op1=ALU.mult))

            place = ExitStack()
            with place:
                sbp, semp = alloc(place)
                spread = sbp("spread", [B, B, P], BF16)
                tri_b = sbp("tri_b", [P, P], BF16)
                ones_b = sbp("ones_b", [P, P], BF16)
                eq = sbp("eq2", [P, 4, 512], BF16)
                pos = sbp("pos", [P, C], F32)
                rec = sbp("rec", [P, 2, STEP, REC], F32)
                in48 = sbp("in48", [P, 2, STEP, HID], F32)
                in8 = sbp("in8", [P, 2, STEP, 8], F32)
                ind = sbp("ind", [P, 2, STEP], I32)
                to = sbp("to", [P, 2, STEP], U32)
                w1s = sbp("w1s", [HID + 1, 2, HID], F32)
                attr_t = sbp("attr_t", [HID + 1, 2, BATCH * P], F32)
                rest = sbp("rest", [P, 2, 2, BATCH, HID], F32)
                consts, eq_ready, table_ready, copied = semp("consts2"), semp("eq_ready2"), semp("table_ready"), semp("copied")
                plink, w1_in, attr_one = semp("plink2"), semp("w1_in"), semp("attr_one")
                in_sem = [semp(f"edges_in{s}") for s in range(2)]
                rec_ready = semp("rec_ready")
                attr_on_pe, attr_ready, hid_on_pe = semp("attr_on_pe"), semp("attr_ready"), semp("hid_on_pe")
                h1_ready, rest_ready, h2_ready, h3_ready = semp("h1_ready"), semp("rest_ready"), semp("h2_ready"), semp("h3_ready")
                scattered = [semp(f"scattered{s}", True) for s in range(2)]
                pool_turn, dve_turn, pe_turn = semp("pool_turn"), semp("dve_turn"), semp("pe_turn2")
                steps = C // STEP
                per = STEP // BATCH
                block = place.enter_context(nc.Block())

                ea48_v = ea48.rearrange("(p c) f -> p c f", p=P)
                ea8_v = ea8.rearrange("(p c) f -> p c f", p=P)
                dst_v = dst.rearrange("(p c) -> p c", p=P)

                def parts(s, k, layer, part):
                    at = PART0[layer] + part * HID
                    return rec[:, s, k * BATCH:(k + 1) * BATCH, :].bitcast(BF16)[:, :, at:at + HID]

                def first(pair, s, k=0):
                    return isinstance(pair, int) and pair == 0 and s == 0 and k < 2

                def attr_ps(half):
                    return ps[0:HID, 2 * half:2 * half + 2, :].rearrange("k b e -> k (b e)")[:, 0:BATCH * P]

                def hid_ps(half, layer):
                    return ps[:, 4 + half, 0:BATCH * 2 * HID].rearrange("p (t l f) -> p t l f", l=2, f=HID)[:, :, layer, :]

                def edge_steps(eng, step):
                    pairs = steps // 2
                    for s in range(2):
                        step(0, s)
                    if pairs > 1:
                        with eng.Fori(1, pairs) as pair:
                            for s in range(2):
                                step(pair, s)
                    if steps % 2:
                        step(pairs, 0)

                @block.sync
                def _(sp):
                    sp.wait_ge(attr_one, 1)
                    for layer in range(2):
                        sp.dma_start(w1s[0:HID, layer, :], w1[layer]).then_inc(w1_in, 16)
                        sp.dma_start(w1s[HID:HID + 1, layer, :], b1[layer]).then_inc(w1_in, 16)

                    def step(pair, s):
                        st = 2 * pair + s
                        if not (isinstance(pair, int) and pair == 0):
                            sp.wait_ge(attr_ready, (st - 1) * per)
                        cols = bass.ds(st * STEP, STEP)
                        sp.dma_start(in48[:, s], ea48_v[:, cols, :]).then_inc(in_sem[s], 16)
                        sp.dma_start(in8[:, s], ea8_v[:, cols, :]).then_inc(in_sem[s], 16)
                        sp.dma_start(ind[:, s], dst_v[:, cols]).then_inc(in_sem[s], 16)
                    edge_steps(sp, step)

                @block.scalar
                def _(act):
                    act.wait_ge(copied, B * len(chunks))

                    def step(pair, s):
                        st = 2 * pair + s
                        act.wait_ge(in_sem[s], 48 * (pair + 1))
                        if not (isinstance(pair, int) and pair == 0):
                            act.wait_ge(scattered[s], 16 * STEP * pair)
                        cols = bass.ds(st * STEP, STEP)
                        small = rec[:, s, :, SMALL:SMALL + CMP]
                        nc.scalar.activation(small[:, :, C_EA8:C_EA8 + 8], in8[:, s], ACT.Copy)
                        nc.scalar.activation(small[:, :, C_RHAT:C_RHAT + 3], rhat[:, cols, :], ACT.Copy)
                        nc.scalar.activation(small[:, :, C_NLO], loc[:, cols], ACT.Copy, scale=-1.0)
                        nc.scalar.activation(small[:, :, C_DST], ind[:, s], ACT.Copy)
                        nc.scalar.activation(to[:, s], pos[:, cols], ACT.Copy).then_inc(rec_ready, 1)
                        for k in range(per):
                            m, half = st * per + k, (s + k) % 2
                            act.wait_ge(attr_on_pe, m + 1)
                            if not first(pair, s, k):
                                act.wait_ge(hid_on_pe, m - 1)
                            nc.scalar.activation(attr_t[0:HID, half, :], attr_ps(half), ACT.Copy)\
                              .then_inc(attr_ready, 1)
                            act.wait_ge(hid_on_pe, m + 1)
                            for layer in range(2):
                                last = nc.scalar.activation(parts(s, k, layer, 1), hid_ps(half, layer), ACT.Relu)
                            last.then_inc(h1_ready, 1)
                    edge_steps(act, step)

                @block.gpsimd
                def _(pool):
                    nc.gpsimd.memset(ones_b[:, :], 1.0).then_inc(plink, 1)
                    pool.wait_ge(plink, 1)
                    nc.gpsimd.affine_select(out=tri_b[:, :], in_=ones_b[:, :], compare_op=ALU.is_gt, fill=0.0,
                                            base=0, pattern=[[1, P]], channel_multiplier=-1)
                    nc.gpsimd.affine_select(out=spread[:, :, :], in_=ones_b[0:B, 0:1].unsqueeze(2).to_broadcast([B, B, P]),
                                            compare_op=ALU.is_equal, fill=0.0, base=0, pattern=[[1, B], [0, P]],
                                            channel_multiplier=-1).then_inc(consts, 1)
                    rec_rows = rec_d.rearrange("g u p (j f) -> (g u p j) f", f=REC)

                    pool.wait_ge(fill_out, 16 * len(fill_cuts))

                    def step(pair, s):
                        pool.wait_ge(rec_ready, 2 * pair + s + 1)
                        pool.wait_ge(h3_ready, (2 * pair + s + 1) * per)
                        pool.sem_inc(pool_turn, 1)
                        for k in range(STEP):
                            nc.gpsimd.indirect_dma_start(
                                out=rec_rows, out_offset=bass.IndirectOffsetOnAxis(ap=to[:, s, k:k + 1], axis=0),
                                in_=rec[:, s, k, :], in_offset=None).then_inc(scattered[s], 16)
                    edge_steps(pool, step)
                    pool.wait_ge(scattered[0], 16 * STEP * ((steps + 1) // 2))
                    pool.wait_ge(scattered[1], 16 * STEP * (steps // 2))
                    pool.sem_inc(pool_turn, 1)

                @block.tensor
                def _(pe):
                    pe.wait_ge(consts, 1)
                    c = 0
                    for n, w in enumerate(chunks):
                        with pe.Fori(0, B // 2) as i:
                            for s in range(2):
                                b = 2 * i + s
                                pe.wait_ge(eq_ready, b + 1 + n * (B + 1))
                                pe.sem_inc(pe_turn, 1)
                                nc.tensor.matmul(ps[:, s, 0:w], tri_b[:, :], eq[:, s, 0:w], start=True, stop=False)
                                sel = spread[:, bass.ds(b, 1), :].rearrange("k o p -> k (o p)")
                                nc.tensor.matmul(ps[:, s, 0:w], sel, base_hi[:, c:c + w], start=False, stop=False)
                                nc.tensor.matmul(ps[:, s, 0:w], sel, base_lo[:, c:c + w], start=False,
                                                 stop=True).then_inc(table_ready, 1)
                        c += w
                    pe.wait_ge(w1_in, 64)
                    pe.wait_ge(copied, B * len(chunks))

                    def step(pair, s):
                        for k in range(per):
                            m, half = (2 * pair + s) * per + k, (s + k) % 2
                            if k == 0:
                                pe.wait_ge(in_sem[s], 48 * (pair + 1))
                            if not first(pair, s, k):
                                pe.wait_ge(attr_ready, m - 1)
                            pe.sem_inc(pe_turn, 1)
                            for t in range(BATCH):
                                last = nc.tensor.transpose(attr_ps(half)[:, t * P:(t + 1) * P],
                                                           in48[:, s, k * BATCH + t, :], ident[:, :])
                            last.then_inc(attr_on_pe, 1)
                            pe.wait_ge(attr_ready, m + 1)
                            if not first(pair, s, k):
                                pe.wait_ge(rest_ready, m - 1)
                            for t in range(BATCH):
                                last = nc.tensor.matmul(ps[:, 4 + half, t * 2 * HID:(t + 1) * 2 * HID],
                                                        attr_t[:, half, t * P:(t + 1) * P],
                                                        w1s[:, :, :].rearrange("k l f -> k (l f)"), start=True, stop=True)
                            last.then_inc(hid_on_pe, 1)
                    edge_steps(pe, step)

                @block.vector
                def _(dve):
                    nc.vector.memset(attr_t[:, :, :], 1.0).then_inc(attr_one, 1)
                    c = 0
                    for n, w in enumerate(chunks):
                        cols = slice(c, c + w)
                        cmp = lambda b, s: nc.vector.tensor_scalar(
                            eq[:, s, 0:w], bucket[:, cols], iota_b[:, bass.ds(b, 1)], None, ALU.is_equal)
                        if n:
                            dve.wait_ge(copied, n * B)
                        cmp(0, 0).then_inc(eq_ready, 1)
                        with dve.Fori(0, B // 2) as i:
                            for s in range(2):
                                b = 2 * i + s
                                dve.wait_ge(copied, b + n * B)
                                cmp(b + 1, 1 - s).then_inc(eq_ready, 1)
                                dve.wait_ge(table_ready, b + 1 + n * B)
                                dve.sem_inc(dve_turn, 1)
                                nc.vector.copy_predicated(pos[:, cols], eq[:, s, 0:w].bitcast(U16),
                                                          ps[:, s, 0:w]).then_inc(copied, 1)
                        c += w

                    def step(pair, s):
                        for k in range(per):
                            m, half = (2 * pair + s) * per + k, (s + k) % 2
                            dve.wait_ge(h1_ready, m + 1)
                            for layer in range(2):
                                last = nc.vector.scalar_tensor_tensor(
                                    out=rest[:, half, layer], in0=hid_ps(half, layer), scalar=0.0,
                                    in1=parts(s, k, layer, 1), op0=ALU.max, op1=ALU.subtract)
                            last.then_inc(rest_ready, 1)
                            dve.wait_ge(rest_ready, m + 1)
                            for layer in range(2):
                                last = nc.vector.tensor_copy(parts(s, k, layer, 0), rest[:, half, layer])
                            last.then_inc(h2_ready, 1)
                            dve.wait_ge(h2_ready, m + 1)
                            for layer in range(2):
                                last = nc.vector.tensor_tensor(parts(s, k, layer, 2), rest[:, half, layer],
                                                               parts(s, k, layer, 0), ALU.subtract)
                            last.then_inc(h3_ready, 1)
                    edge_steps(dve, step)
        clear_spent()
        sh = Kept()
        sh.N, sh.B, sh.G, sh.K, sh.CH, sh.alloc, sh.ps, sh.owner = N, B, G, K, CH, alloc, ps, owner
        sh.ones, sh.ident, sh.iota_p, sh.rcount, sh.rows_sb = ones, ident, iota_p, rcount, rows_sb
        sh.x_sb, sh.h_sb, sh.layernorm_relu, sh.rec_d, sh.cmp_d = x_sb, h_sb, layernorm_relu, rec_d, cmp_d
        sh.ident_b = ident_b
        conv_pass(nc, sh, 0, w2_0, tab0_d, sum0_d)
        nodes_0(nc, sh, sum0_d, tab1_d)
        clear_spent()
        conv_pass(nc, sh, 1, w2_1, tab1_d, sum1_d)
        clear_spent()
        nodes_1(nc, sh, sum1_d, w_msg, tab2_d)
        pass_2(nc, sh, tab2_d, sum2_d)
        nodes_2(nc, sh, sum2_d, w_lin_t, w_upd, w_out, out)


def reduce_units(nc, sh, sum_d, F, tot, tag, sbp, semp):
    K, CH, B, ps = sh.K, sh.CH, sh.B, sh.ps
    lc = 1 << ((512 // F).bit_length() - 1)
    banks = P // lc
    part = sbp(f"part{tag}", [K, 2, P, GU, F], F32)
    part_in = [semp(f"part_in{tag}{s}") for s in range(2)]
    part_used, tot_ready = semp(f"part_used{tag}"), semp(f"tot_ready{tag}")

    def sync(sp):
        for c in range(CH):
            if c >= 2:
                sp.wait_ge(part_used, c - 1)
            sp.dma_start(part[:, c % 2].rearrange("k l u f -> k (l u f)"),
                         sum_d[c * K:(c + 1) * K].rearrange("k l x -> k (l x)"), max_dma_last_dim=16384)\
              .then_inc(part_in[c % 2], 16)

    def tensor(pe):
        for c in range(CH):
            pe.wait_ge(part_in[c % 2], 16 * (c // 2 + 1))
            for u in range(GU):
                for j in range(banks):
                    last = nc.tensor.matmul(ps[0:B, j, 0:lc * F], sh.owner[:, c * GU + u, :],
                                            part[:, c % 2, j * lc:(j + 1) * lc, u, :],
                                            start=(c == 0 and u == 0), stop=(c == CH - 1 and u == GU - 1))
            last.then_inc(part_used, 1)
        pe.wait_ge(tot_ready, 1)

    def scalar(act):
        act.wait_ge(part_used, CH)
        for j in range(banks):
            last = nc.scalar.activation(tot[:, j * lc:(j + 1) * lc, :], ps[0:B, j, 0:lc * F]
                                        .rearrange("b (l f) -> b l f", f=F), ACT.Copy)
        last.then_inc(tot_ready, 1)
    return sync, tensor, scalar, tot_ready


class Linker:

    def __init__(self, dve, sem):
        self.dve, self.sem, self.n = dve, sem, 0

    def __call__(self, ins):
        self.n += 1
        ins.then_inc(self.sem, 1)
        self.dve.wait_ge(self.sem, self.n)


def nodes_0(nc, sh, sum_d, tab_d):
    B, N, ps, ones, rows = sh.B, sh.N, sh.ps, sh.ones, sh.rows_sb
    L = LOCAL
    scope = ExitStack()
    with scope:
        sbp, semp = sh.alloc(scope)
        tot = sbp("tot0", [B, P, F0], F32)
        val = sbp("val0", [B, L, T0], F32)
        sq = sbp("sq0", [B, L, T0], F32)
        m = sbp("m0", [B, 8, NS], F32)
        sync, tensor, scalar, tot_ready = reduce_units(nc, sh, sum_d, F0, tot, 0, sbp, semp)
        link_s, asked, answered = semp("nlink0"), semp("asked0"), semp("answered0")
        root_asked, root_ready, val_ready, tab_out = semp("root_asked0"), semp("root_ready0"), semp("val_ready0"), semp("tab_out0")
        block = scope.enter_context(nc.Block())

        @block.sync
        def _(sp):
            sync(sp)
            sp.wait_ge(val_ready, 1)
            sp.dma_start(tab_d.rearrange("(b l) f -> b l f", l=L), val[:, :, :]).then_inc(tab_out, 16)
            sp.wait_ge(tab_out, 16)

        @block.tensor
        def _(pe):
            tensor(pe)
            for k, row in enumerate((0, 1, 2)):
                pe.wait_ge(asked, k + 1)
                nc.tensor.matmul(ps[0:B, 0, k * NS:(k + 1) * NS], ones[0:B, 0:B], m[:, row, :], start=True,
                                 stop=True).then_inc(answered, 1)

        @block.scalar
        def _(act):
            scalar(act)
            for k in range(2):
                act.wait_ge(root_asked, k + 1)
                nc.scalar.activation(m[:, 4 + k, :], m[:, 4 + k, :], ACT.Sqrt).then_inc(root_ready, 1)

        @block.vector
        def _(dve):
            link = Linker(dve, link_s)
            over_l = lambda a: a.rearrange("b l f -> b f l")
            bc = lambda row, w=NS: m[:, row, 0:w].unsqueeze(1).to_broadcast([B, L, w])
            dve.wait_ge(tot_ready, 1)
            link(nc.vector.tensor_scalar(sh.rcount[:, :], tot[:, 0:L, F0 - 1], 1.0, None, ALU.max))
            link(nc.vector.reciprocal(sh.rcount[:, :], sh.rcount[:, :]))
            link(nc.vector.tensor_tensor(val[:, :, :], tot[:, 0:L, 0:T0],
                                         sh.rcount[:, :].unsqueeze(2).to_broadcast([B, L, T0]), ALU.mult))
            link(nc.vector.tensor_scalar(val[:, :, 0:NS], val[:, :, 0:NS], float(NS) ** -0.5, None, ALU.mult))
            link(nc.vector.tensor_scalar(val[:, :, NS:T0], val[:, :, NS:T0], (3.0 / NS) ** 0.5, None, ALU.mult))
            link(nc.vector.tensor_reduce(m[:, 0, :], over_l(val[:, :, 0:NS]), AX.X, ALU.add))
            dve.engine_nop().then_inc(asked, 1)
            link(nc.vector.tensor_tensor(sq[:, :, NS:T0], val[:, :, NS:T0], val[:, :, NS:T0], ALU.mult))
            link(nc.vector.memset(m[:, 2, :], 0.0))
            link(nc.vector.tensor_reduce(m[:, 7, 0:12], over_l(sq[:, :, NS:T0]), AX.X, ALU.add))
            link(nc.vector.tensor_reduce(m[:, 2, 0:NV], m[:, 7, 0:12].rearrange("b (j c) -> b j c", c=3), AX.X, ALU.add))
            dve.wait_ge(answered, 1)
            link(nc.vector.tensor_scalar(m[:, 3, :], ps[0:B, 0, 0:NS], 1.0 / N, None, ALU.mult))
            link(nc.vector.tensor_tensor(val[:, :, 0:NS], val[:, :, 0:NS], bc(3), ALU.subtract))
            link(nc.vector.tensor_tensor(sq[:, :, 0:NS], val[:, :, 0:NS], val[:, :, 0:NS], ALU.mult))
            link(nc.vector.tensor_reduce(m[:, 1, :], over_l(sq[:, :, 0:NS]), AX.X, ALU.add))
            dve.engine_nop().then_inc(asked, 2)
            dve.wait_ge(answered, 3)
            link(nc.vector.tensor_scalar(m[:, 4, :], ps[0:B, 0, NS:2 * NS], 1.0 / N, EPS, ALU.mult, ALU.add))
            link(nc.vector.tensor_scalar(m[:, 5, :], ps[0:B, 0, 2 * NS:3 * NS], 1.0 / (3 * N), EPS, ALU.mult, ALU.add))
            dve.engine_nop().then_inc(root_asked, 2)
            dve.wait_ge(root_ready, 2)
            link(nc.vector.reciprocal(m[:, 4:6, :], m[:, 4:6, :]))
            link(nc.vector.tensor_tensor(m[:, 4, :], m[:, 4, :], rows[:, 0:NS], ALU.mult))
            link(nc.vector.tensor_tensor(m[:, 5, 0:NV], m[:, 5, 0:NV], rows[:, 2 * NS:2 * NS + NV], ALU.mult))
            link(nc.vector.tensor_copy(m[:, 6, 0:12].rearrange("b (j c) -> b j c", c=3),
                                       m[:, 5, 0:NV].unsqueeze(2).to_broadcast([B, NV, 3])))
            link(nc.vector.tensor_tensor(val[:, :, 0:NS], val[:, :, 0:NS], bc(4), ALU.mult))
            link(nc.vector.tensor_tensor(val[:, :, 0:NS], val[:, :, 0:NS],
                                         rows[:, NS:2 * NS].unsqueeze(1).to_broadcast([B, L, NS]), ALU.add))
            link(nc.vector.tensor_tensor(val[:, :, NS:T0], val[:, :, NS:T0], bc(6, 12), ALU.mult))
            dve.engine_nop().then_inc(val_ready, 1)


def conv_pass(nc, sh, layer, w2, tab_d, sum_d):
    G, ps, iota_p = sh.G, sh.ps, sh.iota_p
    width = NS if layer == 0 else T0
    I, J = (NS, 20) if layer == 0 else (20, NS)
    F = F0 if layer == 0 else NS
    M = 4 + F0 if layer == 0 else NS
    scope = ExitStack()
    with scope:
        sbp, semp = sh.alloc(scope)
        tag = f"_c{layer}"
        recs = sbp("recs" + tag, [P, RING, GU, UNIT * REC], F32)
        comp = sbp("comp" + tag, [P, RING, GROUP, CMP], F32)
        at = sbp("at" + tag, [P, RING, GROUP], I32)
        xs = sbp("xs" + tag, [P, RING, GROUP, width], F32)
        hid = sbp("hid" + tag, [2 * HID + 1, 2, GROUP, 2, P], BF16)
        w32 = sbp("w32" + tag, [2 * HID + 1, 320], F32)
        w_rest = sbp("w_rest" + tag, [2 * HID + 1, 2, 320], F32)
        w_part = sbp("w_part" + tag, [2 * HID + 1, 3, 320], BF16)
        prod = sbp("prod" + tag, [P, 2, 2, J, I], F32)
        vr = sbp("vr" + tag, [P, GROUP, NV, 3], F32)
        msg = sbp("msg" + tag, [P, 2, GROUP, M], F32)
        away = sbp("away" + tag, [P, 2, GROUP, P], F32)
        owns = sbp("owns" + tag, [P, 2, GROUP, P], F32)
        sums = sbp("sums" + tag, [P, RING, GU, F], F32)
        rec_in = [semp(f"rec_in{k}{tag}") for k in range(RING)]
        xs_in = [semp(f"xs_in{k}{tag}", True) for k in range(RING)]
        comp_out = [semp(f"comp_out{k}{tag}") for k in range(RING)]
        sums_out = [semp(f"sums_out{k}{tag}") for k in range(RING)]
        w_in, w_link, w_ready, ones_set = semp("w_in" + tag), semp("w_link" + tag), semp("w_ready" + tag), semp("ones_set" + tag)
        hid_on_pe, hid_ready = semp("hid_on_pe" + tag), semp("hid_ready" + tag)
        comp_ready, at_ready = semp("comp_ready" + tag), semp("at_ready" + tag)
        weights_ready, prod_ready, reduced = semp("weights_ready" + tag), semp("prod_ready" + tag), semp("reduced" + tag)
        away_ready, owns_ready, msg_ready = semp("away_ready" + tag), semp("owns_ready" + tag), semp("msg_ready" + tag)
        summed, sums_ready, vr_ready, xs_ready = semp("summed" + tag), semp("sums_ready" + tag), semp("vr_ready" + tag), semp("xs_ready" + tag)
        pool_turn, pe_turn = semp("pool_turn" + tag), semp("pe_turn" + tag)
        block = scope.enter_context(nc.Block())

        @block.sync
        def _(sp):
            sp.dma_start(w32[0:HID, :], w2[0:HID, :]).then_inc(w_in, 16)
            sp.dma_start(w32[HID:2 * HID + 1, :], w2).then_inc(w_in, 16)
            sp.wait_ge(w_link, 5)
            sp.dma_start(w_part[HID:2 * HID, 2, :], w_part[HID:2 * HID, 0, :]).then_inc(w_ready, 16)

            def step(n):
                if exists(n, 5, G):
                    slot = moved(n, 5)[1]
                    if exists(n, 1, G):
                        sp.wait_ge(hid_on_pe, count(n, 1))
                        sp.wait_ge(at_ready, count(n, 1))
                    sp.dma_start(recs[:, slot], sh.rec_d[bass.ds(index(n, 5), 1)].rearrange("o u p x -> p (o u) x"))\
                      .then_inc(rec_in[slot], 16)
                if layer == 0 and exists(n, 2, G):
                    slot = moved(n, 2)[1]
                    sp.wait_ge(comp_ready, count(n, 2))
                    sp.dma_start(sh.cmp_d[bass.ds(index(n, 2), 1)].rearrange("o p x -> p (o x)"),
                                 comp[:, slot].rearrange("p t f -> p (t f)")).then_inc(comp_out[slot], 16)
                if exists(n, -3, G):
                    slot = moved(n, -3)[1]
                    sp.wait_ge(sums_ready, count(n, -3))
                    sp.dma_start(sum_d[bass.ds(index(n, -3), 1)].rearrange("o p x -> p (o x)"),
                                 sums[:, slot].rearrange("p u f -> p (u f)")).then_inc(sums_out[slot], 16)
            walk(sp, step, G)
            for k in range(RING):
                if layer == 0:
                    sp.wait_ge(comp_out[k], 16 * (G // RING))
                sp.wait_ge(sums_out[k], 16 * (G // RING))

        @block.gpsimd
        def _(pool):
            def step(n):
                if exists(n, 3, G):
                    slot = moved(n, 3)[1]
                    pool.wait_ge(at_ready, count(n, 3))
                    if exists(n, -1, G):
                        pool.wait_ge(prod_ready, count(n, -1, 2))
                    pool.sem_inc(pool_turn, 1)
                    for t in range(GROUP):
                        nc.gpsimd.indirect_dma_start(
                            out=xs[:, slot, t, :], out_offset=None, in_=tab_d,
                            in_offset=bass.IndirectOffsetOnAxis(ap=at[:, slot, t:t + 1], axis=0))\
                          .then_inc(xs_in[slot], 16)
            walk(pool, step, G)

        @block.scalar
        def _(act):
            act.wait_ge(ones_set, 1)

            def step(n):
                if exists(n, 3, G):
                    slot = moved(n, 3)[1]
                    act.wait_ge(rec_in[slot], used(n, 3))
                    if exists(n, -1, G):
                        act.wait_ge(msg_ready, count(n, -1))
                        if layer == 0:
                            act.wait_ge(comp_out[slot], used(n, -1))
                    fields = recs[:, slot].rearrange("p u (j f) -> p (u j) f", f=REC)
                    nc.scalar.activation(comp[:, slot], fields[:, :, SMALL:SMALL + CMP], ACT.Copy).then_inc(comp_ready, 1)
                    if exists(n, -1, G):
                        act.wait_ge(xs_in[slot], used(n, -1, 16 * GROUP))
                    nc.scalar.activation(at[:, slot], fields[:, :, SMALL + C_DST], ACT.Copy).then_inc(at_ready, 1)
                if exists(n, 1, G):
                    half = (n[1] + 1) % 2
                    act.wait_ge(hid_on_pe, count(n, 1))
                    if exists(n, -1, G):
                        act.wait_ge(weights_ready, count(n, -1, 2))
                    nc.scalar.activation(hid[0:2 * HID, half].rearrange("k t w e -> k (t w e)"),
                                         ps[0:2 * HID, half, :].bitcast(BF16), ACT.Copy).then_inc(hid_ready, 1)
                if exists(n, 0, G):
                    half = n[1] % 2
                    act.wait_ge(comp_ready, count(n))
                    for t in range(GROUP):
                        last = nc.scalar.activation(away[:, half, t, :], iota_p[:, :], ACT.Square,
                                                    bias=comp[:, n[1], t, C_NLO:C_NLO + 1])
                    last.then_inc(away_ready, 1)
                if exists(n, -2, G):
                    slot = moved(n, -2)[1]
                    act.wait_ge(summed, count(n, -2))
                    if exists(n, -6, G):
                        act.wait_ge(sums_out[slot], used(n, -6))
                    nc.scalar.activation(sums[:, slot], ps[:, 6 + slot % 2, 0:GU * F]
                                         .rearrange("p (u f) -> p u f", f=F), ACT.Copy).then_inc(sums_ready, 1)
                if exists(n, 0, G):
                    half = n[1] % 2
                    act.wait_ge(away_ready, count(n))
                    nc.scalar.activation(owns[:, half], away[:, half], ACT.Relu, bias=1.0, scale=-1.0)\
                      .then_inc(owns_ready, 1)
            walk(act, step, G)

        @block.tensor
        def _(pe):
            pe.wait_ge(w_link, 5)
            pe.wait_ge(w_ready, 16)

            def step(n):
                if exists(n, 1, G):
                    slot, half = moved(n, 1)[1], (n[1] + 1) % 2
                    pe.wait_ge(rec_in[slot], used(n, 1))
                    if exists(n, -1, G):
                        pe.wait_ge(hid_ready, count(n, -1))
                    pe.sem_inc(pe_turn, 1)
                    for t in range(GROUP):
                        u, j = t // UNIT, t % UNIT
                        start = j * 2 * REC + PART0[layer]
                        for w in range(2):
                            last = nc.tensor.transpose(
                                ps[0:2 * HID, half, :].bitcast(BF16)[:, (2 * t + w) * P:(2 * t + w + 1) * P],
                                recs[:, slot, u, :].bitcast(BF16)[:, start + w * HID:start + (w + 2) * HID],
                                sh.ident_b[:, :])
                    last.then_inc(hid_on_pe, 1)
                if exists(n, 0, G):
                    pe.wait_ge(hid_ready, count(n))
                    for q in range(2):
                        if exists(n, -1, G):
                            pe.wait_ge(prod_ready, count(n, -1, 2) - 1 + q)
                        for t in (2 * q, 2 * q + 1):
                            for part in range(3):
                                last = nc.tensor.matmul(ps[:, 2 + t, 0:320], hid[:, n[1] % 2, t, part // 2, :],
                                                        w_part[:, part, :], start=(part == 0), stop=(part == 2))
                        last.then_inc(weights_ready, 1)
                if exists(n, -1, G):
                    half = (n[1] + 1) % 2
                    pe.wait_ge(msg_ready, count(n, -1))
                    pe.wait_ge(owns_ready, count(n, -1))
                    if exists(n, -3, G):
                        pe.wait_ge(sums_ready, count(n, -3))
                    for u in range(GU):
                        for j in range(UNIT):
                            t = u * UNIT + j
                            last = nc.tensor.matmul(ps[:, 6 + half, u * F:(u + 1) * F], owns[:, half, t, :],
                                                    msg[:, half, t, M - F:], start=(j == 0), stop=(j == UNIT - 1))
                    last.then_inc(summed, 1)
            walk(pe, step, G)

        @block.vector
        def _(dve):
            nc.vector.memset(hid[:, :, :, :, :], 1.0)
            nc.vector.memset(msg[:, :, :, :], 1.0).then_inc(ones_set, 1)
            link = Linker(dve, w_link)
            dve.wait_ge(w_in, 32)
            link(nc.vector.tensor_copy(w_part[:, 0, :], w32[:, :]))
            link(nc.vector.tensor_tensor(w_rest[:, 0, :], w32[:, :], w_part[:, 0, :], ALU.subtract))
            link(nc.vector.tensor_copy(w_part[:, 1, :], w_rest[:, 0, :]))
            link(nc.vector.tensor_tensor(w_rest[:, 1, :], w_rest[:, 0, :], w_part[:, 1, :], ALU.subtract))
            link(nc.vector.tensor_copy(w_part[:, 2, :], w_rest[:, 1, :]))

            def step(n):
                if not exists(n, 0, G):
                    return
                slot, half = n[1], n[1] % 2
                direction = comp[:, slot, :, C_RHAT:C_RHAT + 3].unsqueeze(2).to_broadcast([P, GROUP, NV, 3])
                dve.wait_ge(xs_in[slot], used(n, 0, 16 * GROUP))
                if layer == 1:
                    dve.wait_ge(comp_ready, count(n))
                    nc.vector.tensor_tensor(vr[:, :, :, :], xs[:, slot, :, NS:T0].rearrange("p t (i c) -> p t i c", c=3),
                                            direction, ALU.mult).then_inc(vr_ready, 1)
                    dve.wait_ge(vr_ready, count(n))
                    nc.vector.tensor_reduce(xs[:, slot, :, NS:NS + NV], vr[:, :, :, :], AX.X, ALU.add)\
                      .then_inc(xs_ready, 1)
                    dve.wait_ge(xs_ready, count(n))
                for q in range(2):
                    dve.wait_ge(weights_ready, count(n, 0, 2) - 1 + q)
                    nc.vector.tensor_tensor(
                        prod[:, q], ps[:, 2 + 2 * q:4 + 2 * q, 0:320].rearrange("p t (j i) -> p t j i", i=I),
                        xs[:, slot, 2 * q:2 * q + 2, 0:I].unsqueeze(2).to_broadcast([P, 2, J, I]),
                        ALU.mult).then_inc(prod_ready, 1)
                if exists(n, -2, G):
                    dve.wait_ge(summed, count(n, -2))
                for q in range(2):
                    dve.wait_ge(prod_ready, count(n, 0, 2) - 1 + q)
                    last = nc.vector.tensor_reduce(msg[:, half, 2 * q:2 * q + 2, 0:J], prod[:, q], AX.X, ALU.add)
                if layer == 1:
                    last.then_inc(msg_ready, 1)
                    return
                last.then_inc(reduced, 1)
                dve.wait_ge(reduced, count(n))
                dve.wait_ge(comp_ready, count(n))
                nc.vector.tensor_tensor(
                    msg[:, half, :, 20:32].rearrange("p t (j c) -> p t j c", c=3),
                    msg[:, half, :, 0:NV].unsqueeze(3).to_broadcast([P, GROUP, NV, 3]), direction,
                    ALU.mult).then_inc(msg_ready, 1)
            walk(dve, step, G)


def block_diagonal(sp, dst, src, blocks, width, done):
    for k in range(blocks):
        sp.dma_start(dst[k * NS:(k + 1) * NS, k * width:(k + 1) * width], src).then_inc(done, 16)


NB = 5


def nodes_1(nc, sh, sum_d, w_msg, tab_d):
    B, N, ps, ones, rows = sh.B, sh.N, sh.ps, sh.ones, sh.rows_sb
    L = LOCAL
    steps = L // NB
    scope = ExitStack()
    with scope:
        sbp, semp = sh.alloc(scope)
        tot = sbp("tot1", [B, P, NS], F32)
        val = sbp("val1", [B, L, NS], F32)
        sq = sbp("sq1", [B, L, NS], F32)
        m = sbp("m1", [B, 8, NS], F32)
        lnv = sbp("lnv1", [B, L], F32)
        wd = sbp("wd", [NB * NS, NB * P], F32)
        h_t = sbp("h_t", [NB * NS, 2, B], F32)
        tab = sbp("tab", [B, 4, NB * P], F32)
        sync, tensor, scalar, tot_ready = reduce_units(nc, sh, sum_d, NS, tot, 1, sbp, semp)
        link_s, asked, answered = semp("nlink1"), semp("asked1"), semp("answered1")
        root_asked, root_ready, h_ready = semp("root_asked1"), semp("root_ready1"), semp("h_ready1")
        wd_zero, wd_in, h_on_pe, h_t_ready = semp("wd_zero"), semp("wd_in"), semp("h_on_pe"), semp("h_t_ready")
        rows_on_pe, tab_ready = semp("rows_on_pe"), semp("tab_ready")
        tab_out = [semp(f"tab_out1{s}") for s in range(4)]
        block = scope.enter_context(nc.Block())

        @block.gpsimd
        def _(pool):
            nc.gpsimd.memset(wd[:, :], 0.0).then_inc(wd_zero, 1)

        @block.sync
        def _(sp):
            sync(sp)
            sp.wait_ge(wd_zero, 1)
            block_diagonal(sp, wd, w_msg, NB, P, wd_in)
            tab_v = tab_d.rearrange("(b l) f -> b l f", l=L)
            for k in range(steps):
                sp.wait_ge(tab_ready, k + 1)
                sp.dma_start(tab_v[:, k * NB:(k + 1) * NB, :].rearrange("b l f -> b (l f)"), tab[:, k % 4, :])\
                  .then_inc(tab_out[k % 4], 16)
            for s in range(4):
                sp.wait_ge(tab_out[s], 16 * len(range(s, steps, 4)))

        @block.tensor
        def _(pe):
            tensor(pe)
            for k in range(2):
                pe.wait_ge(asked, k + 1)
                nc.tensor.matmul(ps[0:B, 0, k * NS:(k + 1) * NS], ones[0:B, 0:B], m[:, k, :], start=True,
                                 stop=True).then_inc(answered, 1)
            pe.wait_ge(h_ready, 1)
            pe.wait_ge(wd_in, 16 * NB)

            def turn(k):
                if k >= 2:
                    pe.wait_ge(h_t_ready, k - 1)
                nc.tensor.transpose(ps[0:NB * NS, 1 + k % 2, 0:B],
                                    sh.h_sb[:, k * NB:(k + 1) * NB, :].rearrange("b l f -> b (l f)"),
                                    sh.ident[0:B, 0:B]).then_inc(h_on_pe, 1)
            turn(0)
            for k in range(steps):
                if k + 1 < steps:
                    turn(k + 1)
                pe.wait_ge(h_t_ready, k + 1)
                if k >= 2:
                    pe.wait_ge(tab_ready, k - 1)
                for s in range(2):
                    half = NB * P // 2
                    last = nc.tensor.matmul(ps[0:B, 4 + 2 * (k % 2) + s, 0:half], h_t[:, k % 2, :],
                                            wd[:, s * half:(s + 1) * half], start=True, stop=True)
                last.then_inc(rows_on_pe, 1)

        @block.scalar
        def _(act):
            scalar(act)
            act.wait_ge(root_asked, 1)
            nc.scalar.activation(m[:, 4, :], m[:, 4, :], ACT.Sqrt).then_inc(root_ready, 1)
            act.wait_ge(root_asked, 2)
            nc.scalar.activation(lnv[:, :], lnv[:, :], ACT.Sqrt).then_inc(root_ready, 1)
            for k in range(steps):
                act.wait_ge(rows_on_pe, k + 1)
                if k >= 4:
                    act.wait_ge(tab_out[k % 4], 16 * (k // 4))
                half = NB * P // 2
                nc.scalar.activation(tab[:, k % 4, :].rearrange("b (s x) -> b s x", s=2),
                                     ps[0:B, 4 + 2 * (k % 2):6 + 2 * (k % 2), 0:half], ACT.Copy).then_inc(tab_ready, 1)

        @block.vector
        def _(dve):
            link = Linker(dve, link_s)
            over_l = lambda a: a.rearrange("b l f -> b f l")
            bc = lambda row: m[:, row, :].unsqueeze(1).to_broadcast([B, L, NS])
            dve.wait_ge(tot_ready, 1)
            link(nc.vector.tensor_tensor(val[:, :, :], tot[:, 0:L, :],
                                         sh.rcount[:, :].unsqueeze(2).to_broadcast([B, L, NS]), ALU.mult))
            link(nc.vector.tensor_scalar(val[:, :, :], val[:, :, :], float(NS + NV) ** -0.5, None, ALU.mult))
            link(nc.vector.tensor_reduce(m[:, 0, :], over_l(val[:, :, :]), AX.X, ALU.add))
            dve.engine_nop().then_inc(asked, 1)
            dve.wait_ge(answered, 1)
            link(nc.vector.tensor_scalar(m[:, 3, :], ps[0:B, 0, 0:NS], 1.0 / N, None, ALU.mult))
            link(nc.vector.tensor_tensor(val[:, :, :], val[:, :, :], bc(3), ALU.subtract))
            link(nc.vector.tensor_tensor(sq[:, :, :], val[:, :, :], val[:, :, :], ALU.mult))
            link(nc.vector.tensor_reduce(m[:, 1, :], over_l(sq[:, :, :]), AX.X, ALU.add))
            dve.engine_nop().then_inc(asked, 1)
            dve.wait_ge(answered, 2)
            link(nc.vector.tensor_scalar(m[:, 4, :], ps[0:B, 0, NS:2 * NS], 1.0 / N, EPS, ALU.mult, ALU.add))
            dve.engine_nop().then_inc(root_asked, 1)
            dve.wait_ge(root_ready, 1)
            link(nc.vector.reciprocal(m[:, 4, :], m[:, 4, :]))
            g0 = 2 * NS + NV
            link(nc.vector.tensor_tensor(m[:, 4, :], m[:, 4, :], rows[:, g0:g0 + NS], ALU.mult))
            link(nc.vector.tensor_tensor(val[:, :, :], val[:, :, :], bc(4), ALU.mult))
            link(nc.vector.tensor_tensor(val[:, :, :], val[:, :, :],
                                         rows[:, g0 + NS:g0 + 2 * NS].unsqueeze(1).to_broadcast([B, L, NS]), ALU.add))
            link(nc.vector.tensor_tensor(sh.x_sb[:, :, :], sh.x_sb[:, :, :], val[:, :, :], ALU.add))
            sh.layernorm_relu(dve, link, sh.x_sb, sh.h_sb, lnv, sq, root_asked, root_ready, 2)
            dve.engine_nop().then_inc(h_ready, 1)
            for k in range(steps):
                dve.wait_ge(h_on_pe, k + 1)
                if k >= 2:
                    dve.wait_ge(rows_on_pe, k - 1)
                nc.vector.tensor_copy(h_t[:, k % 2, :], ps[0:NB * NS, 1 + k % 2, 0:B]).then_inc(h_t_ready, 1)


def pass_2(nc, sh, tab_d, sum_d):
    G, ps = sh.G, sh.ps
    scope = ExitStack()
    with scope:
        sbp, semp = sh.alloc(scope)
        comp = sbp("comp2", [P, RING, GROUP, CMP], F32)
        at = sbp("at2", [P, RING, GROUP], I32)
        ys = sbp("ys", [P, RING, GROUP, NS * 8], F32)
        prod = sbp("prod2", [P, 2, GROUP, NS, 8], F32)
        pre = sbp("pre2", [P, 2, GROUP, NS], F32)
        msg = sbp("msg2", [P, 2, GROUP, NS], F32)
        away = sbp("away2", [P, 2, GROUP, P], F32)
        owns = sbp("owns2", [P, 2, GROUP, P], F32)
        sums = sbp("sums2_sb", [P, RING, GU, NS], F32)
        comp_in = [semp(f"comp_in2{k}") for k in range(RING)]
        ys_in = [semp(f"ys_in{k}", True) for k in range(RING)]
        sums_out = [semp(f"sums_out2{k}") for k in range(RING)]
        at_ready, prod_ready, pre_ready, msg_ready = semp("at_ready2"), semp("prod_ready2"), semp("pre_ready2"), semp("msg_ready2")
        away_ready = semp("away_ready2")
        owns_ready, summed, sums_ready, turn = semp("owns_ready2"), semp("summed2"), semp("sums_ready2"), semp("pool_turn2")
        block = scope.enter_context(nc.Block())

        @block.sync
        def _(sp):
            def step(n):
                if exists(n, 5, G):
                    slot = moved(n, 5)[1]
                    if exists(n, 1, G):
                        sp.wait_ge(at_ready, count(n, 1))
                        sp.wait_ge(prod_ready, count(n, 1))
                        sp.wait_ge(away_ready, count(n, 1))
                    sp.dma_start(comp[:, slot].rearrange("p t f -> p (t f)"),
                                 sh.cmp_d[bass.ds(index(n, 5), 1)].rearrange("o p x -> p (o x)"))\
                      .then_inc(comp_in[slot], 16)
                if exists(n, -1, G):
                    slot = moved(n, -1)[1]
                    sp.wait_ge(sums_ready, count(n, -1))
                    sp.dma_start(sum_d[bass.ds(index(n, -1), 1)].rearrange("o p x -> p (o x)"),
                                 sums[:, slot].rearrange("p u f -> p (u f)")).then_inc(sums_out[slot], 16)
            walk(sp, step, G)
            for k in range(RING):
                sp.wait_ge(sums_out[k], 16 * (G // RING))

        @block.gpsimd
        def _(pool):
            def step(n):
                if exists(n, 3, G):
                    slot = moved(n, 3)[1]
                    pool.wait_ge(at_ready, count(n, 3))
                    if exists(n, -1, G):
                        pool.wait_ge(prod_ready, count(n, -1))
                    pool.sem_inc(turn, 1)
                    for t in range(GROUP):
                        nc.gpsimd.indirect_dma_start(
                            out=ys[:, slot, t, :], out_offset=None, in_=tab_d,
                            in_offset=bass.IndirectOffsetOnAxis(ap=at[:, slot, t:t + 1], axis=0))\
                          .then_inc(ys_in[slot], 16)
            walk(pool, step, G)

        @block.scalar
        def _(act):
            def step(n):
                if exists(n, 3, G):
                    slot = moved(n, 3)[1]
                    act.wait_ge(comp_in[slot], used(n, 3))
                    if exists(n, -1, G):
                        act.wait_ge(ys_in[slot], used(n, -1, 16 * GROUP))
                    nc.scalar.activation(at[:, slot], comp[:, slot, :, C_DST], ACT.Copy).then_inc(at_ready, 1)
                if exists(n, 0, G):
                    half = n[1] % 2
                    for t in range(GROUP):
                        last = nc.scalar.activation(away[:, half, t, :], sh.iota_p[:, :], ACT.Square,
                                                    bias=comp[:, n[1], t, C_NLO:C_NLO + 1])
                    last.then_inc(away_ready, 1)
                if exists(n, -1, G):
                    half = (n[1] + 1) % 2
                    act.wait_ge(pre_ready, count(n, -1))
                    if exists(n, -3, G):
                        act.wait_ge(summed, count(n, -3))
                    nc.scalar.activation(msg[:, half], pre[:, half], ACT.Silu, scale=float(NS * 8) ** -0.5)\
                      .then_inc(msg_ready, 1)
                if exists(n, 0, G):
                    half = n[1] % 2
                    act.wait_ge(away_ready, count(n))
                    if exists(n, -2, G):
                        act.wait_ge(summed, count(n, -2))
                    nc.scalar.activation(owns[:, half], away[:, half], ACT.Relu, bias=1.0, scale=-1.0)\
                      .then_inc(owns_ready, 1)
                if exists(n, -3, G):
                    slot = moved(n, -3)[1]
                    act.wait_ge(summed, count(n, -3))
                    if exists(n, -7, G):
                        act.wait_ge(sums_out[slot], used(n, -7))
                    nc.scalar.activation(sums[:, slot], ps[:, 6 + slot % 2, 0:GU * NS]
                                         .rearrange("p (u f) -> p u f", f=NS), ACT.Copy).then_inc(sums_ready, 1)
            walk(act, step, G)

        @block.tensor
        def _(pe):
            def step(n):
                if exists(n, -1, G):
                    half = (n[1] + 1) % 2
                    pe.wait_ge(msg_ready, count(n, -1))
                    pe.wait_ge(owns_ready, count(n, -1))
                    if exists(n, -3, G):
                        pe.wait_ge(sums_ready, count(n, -3))
                    for u in range(GU):
                        for j in range(UNIT):
                            t = u * UNIT + j
                            last = nc.tensor.matmul(ps[:, 6 + half, u * NS:(u + 1) * NS], owns[:, half, t, :],
                                                    msg[:, half, t, :], start=(j == 0), stop=(j == UNIT - 1))
                    last.then_inc(summed, 1)
            walk(pe, step, G)

        @block.vector
        def _(dve):
            def step(n):
                if not exists(n, 0, G):
                    return
                slot, half = n[1], n[1] % 2
                dve.wait_ge(ys_in[slot], used(n, 0, 16 * GROUP))
                dve.wait_ge(comp_in[slot], used(n))
                nc.vector.tensor_tensor(prod[:, half], ys[:, slot].rearrange("p t (h j) -> p t h j", j=8),
                                        comp[:, slot, :, C_EA8:C_EA8 + 8].unsqueeze(2).to_broadcast([P, GROUP, NS, 8]),
                                        ALU.mult).then_inc(prod_ready, 1)
                dve.wait_ge(prod_ready, count(n))
                if exists(n, -2, G):
                    dve.wait_ge(msg_ready, count(n, -2))
                nc.vector.tensor_reduce(pre[:, half], prod[:, half], AX.X, ALU.add).then_inc(pre_ready, 1)
            walk(dve, step, G)


def nodes_2(nc, sh, sum_d, w_lin_t, w_upd, w_out, out):
    B, ps = sh.B, sh.ps
    L = LOCAL
    steps = L // NB
    W = NB * NS
    scope = ExitStack()
    with scope:
        sbp, semp = sh.alloc(scope)
        tot = sbp("tot2", [B, P, NS], F32)
        lin_d = sbp("lin_d", [W, W], F32)
        upd_d = sbp("upd_d", [W, NB * 256], F32)
        both_d = sbp("both_d", [W, NB * 256], F32)
        out_d = sbp("out_d", [W, W], F32)
        a_t = sbp("a_t", [W, 2, B], F32)
        hv = sbp("hv", [B, 2, NB * 256], F32)
        u = sbp("u", [B, L, NS], F32)
        su = sbp("su", [B, L, NS], F32)
        sync, tensor, scalar, tot_ready = reduce_units(nc, sh, sum_d, NS, tot, 2, sbp, semp)
        zero, w_in, both_on_pe, both_ready = semp("zero2"), semp("w_in2"), semp("both_on_pe"), semp("both_ready")
        a_on_pe, a_t_ready, v_on_pe, hv_ready = semp("a_on_pe"), semp("a_t_ready"), semp("v_on_pe"), semp("hv_ready")
        u_ready, su_ready, s_on_pe, s_t_ready = semp("u_ready"), semp("su_ready"), semp("s_on_pe"), semp("s_t_ready")
        o_on_pe, x_ready, out_done, xh_ready = semp("o_on_pe"), semp("x_ready"), semp("out_done"), semp("xh_ready")
        block = scope.enter_context(nc.Block())
        v_cuts = [(0, 2), (2, 4), (4, 5)]

        @block.gpsimd
        def _(pool):
            for t in (lin_d, upd_d, out_d):
                nc.gpsimd.memset(t[:, :], 0.0).then_inc(zero, 1)

        @block.sync
        def _(sp):
            sync(sp)
            sp.wait_ge(zero, 3)
            block_diagonal(sp, lin_d, w_lin_t, NB, NS, w_in)
            block_diagonal(sp, upd_d, w_upd, NB, 256, w_in)
            block_diagonal(sp, out_d, w_out, NB, NS, w_in)
            sp.wait_ge(x_ready, steps)
            sp.dma_start(out.rearrange("(b l) f -> b l f", l=L), sh.x_sb[:, :, :]).then_inc(out_done, 16)
            sp.wait_ge(out_done, 16)

        @block.tensor
        def _(pe):
            tensor(pe)
            pe.wait_ge(w_in, 16 * 3 * NB)
            for c, (a, b) in enumerate(v_cuts):
                last = nc.tensor.matmul(ps[0:W, c, 0:(b - a) * 256], lin_d[:, :], upd_d[:, a * 256:b * 256],
                                        start=True, stop=True)
            last.then_inc(both_on_pe, 1)
            pe.wait_ge(both_ready, 1)
            for k in range(steps):
                l0 = slice(k * NB, (k + 1) * NB)
                if k >= 1:
                    pe.wait_ge(a_t_ready, k)
                nc.tensor.transpose(ps[0:W, 7, 0:B], tot[:, l0, :].rearrange("b l f -> b (l f)"),
                                    sh.ident[0:B, 0:B]).then_inc(a_on_pe, 1)
                pe.wait_ge(a_t_ready, k + 1)
                if k >= 2:
                    pe.wait_ge(hv_ready, k - 1)
                for c, (a, b) in enumerate(v_cuts):
                    last = nc.tensor.matmul(ps[0:B, 3 * (k % 2) + c, 0:(b - a) * 256], a_t[:, k % 2, :],
                                            both_d[:, a * 256:b * 256], start=True, stop=True)
                last.then_inc(v_on_pe, 1)
            pe.wait_ge(su_ready, 1)
            for k in range(steps):
                l0 = slice(k * NB, (k + 1) * NB)
                if k >= 2:
                    pe.wait_ge(s_t_ready, k - 1)
                nc.tensor.transpose(ps[0:W, k % 2, 0:B], su[:, l0, :].rearrange("b l f -> b (l f)"),
                                    sh.ident[0:B, 0:B]).then_inc(s_on_pe, 1)
                pe.wait_ge(s_t_ready, k + 1)
                if k >= 2:
                    pe.wait_ge(x_ready, k - 1)
                nc.tensor.matmul(ps[0:B, 2 + k % 2, 0:W], a_t[:, k % 2, :], out_d[:, :], start=True,
                                 stop=True).then_inc(o_on_pe, 1)

        @block.scalar
        def _(act):
            scalar(act)
            act.wait_ge(both_on_pe, 1)
            for c, (a, b) in enumerate(v_cuts):
                last = nc.scalar.activation(both_d[:, a * 256:b * 256], ps[0:W, c, 0:(b - a) * 256], ACT.Copy)
            last.then_inc(both_ready, 1)
            for k in range(steps):
                act.wait_ge(a_on_pe, k + 1)
                if k >= 2:
                    act.wait_ge(v_on_pe, k - 1)
                nc.scalar.activation(a_t[:, k % 2, :], ps[0:W, 7, 0:B], ACT.Copy).then_inc(a_t_ready, 1)
            act.wait_ge(u_ready, steps)
            nc.scalar.activation(su[:, :, :], u[:, :, :], ACT.Silu, scale=(NS * NS * NS) ** -0.5).then_inc(su_ready, 1)
            for k in range(steps):
                act.wait_ge(s_on_pe, k + 1)
                if k >= 2:
                    act.wait_ge(o_on_pe, k - 1)
                nc.scalar.activation(a_t[:, k % 2, :], ps[0:W, k % 2, 0:B], ACT.Copy).then_inc(s_t_ready, 1)

        @block.vector
        def _(dve):
            nc.vector.tensor_tensor(sh.x_sb[:, :, :], sh.x_sb[:, :, :], sh.h_sb[:, :, :], ALU.add).then_inc(xh_ready, 1)
            for k in range(steps):
                dve.wait_ge(v_on_pe, k + 1)
                for c, (a, b) in enumerate(v_cuts):
                    h_of = sh.h_sb[:, k * NB + a:k * NB + b, :].unsqueeze(2).to_broadcast([B, b - a, NS, NS])
                    last = nc.vector.tensor_tensor(
                        hv[:, k % 2, a * 256:b * 256].rearrange("b (l k i) -> b l k i", k=NS, i=NS),
                        ps[0:B, 3 * (k % 2) + c, 0:(b - a) * 256].rearrange("b (l k i) -> b l k i", k=NS, i=NS),
                        h_of, ALU.mult)
                last.then_inc(hv_ready, 1)
                dve.wait_ge(hv_ready, k + 1)
                nc.vector.tensor_reduce(u[:, k * NB:(k + 1) * NB, :], hv[:, k % 2, :]
                                        .rearrange("b (l k i) -> b l k i", k=NS, i=NS), AX.X, ALU.add).then_inc(u_ready, 1)
            dve.wait_ge(xh_ready, 1)
            for k in range(steps):
                dve.wait_ge(o_on_pe, k + 1)
                x_of = sh.x_sb[:, k * NB:(k + 1) * NB, :].rearrange("b l f -> b (l f)")
                nc.vector.scalar_tensor_tensor(out=x_of, in0=ps[0:B, 2 + k % 2, 0:W], scalar=float(NS) ** -0.5,
                                               in1=x_of, op0=ALU.mult, op1=ALU.add).then_inc(x_ready, 1)


_INS = ["x", "src", "dst", "ea3", "ea48", "ea8", "w1", "b1", "w2_0", "w2_1", "rows", "w_msg", "w_lin_t", "w_upd", "w_out"]


def lay_out(i):
    f = lambda n: np.ascontiguousarray(i[n])
    g = "L0_gnn_"

    def second(k):
        w, b = f(f"{g}fc{k}_w2"), f(f"{g}fc{k}_b2")
        w = np.concatenate([w, b[None, :]], 0)
        a, v = w[:, :NS * NS].reshape(-1, NS, NS), w[:, NS * NS:]
        if k == 0:
            v = v.reshape(-1, NS, NV)
            return np.ascontiguousarray(np.concatenate([v.transpose(0, 2, 1), a.transpose(0, 2, 1)], 1).reshape(-1, 320))
        v = v.reshape(-1, NV, NS)
        return np.ascontiguousarray(np.concatenate([a.transpose(0, 2, 1), v.transpose(0, 2, 1)], 2).reshape(-1, 320))

    rows = np.concatenate([f(g + n) for n in ("bn0_gs", "bn0_bs", "bn0_gv", "bn1_gs", "bn1_bs")])[None, :]
    return {
        "x": f("x"), "src": f("src"), "dst": f("dst"), "ea3": f("edge_attr_3"), "ea48": f("edge_attr_48"),
        "ea8": f("edge_attr_8"),
        "w1": np.stack([f(g + "fc0_w1"), f(g + "fc1_w1")]), "b1": np.stack([f(g + "fc0_b1"), f(g + "fc1_b1")])[:, None, :],
        "w2_0": second(0), "w2_1": second(1), "rows": np.ascontiguousarray(rows),
        "w_msg": np.ascontiguousarray(f("L1_gnn_W_msg_tp").transpose(0, 2, 1).reshape(NS, 128)),
        "w_lin_t": np.ascontiguousarray(f("L1_gnn_W_msg_lin").T),
        "w_upd": np.ascontiguousarray(f("L1_gnn_W_upd_tp").transpose(1, 2, 0).reshape(NS, 256)),
        "w_out": f("L1_gnn_W_upd_lin"),
    }


def kernel(**inputs):
    import numpy as _np
    import concourse.bacc as _bacc
    from concourse import mybir as _mybir
    from concourse.bass_utils import run_bass_kernel_spmd as _run

    nc = _bacc.Bacc("TRN2", target_bir_lowering=False, num_devices=1)
    given = lay_out({n: _np.asarray(a) for n, a in inputs.items()})
    arrays, args = {}, []
    for name in _INS:
        a = given[name]
        arrays[f"in_{name}"] = a
        args.append(nc.dram_tensor(f"in_{name}", a.shape, _mybir.dt.from_np(a.dtype), kind="ExternalInput").ap())
    out = nc.dram_tensor("out_0", given["x"].shape, _mybir.dt.float32, kind="ExternalOutput").ap()
    gnn(nc, *args, out)
    r = _run(nc, [arrays], core_ids=[0])
    return r.results[0]["out_0"]
```

```python
import numpy as np
import concourse.bass as bass
from concourse import mybir
from contextlib import ExitStack

F32 = mybir.dt.float32
BF16 = mybir.dt.bfloat16
FP16 = mybir.dt.float16
I32 = mybir.dt.int32
U32 = mybir.dt.uint32
U16 = mybir.dt.uint16
ALU = mybir.AluOpType
ACT = mybir.ActivationFunctionType
AX = mybir.AxisListType

P = 128
LOCAL = 125
UNIT = 2
GROUP = 4
GU = GROUP // UNIT
RING = 4
EPS = 1e-5

SMALL = 72
CMP = 13
C_EA8, C_RHAT, C_NLO, C_DST = 0, 8, 11, 12
READ = SMALL + CMP
PART0 = (0, 2 * READ)

NS, NV, HID = 16, 4, 48
REC = 2 * SMALL + CMP
F0 = NS + 3 * NV + 1
T0 = NS + 3 * NV



def moved(n, by):
    body, slot = n
    return body + (slot + by) // RING, (slot + by) % RING


def exists(n, by, groups):
    body, slot = moved(n, by)
    return not isinstance(body, int) or 0 <= body * RING + slot < groups


def index(n, by=0):
    body, slot = moved(n, by)
    return body * RING + slot


def count(n, by=0, per=1, start=0):
    return index(n, by) * per + per + start


def used(n, by=0, each=16):
    return moved(n, by)[0] * each + each


def walk(eng, step, groups):
    bodies = groups // RING
    for g in range(-2 * RING, 2 * RING):
        step((g // RING, g % RING))
    with eng.Fori(2, bodies - 2) as body:
        for slot in range(RING):
            step((body, slot))
    for g in range((bodies - 2) * RING, (bodies + 2) * RING):
        step((g // RING, g % RING))


class Kept:
    pass


def gnn(nc, x, src, dst, ea3, ea48, ea8, w1, b1, w2_0, w2_1, rows, w_msg, w_lin_t, w_upd, w_out, out):
    N, E = x.shape[0], src.shape[0]
    B = N // LOCAL
    C = E // P
    assert N == B * LOCAL and E == C * P and B <= 100
    units = -(-E // (P * UNIT)) + B
    G = -(-units // (GU * RING)) * RING
    K = max(k for k in range(1, P + 1) if G % k == 0)
    CH = G // K
    STEP, BATCH = 25, 5
    assert C % STEP == 0
    even = C // STEP // 2 * 2 * STEP
    chunks = [10 * STEP, 10 * STEP] + [min(20 * STEP, even - c) for c in range(20 * STEP, even, 20 * STEP)]
    chunks += [C - even] if C > even else []
    LAST = G * GU * UNIT * P - E - B * UNIT * P + P
    assert UNIT == 2 and LAST >= P and B <= P

    rec_d = nc.dram_tensor("rec_sorted", (G, GU, P, UNIT * REC), F32, kind="Internal").ap()
    cmp_d = nc.dram_tensor("cmp_sorted", (G, P, GROUP * CMP), F32, kind="Internal").ap()
    sum0_d = nc.dram_tensor("sums0", (G, P, GU * F0), F32, kind="Internal").ap()
    sum1_d = nc.dram_tensor("sums1", (G, P, GU * NS), F32, kind="Internal").ap()
    sum2_d = nc.dram_tensor("sums2", (G, P, GU * NS), F32, kind="Internal").ap()
    tab0_d = nc.dram_tensor("table0", (N, NS), F32, kind="Internal").ap()
    tab1_d = nc.dram_tensor("table1", (N, T0), F32, kind="Internal").ap()
    tab2_d = nc.dram_tensor("table2", (N, NS * 8), F32, kind="Internal").ap()

    whole = ExitStack()
    with whole:
        spent = []

        def alloc(scope):
            def semaphore(name, by_pool_dma=False):
                s = nc.alloc_semaphore(name)
                if not by_pool_dma:
                    spent.append(s)
                return s
            return lambda name, shape, dt: scope.enter_context(nc.sbuf_tensor(name, shape, dt)), semaphore

        def clear_spent():
            nc.clear_and_free_semaphores(list(spent))
            spent.clear()
            nc.all_engine_barrier()
        sb, sem = alloc(whole)
        ps = whole.enter_context(nc.psum_tensor("ps", [P, 8, 512], F32))

        x_sb = sb("x_sb", [B, LOCAL, NS], F32)
        h_sb = sb("h_sb", [B, LOCAL, NS], F32)
        rcount = sb("rcount", [B, LOCAL], F32)
        owner = sb("owner", [K, CH * GU, B], F32)
        ident = sb("ident", [P, P], F32)
        ident_b = sb("ident_b", [P, P], BF16)
        ones = sb("ones", [P, P], F32)
        rows_sb = sb("rows_sb", [B, rows.shape[1]], F32)
        iota_p = sb("iota_p", [P, P], F32)
        iota_n = sb("iota_n", [P, P], F32)

        bc_ln = lambda a: a[:, :].unsqueeze(2).to_broadcast([B, LOCAL, NS])

        def ln_before(link, xin, hout, var, tmp, sq_ready):
            link(nc.vector.tensor_reduce(var[:, :], xin[:, :, :], AX.X, ALU.add))
            link(nc.vector.tensor_scalar(var[:, :], var[:, :], 1.0 / NS, None, ALU.mult))
            link(nc.vector.tensor_tensor(hout[:, :, :], xin[:, :, :], bc_ln(var), ALU.subtract))
            link(nc.vector.tensor_tensor(tmp[:, :, 0:NS], hout[:, :, :], hout[:, :, :], ALU.mult))
            link(nc.vector.tensor_reduce(var[:, :], tmp[:, :, 0:NS], AX.X, ALU.add))
            nc.vector.tensor_scalar(var[:, :], var[:, :], 1.0 / NS, EPS, ALU.mult, ALU.add).then_inc(sq_ready, 1)

        def ln_behind(link, hout, var):
            link(nc.vector.reciprocal(var[:, :], var[:, :]))
            link(nc.vector.tensor_tensor(hout[:, :, :], hout[:, :, :], bc_ln(var), ALU.mult))
            link(nc.vector.tensor_scalar(hout[:, :, :], hout[:, :, :], 0.0, None, ALU.max))

        sort = ExitStack()
        with sort:
            sbs, sems = alloc(sort)
            fill_out = sems("fill_out")
            loc = sbs("loc", [P, C], F32)
            rhat = sbs("rhat", [P, C, 3], F32)
            bucket = sbs("bucket", [P, C], BF16)
            base_hi = sbs("base_hi", [B, C], BF16)
            base_lo = sbs("base_lo", [B, C], FP16)
            iota_b = sbs("iota_b", [P, P], F32)
            spread = sbs("spread", [B, B, P], BF16)
            tri_b = sbs("tri_b", [P, P], BF16)
            ones_b = sbs("ones_b", [P, P], BF16)
            pads_out = sems("pads_out", True)
            pads_early = B // 5
            pad = sbs("pad", [P, 2, REC], F32)
            pad_to = sbs("pad_to", [P, B], U32)
            span = sbs("span", [K, 2 * P], F32)
            unit_no = sbs("unit_no", [K, CH * GU], F32)

            def write_pads(b):
                nc.gpsimd.indirect_dma_start(
                    out=rec_d.rearrange("g u p (j f) -> (g u p j) f", f=2 * REC),
                    out_offset=bass.IndirectOffsetOnAxis(ap=pad_to[:, b:b + 1], axis=0),
                    in_=pad[:, :, :].rearrange("p j f -> p (j f)"), in_offset=None).then_inc(pads_out, 16)

            prep = ExitStack()
            with prep:
                sbp, semp = alloc(prep)
                srci = sbp("srci", [P, C], I32)
                f0 = sbp("f0", [P, C], F32)
                f1 = sbp("f1", [P, C], F32)
                f2 = sbp("f2", [P, C], F32)
                lnv = sbp("lnv", [B, LOCAL], F32)
                lnt = sbp("lnt", [B, LOCAL, NS], F32)
                rows1 = sbp("rows1", [1, rows.shape[1]], F32)
                eq = sbp("eq", [P, 4, C], BF16)
                pick = sbp("pick", [P, 2 * P], BF16)
                zb = sbp("zb", [P, 512], BF16)
                tri = sbp("tri", [P, P], F32)
                tri_in = sbp("tri_in", [P, P], F32)
                nb = sbp("nb", [B, 5], F32)
                ends = sbp("ends", [B, 3], F32)
                ends_bc = sbp("ends_bc", [P, 3, B], F32)
                order = sbp("order", [P, 1], F32)
                spares = sbp("spares", [B, 1], F32)
                spare = sbp("spare", [P, B], F32)
                pad_f = sbp("pad_f", [P, B], F32)
                nbi = sbp("nbi", [B, 1], I32)
                src_in, x_in, v_in, rows_in = semp("src_in"), semp("x_in"), semp("v_in"), semp("rows_in")
                fill_ready, tab_out = semp("fill_ready"), semp("tab_out")
                const_ready, link_s, sq_ready, rt_ready = semp("const_ready"), semp("link_s"), semp("sq_ready"), semp("rt_ready")
                eq_ready, eq_used, counted = semp("eq_ready"), semp("eq_used"), semp("counted")
                pe_turn = semp("pe_turn")
                ends_ready, ends_on_pe = semp("ends_ready"), semp("ends_on_pe")
                n_ready, starts_ready, rows_bc, h_ready = semp("n_ready"), semp("starts_ready"), semp("rows_bc"), semp("h_ready")
                pool_link, pads_placed = semp("pool_link"), semp("pads_placed")
                count_cols = [(c, min(448, C - c)) for c in range(0, C, 448)]

                block = prep.enter_context(nc.Block())

                @block.sync
                def _(sp):
                    sp.dma_start(srci[:, :], src.rearrange("(p c) -> p c", p=P)).then_inc(src_in, 16)
                    sp.dma_start(rhat[:, :, :], ea3.rearrange("(p c) f -> p c f", p=P)).then_inc(v_in, 16)
                    sp.dma_start(x_sb[:, :, :], x.rearrange("(b l) f -> b l f", l=LOCAL)).then_inc(x_in, 16)
                    sp.dma_start(rows1[:, :], rows).then_inc(rows_in, 16)
                    sp.wait_ge(fill_ready, 2)
                    rec_f = rec_d.rearrange("g u p (j f) -> (g u p j) f", f=REC)[G * GU * UNIT * P - LAST:, :]
                    sp.dma_start(rec_f.rearrange("(r p) x -> p r x", p=P), pad[:, 0, :].unsqueeze(1)
                                 .to_broadcast([P, LAST // P, REC])).then_inc(fill_out, 16)
                    sp.wait_ge(fill_out, 16)
                    sp.wait_ge(h_ready, 1)
                    sp.dma_start(tab0_d.rearrange("(b l) f -> b l f", l=LOCAL), h_sb[:, :, :]).then_inc(tab_out, 16)
                    sp.wait_ge(tab_out, 16)

                @block.gpsimd
                def _(pool):
                    nc.gpsimd.memset(pad[:, :, :], 0.0).then_inc(fill_ready, 1)
                    pool.wait_ge(fill_ready, 1)
                    nc.gpsimd.memset(pad[:, :, SMALL + C_NLO:SMALL + C_NLO + 1], 1.0).then_inc(fill_ready, 1)
                    nc.gpsimd.iota(iota_n[:, :], pattern=[[-1, P]], base=0, channel_multiplier=0,
                                   allow_small_or_imprecise_dtypes=True)
                    nc.gpsimd.iota(order[:, :], pattern=[[0, 1]], base=0, channel_multiplier=1,
                                   allow_small_or_imprecise_dtypes=True)
                    nc.gpsimd.iota(iota_p[:, :], pattern=[[1, P]], base=0, channel_multiplier=0,
                                   allow_small_or_imprecise_dtypes=True)
                    nc.gpsimd.iota(iota_b[:, :], pattern=[[1, P]], base=0, channel_multiplier=0,
                                   allow_small_or_imprecise_dtypes=True)
                    nc.gpsimd.iota(unit_no[:, :], pattern=[[GU * K, CH], [1, GU]], base=0, channel_multiplier=GU,
                                   allow_small_or_imprecise_dtypes=True)
                    nc.gpsimd.iota(spares[:, :], pattern=[[0, 1]], base=0, channel_multiplier=P,
                                   allow_small_or_imprecise_dtypes=True)
                    nc.gpsimd.memset(ones[:, :], 1.0)
                    nc.gpsimd.memset(ident[:, :], 0.0)
                    nc.gpsimd.memset(zb[:, :], 0.0)
                    nc.gpsimd.memset(ones_b[:, :], 1.0)
                    nc.gpsimd.memset(pick[:, :], 0.0).then_inc(pool_link, 1)
                    pool.wait_ge(pool_link, 1)
                    nc.gpsimd.memset(pick[:, P:P + 1], 1.0)
                    nc.gpsimd.affine_select(out=ident[:, :], in_=ident[:, :], compare_op=ALU.not_equal, fill=1.0,
                                            base=0, pattern=[[-1, P]], channel_multiplier=1)
                    nc.gpsimd.affine_select(out=tri[:, :], in_=ones[:, :], compare_op=ALU.is_gt, fill=0.0,
                                            base=0, pattern=[[1, P]], channel_multiplier=-1)
                    nc.gpsimd.affine_select(out=tri_in[:, :], in_=ones[:, :], compare_op=ALU.is_ge, fill=0.0,
                                            base=0, pattern=[[1, P]], channel_multiplier=-1).then_inc(const_ready, 1)
                    nc.gpsimd.affine_select(out=tri_b[:, :], in_=ones_b[:, :], compare_op=ALU.is_gt, fill=0.0,
                                            base=0, pattern=[[1, P]], channel_multiplier=-1)
                    nc.gpsimd.affine_select(out=spread[:, :, :], in_=ones_b[0:B, 0:1].unsqueeze(2).to_broadcast([B, B, P]),
                                            compare_op=ALU.is_equal, fill=0.0, base=0, pattern=[[1, B], [0, P]],
                                            channel_multiplier=-1)
                    pool.wait_ge(fill_out, 16)
                    pool.wait_ge(pads_placed, 1)
                    for b in range(pads_early):
                        write_pads(b)

                @block.scalar
                def _(act):
                    act.wait_ge(sq_ready, 1)
                    nc.scalar.activation(f1[:, :], f0[:, :], ACT.Sqrt).then_inc(rt_ready, 1)
                    act.wait_ge(sq_ready, 2)
                    nc.scalar.activation(lnv[:, :], lnv[:, :], ACT.Sqrt).then_inc(rt_ready, 1)

                @block.tensor
                def _(pe):
                    pe.wait_ge(rows_in, 16)
                    pe.wait_ge(const_ready, 1)
                    nc.tensor.matmul(ps[0:B, 7, 0:rows.shape[1]], ones[0:1, 0:B], rows1[:, :], start=True,
                                     stop=True).then_inc(rows_bc, 1)
                    for j, (c, w) in enumerate(count_cols):
                        nc.tensor.matmul(ps[0:B, j, 0:w], zb[:, 0:B], zb[:, 0:w], start=True, stop=False)
                    with pe.Fori(0, B // 4) as i:
                        for s in range(4):
                            pe.wait_ge(eq_ready, 4 * i + s + 1)
                            pe.sem_inc(pe_turn, 1)
                            for j, (c, w) in enumerate(count_cols):
                                last = nc.tensor.matmul(ps[0:B, j, 0:w], pick[:, bass.ds(P - s - 4 * i, B)],
                                                        eq[:, s, c:c + w], start=False, stop=False)
                            last.then_inc(eq_used, 1)
                    for j, (c, w) in enumerate(count_cols):
                        last = nc.tensor.matmul(ps[0:B, j, 0:w], zb[:, 0:B], zb[:, 0:w], start=False, stop=True)
                    last.then_inc(counted, 1)
                    pe.wait_ge(n_ready, 1)
                    nc.tensor.matmul(ps[0:B, 7, 64:65], tri[0:B, 0:B], nb[:, 3:4], start=True, stop=True)
                    units_bc = nb[:, 3:4].to_broadcast([B, K])
                    nc.tensor.matmul(ps[0:K, 7, 128:128 + B], units_bc, tri[0:B, 0:B], start=True, stop=True)
                    nc.tensor.matmul(ps[0:K, 7, 256:256 + B], units_bc, tri_in[0:B, 0:B], start=True, stop=True)
                    nc.tensor.matmul(ps[0:B, 7, 65:66], ones[0:B, 0:B], nb[:, 3:4], start=True,
                                     stop=True).then_inc(starts_ready, 1)
                    pe.wait_ge(ends_ready, 1)
                    nc.tensor.matmul(ps[0:B, 7, 66:67], tri[0:B, 0:B], ends[:, 1:2], start=True, stop=True)\
                      .then_inc(ends_on_pe, 1)
                    pe.wait_ge(ends_ready, 2)
                    for k in range(3):
                        last = nc.tensor.matmul(ps[:, 6, k * P:k * P + B], ends[:, k:k + 1].to_broadcast([B, P]),
                                                ident[0:B, 0:B], start=True, stop=True)
                    last.then_inc(ends_on_pe, 1)

                @block.vector
                def _(dve):
                    linked = [0]

                    def link(ins):
                        linked[0] += 1
                        ins.then_inc(link_s, 1)
                        dve.wait_ge(link_s, linked[0])

                    def floor_of(out, value, whole_i, more):
                        link(nc.vector.tensor_copy(whole_i, value))
                        link(nc.vector.tensor_copy(out, whole_i))
                        link(nc.vector.tensor_tensor(more, out, value, ALU.is_gt))
                        link(nc.vector.tensor_tensor(out, out, more, ALU.subtract))

                    dve.wait_ge(src_in, 16)
                    link(nc.vector.tensor_copy(f0[:, :], srci[:, :]))
                    link(nc.vector.tensor_scalar(f1[:, :], f0[:, :], 1.0 / LOCAL, None, ALU.mult))
                    floor_of(f2[:, :], f1[:, :], srci[:, :], loc[:, :])
                    link(nc.vector.scalar_tensor_tensor(out=loc[:, :], in0=f2[:, :], scalar=-float(LOCAL), in1=f0[:, :],
                                                        op0=ALU.mult, op1=ALU.add))
                    link(nc.vector.tensor_scalar(f1[:, :], loc[:, :], 0.0, None, ALU.is_lt))
                    link(nc.vector.tensor_scalar(f0[:, :], loc[:, :], float(LOCAL), None, ALU.is_ge))
                    link(nc.vector.tensor_tensor(f0[:, :], f0[:, :], f1[:, :], ALU.subtract))
                    link(nc.vector.tensor_tensor(bucket[:, :], f2[:, :], f0[:, :], ALU.add))
                    link(nc.vector.scalar_tensor_tensor(out=loc[:, :], in0=f0[:, :], scalar=-float(LOCAL), in1=loc[:, :],
                                                        op0=ALU.mult, op1=ALU.add))
                    dve.wait_ge(const_ready, 1)
                    nc.vector.tensor_copy(ident_b[:, :], ident[:, :])
                    dve.wait_ge(rows_bc, 1)
                    nc.vector.tensor_copy(rows_sb[:, :], ps[0:B, 7, 0:rows.shape[1]])

                    def table_a():
                        dve.wait_ge(x_in, 16)
                        ln_before(link, x_sb, h_sb, lnv, lnt, sq_ready)

                    def table_b():
                        dve.wait_ge(rt_ready, 2)
                        ln_behind(link, h_sb, lnv)
                        dve.engine_nop().then_inc(h_ready, 1)

                    def square(c, out):
                        link(nc.vector.tensor_tensor(out[:, :], rhat[:, :, c], rhat[:, :, c], ALU.mult))

                    def directions_a():
                        dve.wait_ge(v_in, 16)
                        square(0, f0)

                    def directions_b(c):
                        square(c, f1)
                        link(nc.vector.tensor_tensor(f0[:, :], f0[:, :], f1[:, :], ALU.add))
                        if c == 2:
                            dve.engine_nop().then_inc(sq_ready, 1)

                    def directions_c():
                        dve.wait_ge(rt_ready, 1)
                        link(nc.vector.tensor_scalar(f1[:, :], f1[:, :], 1e-12, None, ALU.add))

                    def directions_d(q):
                        cols = slice(C * q // 4, C * (q + 1) // 4)
                        link(nc.vector.reciprocal(f0[:, cols], f1[:, cols]))

                    def directions_e(c):
                        nc.vector.tensor_tensor(rhat[:, :, c], rhat[:, :, c], f0[:, :], ALU.mult)

                    between = [directions_a, lambda: directions_b(1), lambda: directions_b(2), directions_c,
                               lambda: directions_d(0), lambda: directions_d(1), lambda: directions_d(2),
                               lambda: directions_d(3), lambda: directions_e(0), lambda: directions_e(1),
                               lambda: directions_e(2), table_a, table_b]
                    for s in range(4):
                        nc.vector.tensor_scalar(eq[:, s, :], bucket[:, :], iota_b[:, s:s + 1], None,
                                                ALU.is_equal).then_inc(eq_ready, 1)
                    rounds = B // 4 - 1
                    for k, work in enumerate(between):
                        work()
                        a, b = 1 + rounds * k // len(between), 1 + rounds * (k + 1) // len(between)
                        if a < b:
                            with dve.Fori(a, b) as i:
                                for s in range(4):
                                    dve.wait_ge(eq_used, 4 * i + s - 3)
                                    nc.vector.tensor_scalar(eq[:, s, :], bucket[:, :], iota_b[:, bass.ds(4 * i + s, 1)],
                                                            None, ALU.is_equal).then_inc(eq_ready, 1)
                    dve.wait_ge(counted, 1)
                    for j, (c, w) in enumerate(count_cols):
                        last = nc.vector.tensor_copy(f0[0:B, c:c + w], ps[0:B, j, 0:w])
                    link(last)
                    link(nc.vector.tensor_tensor_scan(f1[0:B, :], ones[0:B, 0:1].to_broadcast([B, C]), f0[0:B, :], 0.0,
                                                      ALU.mult, ALU.add))
                    link(nc.vector.tensor_tensor(f1[0:B, :], f1[0:B, :], f0[0:B, :], ALU.subtract))
                    link(nc.vector.tensor_tensor(nb[:, 0:1], f1[0:B, C - 1:C], f0[0:B, C - 1:C], ALU.add))
                    link(nc.vector.tensor_scalar(nb[:, 1:2], nb[:, 0:1], float(UNIT * P - 1), 1.0 / (UNIT * P),
                                                 ALU.add, ALU.mult))
                    link(nc.vector.tensor_copy(nbi[:, :], nb[:, 1:2]))
                    link(nc.vector.tensor_copy(nb[:, 3:4], nbi[:, :]))
                    link(nc.vector.tensor_tensor(nb[:, 2:3], nb[:, 3:4], nb[:, 1:2], ALU.is_gt))
                    link(nc.vector.tensor_tensor(nb[:, 3:4], nb[:, 3:4], nb[:, 2:3], ALU.subtract))
                    dve.engine_nop().then_inc(n_ready, 1)
                    dve.wait_ge(starts_ready, 1)
                    link(nc.vector.tensor_scalar(nb[:, 4:5], nb[:, 0:1], 0.5, None, ALU.mult))
                    floor_of(nb[:, 0:1], nb[:, 4:5], nbi[:, :], nb[:, 2:3])
                    link(nc.vector.scalar_tensor_tensor(out=ends[:, 1:2], in0=nb[:, 3:4], scalar=float(P),
                                                        in1=nb[:, 0:1], op0=ALU.mult, op1=ALU.subtract))
                    link(nc.vector.scalar_tensor_tensor(out=ends[:, 0:1], in0=ps[0:B, 7, 64:65], scalar=float(P),
                                                        in1=nb[:, 0:1], op0=ALU.mult, op1=ALU.add))
                    dve.engine_nop().then_inc(ends_ready, 1)
                    dve.wait_ge(ends_on_pe, 1)
                    link(nc.vector.tensor_scalar(nb[:, 4:5], ps[0:B, 7, 65:66], float(P), None, ALU.mult))
                    link(nc.vector.tensor_tensor(nb[:, 4:5], nb[:, 4:5], ps[0:B, 7, 66:67], ALU.subtract))
                    link(nc.vector.tensor_tensor(nb[:, 4:5], nb[:, 4:5], ends[:, 1:2], ALU.subtract))
                    link(nc.vector.tensor_tensor(ends[:, 2:3], nb[:, 4:5], spares[:, :], ALU.add))
                    dve.engine_nop().then_inc(ends_ready, 1)
                    dve.wait_ge(ends_on_pe, 2)
                    link(nc.vector.tensor_copy(ends_bc[:, :, :], ps[:, 6, 0:3 * P].rearrange("p (k b) -> p k b", b=P)[:, :, 0:B]))
                    link(nc.vector.tensor_scalar(spare[:, :], ends_bc[:, 1, :], order[:, 0:1], None, ALU.is_le))
                    link(nc.vector.tensor_tensor(pad_f[:, :], ends_bc[:, 2, :], ends_bc[:, 0, :], ALU.subtract))
                    link(nc.vector.tensor_tensor(pad_f[:, :], pad_f[:, :], spare[:, :], ALU.mult))
                    link(nc.vector.tensor_tensor(pad_f[:, :], pad_f[:, :], ends_bc[:, 0, :], ALU.add))
                    nc.vector.tensor_scalar(pad_to[:, :], pad_f[:, :], order[:, 0:1], None, ALU.add).then_inc(pads_placed, 1)
                    link(nc.vector.tensor_scalar(nb[:, 0:1], ps[0:B, 7, 64:65], float(UNIT * P), None, ALU.mult))
                    link(nc.vector.tensor_copy(span[:, 0:B], ps[0:K, 7, 128:128 + B]))
                    link(nc.vector.tensor_copy(span[:, P:P + B], ps[0:K, 7, 256:256 + B]))
                    link(nc.vector.tensor_scalar(f1[0:B, :], f1[0:B, :], nb[:, 0:1], None, ALU.add))
                    link(nc.vector.tensor_scalar(f0[0:B, :], f1[0:B, :], 1.0 / 2048, None, ALU.mult))
                    link(nc.vector.tensor_copy(srci[0:B, :], f0[0:B, :]))
                    link(nc.vector.tensor_copy(f2[0:B, :], srci[0:B, :]))
                    link(nc.vector.tensor_tensor(f0[0:B, :], f2[0:B, :], f0[0:B, :], ALU.is_gt))
                    link(nc.vector.tensor_tensor(f2[0:B, :], f2[0:B, :], f0[0:B, :], ALU.subtract))
                    link(nc.vector.tensor_scalar(base_hi[:, :], f2[0:B, :], 2048.0, None, ALU.mult))
                    link(nc.vector.scalar_tensor_tensor(out=base_lo[:, :], in0=f2[0:B, :], scalar=-2048.0,
                                                        in1=f1[0:B, :], op0=ALU.mult, op1=ALU.add))

            place = ExitStack()
            with place:
                sbp, semp = alloc(place)
                eq = sbp("eq2", [P, 4, 512], BF16)
                pos = sbp("pos", [P, C], F32)
                behind = sbp("behind", [K, CH * GU, B], F32)
                rec = sbp("rec", [P, 2, STEP, REC], F32)
                in48 = sbp("in48", [P, 2, STEP, HID], F32)
                in8 = sbp("in8", [P, 2, STEP, 8], F32)
                ind = sbp("ind", [P, 2, STEP], I32)
                to = sbp("to", [P, 2, STEP], U32)
                w1s = sbp("w1s", [HID + 1, 2, HID], F32)
                attr_t = sbp("attr_t", [HID + 1, 2, BATCH * P], F32)
                rest = sbp("rest", [P, 2, 2, BATCH, HID], F32)
                eq_ready, table_ready, copied = semp("eq_ready2"), semp("table_ready"), semp("copied")
                w1_in, attr_one = semp("w1_in"), semp("attr_one")
                in_sem = [semp(f"edges_in{s}") for s in range(2)]
                rec_ready = semp("rec_ready")
                attr_on_pe, attr_ready, hid_on_pe = semp("attr_on_pe"), semp("attr_ready"), semp("hid_on_pe")
                h1_ready, rest_ready, h2_ready, h3_ready = semp("h1_ready"), semp("rest_ready"), semp("h2_ready"), semp("h3_ready")
                scattered = [semp(f"scattered{s}", True) for s in range(2)]
                behind_ready = semp("behind_ready")
                pool_turn, dve_turn, pe_turn = semp("pool_turn"), semp("dve_turn"), semp("pe_turn2")
                steps = C // STEP
                per = STEP // BATCH
                block = place.enter_context(nc.Block())

                ea48_v = ea48.rearrange("(p c) f -> p c f", p=P)
                ea8_v = ea8.rearrange("(p c) f -> p c f", p=P)
                dst_v = dst.rearrange("(p c) -> p c", p=P)

                def parts(s, k, layer, part):
                    at = PART0[layer] + part * HID
                    return rec[:, s, k * BATCH:(k + 1) * BATCH, :].bitcast(BF16)[:, :, at:at + HID]

                def first(pair, s, k=0):
                    return isinstance(pair, int) and pair == 0 and s == 0 and k < 2

                def attr_ps(half):
                    return ps[0:HID, 2 * half:2 * half + 2, :].rearrange("k b e -> k (b e)")[:, 0:BATCH * P]

                def hid_ps(half, layer):
                    return ps[:, 4 + half, 0:BATCH * 2 * HID].rearrange("p (t l f) -> p t l f", l=2, f=HID)[:, :, layer, :]

                def edge_steps(eng, step, chunk=None):
                    done = 0
                    for n, w in enumerate(chunks):
                        if chunk:
                            chunk(n)
                        pairs = w // STEP // 2
                        lone = 1 if done == 0 else 0
                        if lone:
                            for s in range(2):
                                step(0, s, n, 0)
                        if pairs - lone == 1:
                            for s in range(2):
                                step(done + lone, s, n, lone)
                        elif pairs > lone:
                            with eng.Fori(done + lone, done + pairs) as pair:
                                for s in range(2):
                                    step(pair, s, n, pair - done)
                        done += pairs
                        if w // STEP % 2:
                            step(done, 0, n, 0)

                def ahead(n, within, s, k):
                    if n + 1 >= len(chunks):
                        return []
                    each = B * STEP // chunks[n]
                    assert each * chunks[n] == B * STEP
                    return [((2 * within + s) * each + q, (s * each + q) % 2)
                            for q in range(each * k // per, each * (k + 1) // per)]

                @block.sync
                def _(sp):
                    sp.wait_ge(attr_one, 1)
                    for layer in range(2):
                        sp.dma_start(w1s[0:HID, layer, :], w1[layer]).then_inc(w1_in, 16)
                        sp.dma_start(w1s[HID:HID + 1, layer, :], b1[layer]).then_inc(w1_in, 16)

                    def step(pair, s, n, within):
                        st = 2 * pair + s
                        if not (isinstance(pair, int) and pair == 0):
                            sp.wait_ge(attr_ready, (st - 1) * per)
                        cols = bass.ds(st * STEP, STEP)
                        sp.dma_start(in48[:, s], ea48_v[:, cols, :]).then_inc(in_sem[s], 16)
                        sp.dma_start(in8[:, s], ea8_v[:, cols, :]).then_inc(in_sem[s], 16)
                        sp.dma_start(ind[:, s], dst_v[:, cols]).then_inc(in_sem[s], 16)
                    edge_steps(sp, step)

                @block.scalar
                def _(act):
                    def step(pair, s, n, within):
                        st = 2 * pair + s
                        act.wait_ge(in_sem[s], 48 * (pair + 1))
                        if not (isinstance(pair, int) and pair == 0):
                            act.wait_ge(scattered[s], 16 * STEP * pair)
                        cols = bass.ds(st * STEP, STEP)
                        small = rec[:, s, :, SMALL:SMALL + CMP]
                        nc.scalar.activation(small[:, :, C_EA8:C_EA8 + 8], in8[:, s], ACT.Copy)
                        nc.scalar.activation(small[:, :, C_RHAT:C_RHAT + 3], rhat[:, cols, :], ACT.Copy)
                        nc.scalar.activation(small[:, :, C_NLO], loc[:, cols], ACT.Copy, scale=-1.0)
                        nc.scalar.activation(small[:, :, C_DST], ind[:, s], ACT.Copy)
                        nc.scalar.activation(to[:, s], pos[:, cols], ACT.Copy).then_inc(rec_ready, 1)

                        def attributes(k):
                            m, half = st * per + k, (s + k) % 2
                            act.wait_ge(attr_on_pe, m + 1)
                            if not first(pair, s, k):
                                act.wait_ge(hid_on_pe, m - 1)
                            nc.scalar.activation(attr_t[0:HID, half, :], attr_ps(half), ACT.Copy)\
                              .then_inc(attr_ready, 1)

                        attributes(0)
                        for k in range(per):
                            m, half = st * per + k, (s + k) % 2
                            if k + 1 < per:
                                attributes(k + 1)
                            act.wait_ge(hid_on_pe, m + 1)
                            for layer in range(2):
                                last = nc.scalar.activation(parts(s, k, layer, 1), hid_ps(half, layer), ACT.Relu)
                            last.then_inc(h1_ready, 1)
                    edge_steps(act, step, lambda n: act.wait_ge(copied, (n + 1) * B))

                @block.gpsimd
                def _(pool):
                    rec_rows = rec_d.rearrange("g u p (j f) -> (g u p j) f", f=REC)

                    for b in range(pads_early, B):
                        write_pads(b)
                    pool.wait_ge(pads_out, 16 * B)
                    pool.sem_inc(pool_turn, 1)

                    def step(pair, s, n, within):
                        pool.wait_ge(rec_ready, 2 * pair + s + 1)
                        pool.wait_ge(h3_ready, (2 * pair + s + 1) * per)
                        pool.sem_inc(pool_turn, 1)
                        for k in range(STEP):
                            nc.gpsimd.indirect_dma_start(
                                out=rec_rows, out_offset=bass.IndirectOffsetOnAxis(ap=to[:, s, k:k + 1], axis=0),
                                in_=rec[:, s, k, :], in_offset=None).then_inc(scattered[s], 16)
                    edge_steps(pool, step)
                    pool.wait_ge(scattered[0], 16 * STEP * ((steps + 1) // 2))
                    pool.wait_ge(scattered[1], 16 * STEP * (steps // 2))
                    pool.sem_inc(pool_turn, 1)

                @block.tensor
                def _(pe):
                    def position(n, b, s):
                        c, w = sum(chunks[:n]), chunks[n]
                        pe.wait_ge(eq_ready, b + 1 + n * (B + 1))
                        pe.sem_inc(pe_turn, 1)
                        nc.tensor.matmul(ps[:, 6 + s, 0:w], tri_b[:, :], eq[:, s, 0:w], start=True, stop=False)
                        sel = spread[:, bass.ds(b, 1), :].rearrange("k o p -> k (o p)")
                        nc.tensor.matmul(ps[:, 6 + s, 0:w], sel, base_hi[:, c:c + w], start=False, stop=False)
                        nc.tensor.matmul(ps[:, 6 + s, 0:w], sel, base_lo[:, c:c + w], start=False,
                                         stop=True).then_inc(table_ready, 1)

                    with pe.Fori(0, B // 2) as i:
                        for s in range(2):
                            position(0, 2 * i + s, s)
                    pe.wait_ge(w1_in, 64)

                    def attributes(pair, s, k):
                        m, half = (2 * pair + s) * per + k, (s + k) % 2
                        if k == 0:
                            pe.wait_ge(in_sem[s], 48 * (pair + 1))
                        if not first(pair, s, k):
                            pe.wait_ge(attr_ready, m - 1)
                        pe.sem_inc(pe_turn, 1)
                        for t in range(BATCH):
                            last = nc.tensor.transpose(attr_ps(half)[:, t * P:(t + 1) * P],
                                                       in48[:, s, k * BATCH + t, :], ident[:, :])
                        last.then_inc(attr_on_pe, 1)

                    def step(pair, s, n, within):
                        attributes(pair, s, 0)
                        for k in range(per):
                            m, half = (2 * pair + s) * per + k, (s + k) % 2
                            if k + 1 < per:
                                attributes(pair, s, k + 1)
                            for b, slot in ahead(n, within, s, k):
                                position(n + 1, b, slot)
                            pe.wait_ge(attr_ready, m + 1)
                            if not first(pair, s, k):
                                pe.wait_ge(rest_ready, m - 1)
                            for t in range(BATCH):
                                last = nc.tensor.matmul(ps[:, 4 + half, t * 2 * HID:(t + 1) * 2 * HID],
                                                        attr_t[:, half, t * P:(t + 1) * P],
                                                        w1s[:, :, :].rearrange("k l f -> k (l f)"), start=True, stop=True)
                            last.then_inc(hid_on_pe, 1)
                    edge_steps(pe, step)

                @block.vector
                def _(dve):
                    nc.vector.memset(attr_t[:, :, :], 1.0).then_inc(attr_one, 1)
                    def compare(n, b, s):
                        c, w = sum(chunks[:n]), chunks[n]
                        nc.vector.tensor_scalar(eq[:, s, 0:w], bucket[:, c:c + w], iota_b[:, bass.ds(b, 1)], None,
                                                ALU.is_equal).then_inc(eq_ready, 1)

                    def position(n, b, s):
                        c, w = sum(chunks[:n]), chunks[n]
                        dve.wait_ge(copied, b + n * B)
                        compare(n, b + 1, 1 - s)
                        dve.wait_ge(table_ready, b + 1 + n * B)
                        dve.sem_inc(dve_turn, 1)
                        nc.vector.copy_predicated(pos[:, c:c + w], eq[:, s, 0:w].bitcast(U16),
                                                  ps[:, 6 + s, 0:w]).then_inc(copied, 1)

                    def chunk(n):
                        if n + 1 < len(chunks):
                            dve.wait_ge(copied, (n + 1) * B)
                            compare(n + 1, 0, 0)
                        else:
                            Q = CH * GU
                            units_of = unit_no[:, :].unsqueeze(2).to_broadcast([K, Q, B])
                            nc.vector.tensor_tensor(owner[:, :, :], units_of, span[:, 0:B].unsqueeze(1).to_broadcast([K, Q, B]),
                                                    ALU.is_ge)
                            nc.vector.tensor_tensor(behind[:, :, :], span[:, P:P + B].unsqueeze(1).to_broadcast([K, Q, B]), units_of,
                                                    ALU.is_gt).then_inc(behind_ready, 1)
                            dve.wait_ge(behind_ready, 1)
                            nc.vector.tensor_tensor(owner[:, :, :], owner[:, :, :], behind[:, :, :], ALU.mult)

                    compare(0, 0, 0)
                    with dve.Fori(0, B // 2) as i:
                        for s in range(2):
                            position(0, 2 * i + s, s)

                    def step(pair, s, n, within):
                        for k in range(per):
                            m, half = (2 * pair + s) * per + k, (s + k) % 2
                            for b, slot in ahead(n, within, s, k):
                                position(n + 1, b, slot)
                            dve.wait_ge(h1_ready, m + 1)
                            for layer in range(2):
                                last = nc.vector.scalar_tensor_tensor(
                                    out=rest[:, half, layer], in0=hid_ps(half, layer), scalar=0.0,
                                    in1=parts(s, k, layer, 1), op0=ALU.max, op1=ALU.subtract)
                            last.then_inc(rest_ready, 1)
                            dve.wait_ge(rest_ready, m + 1)
                            for layer in range(2):
                                last = nc.vector.tensor_copy(parts(s, k, layer, 0), rest[:, half, layer])
                            last.then_inc(h2_ready, 1)
                            dve.wait_ge(h2_ready, m + 1)
                            for layer in range(2):
                                last = nc.vector.tensor_tensor(parts(s, k, layer, 2), rest[:, half, layer],
                                                               parts(s, k, layer, 0), ALU.subtract)
                            last.then_inc(h3_ready, 1)
                    edge_steps(dve, step, chunk)
        clear_spent()
        sh = Kept()
        sh.N, sh.B, sh.G, sh.K, sh.CH, sh.alloc, sh.ps, sh.owner = N, B, G, K, CH, alloc, ps, owner
        sh.ones, sh.ident, sh.iota_p, sh.iota_n, sh.rcount, sh.rows_sb = ones, ident, iota_p, iota_n, rcount, rows_sb
        sh.x_sb, sh.h_sb, sh.ln_before, sh.ln_behind, sh.rec_d, sh.cmp_d = x_sb, h_sb, ln_before, ln_behind, rec_d, cmp_d
        sh.ident_b = ident_b
        conv_pass(nc, sh, 0, w2_0, tab0_d, sum0_d)
        nodes_0(nc, sh, sum0_d, tab1_d)
        clear_spent()
        conv_pass(nc, sh, 1, w2_1, tab1_d, sum1_d)
        clear_spent()
        nodes_1(nc, sh, sum1_d, w_msg, tab2_d)
        pass_2(nc, sh, tab2_d, sum2_d)
        nodes_2(nc, sh, sum2_d, w_lin_t, w_upd, w_out, out)


def reduce_units(nc, sh, sum_d, F, tot, tag, sbp, semp):
    K, CH, B, ps = sh.K, sh.CH, sh.B, sh.ps
    lc = 1 << ((512 // F).bit_length() - 1)
    banks = P // lc
    part = sbp(f"part{tag}", [K, 2, P, GU, F], F32)
    part_in = [semp(f"part_in{tag}{s}") for s in range(2)]
    part_used, tot_ready = semp(f"part_used{tag}"), semp(f"tot_ready{tag}")

    def sync(sp):
        for c in range(CH):
            if c >= 2:
                sp.wait_ge(part_used, c - 1)
            sp.dma_start(part[:, c % 2].rearrange("k l u f -> k (l u f)"),
                         sum_d[c * K:(c + 1) * K].rearrange("k l x -> k (l x)"), max_dma_last_dim=16384)\
              .then_inc(part_in[c % 2], 16)

    def tensor(pe):
        for c in range(CH):
            pe.wait_ge(part_in[c % 2], 16 * (c // 2 + 1))
            for u in range(GU):
                for j in range(banks):
                    last = nc.tensor.matmul(ps[0:B, j, 0:lc * F], sh.owner[:, c * GU + u, :],
                                            part[:, c % 2, j * lc:(j + 1) * lc, u, :],
                                            start=(c == 0 and u == 0), stop=(c == CH - 1 and u == GU - 1))
            last.then_inc(part_used, 1)
        pe.wait_ge(tot_ready, 1)

    def scalar(act):
        act.wait_ge(part_used, CH)
        for j in range(banks):
            last = nc.scalar.activation(tot[:, j * lc:(j + 1) * lc, :], ps[0:B, j, 0:lc * F]
                                        .rearrange("b (l f) -> b l f", f=F), ACT.Copy)
        last.then_inc(tot_ready, 1)
    return sync, tensor, scalar, tot_ready


class Linker:

    def __init__(self, dve, sem):
        self.dve, self.sem, self.n = dve, sem, 0

    def __call__(self, ins):
        self.n += 1
        ins.then_inc(self.sem, 1)
        self.dve.wait_ge(self.sem, self.n)


def nodes_0(nc, sh, sum_d, tab_d):
    B, N, ps, ones, rows = sh.B, sh.N, sh.ps, sh.ones, sh.rows_sb
    L = LOCAL
    scope = ExitStack()
    with scope:
        sbp, semp = sh.alloc(scope)
        tot = sbp("tot0", [B, P, F0], F32)
        val = sbp("val0", [B, L, T0], F32)
        sq = sbp("sq0", [B, L, T0], F32)
        m = sbp("m0", [B, 8, NS], F32)
        sync, tensor, scalar, tot_ready = reduce_units(nc, sh, sum_d, F0, tot, 0, sbp, semp)
        link_s, asked, answered = semp("nlink0"), semp("asked0"), semp("answered0")
        root_asked, root_ready, val_ready, tab_out = semp("root_asked0"), semp("root_ready0"), semp("val_ready0"), semp("tab_out0")
        block = scope.enter_context(nc.Block())

        @block.sync
        def _(sp):
            sync(sp)
            sp.wait_ge(val_ready, 1)
            sp.dma_start(tab_d.rearrange("(b l) f -> b l f", l=L), val[:, :, :]).then_inc(tab_out, 16)
            sp.wait_ge(tab_out, 16)

        @block.tensor
        def _(pe):
            tensor(pe)
            for k, row in enumerate((0, 1, 2)):
                pe.wait_ge(asked, k + 1)
                nc.tensor.matmul(ps[0:B, 0, k * NS:(k + 1) * NS], ones[0:B, 0:B], m[:, row, :], start=True,
                                 stop=True).then_inc(answered, 1)

        @block.scalar
        def _(act):
            scalar(act)
            for k in range(2):
                act.wait_ge(root_asked, k + 1)
                nc.scalar.activation(m[:, 4 + k, :], m[:, 4 + k, :], ACT.Sqrt).then_inc(root_ready, 1)

        @block.vector
        def _(dve):
            link = Linker(dve, link_s)
            over_l = lambda a: a.rearrange("b l f -> b f l")
            bc = lambda row, w=NS: m[:, row, 0:w].unsqueeze(1).to_broadcast([B, L, w])
            dve.wait_ge(tot_ready, 1)
            link(nc.vector.tensor_scalar(sh.rcount[:, :], tot[:, 0:L, F0 - 1], 1.0, None, ALU.max))
            link(nc.vector.reciprocal(sh.rcount[:, :], sh.rcount[:, :]))
            link(nc.vector.tensor_tensor(val[:, :, :], tot[:, 0:L, 0:T0],
                                         sh.rcount[:, :].unsqueeze(2).to_broadcast([B, L, T0]), ALU.mult))
            link(nc.vector.tensor_scalar(val[:, :, 0:NS], val[:, :, 0:NS], float(NS) ** -0.5, None, ALU.mult))
            link(nc.vector.tensor_scalar(val[:, :, NS:T0], val[:, :, NS:T0], (3.0 / NS) ** 0.5, None, ALU.mult))
            link(nc.vector.tensor_reduce(m[:, 0, :], over_l(val[:, :, 0:NS]), AX.X, ALU.add))
            dve.engine_nop().then_inc(asked, 1)
            link(nc.vector.tensor_tensor(sq[:, :, NS:T0], val[:, :, NS:T0], val[:, :, NS:T0], ALU.mult))
            link(nc.vector.memset(m[:, 2, :], 0.0))
            link(nc.vector.tensor_reduce(m[:, 7, 0:12], over_l(sq[:, :, NS:T0]), AX.X, ALU.add))
            link(nc.vector.tensor_reduce(m[:, 2, 0:NV], m[:, 7, 0:12].rearrange("b (j c) -> b j c", c=3), AX.X, ALU.add))
            dve.wait_ge(answered, 1)
            link(nc.vector.tensor_scalar(m[:, 3, :], ps[0:B, 0, 0:NS], 1.0 / N, None, ALU.mult))
            link(nc.vector.tensor_tensor(val[:, :, 0:NS], val[:, :, 0:NS], bc(3), ALU.subtract))
            link(nc.vector.tensor_tensor(sq[:, :, 0:NS], val[:, :, 0:NS], val[:, :, 0:NS], ALU.mult))
            link(nc.vector.tensor_reduce(m[:, 1, :], over_l(sq[:, :, 0:NS]), AX.X, ALU.add))
            dve.engine_nop().then_inc(asked, 2)
            dve.wait_ge(answered, 3)
            link(nc.vector.tensor_scalar(m[:, 4, :], ps[0:B, 0, NS:2 * NS], 1.0 / N, EPS, ALU.mult, ALU.add))
            link(nc.vector.tensor_scalar(m[:, 5, :], ps[0:B, 0, 2 * NS:3 * NS], 1.0 / (3 * N), EPS, ALU.mult, ALU.add))
            dve.engine_nop().then_inc(root_asked, 2)
            dve.wait_ge(root_ready, 2)
            link(nc.vector.reciprocal(m[:, 4:6, :], m[:, 4:6, :]))
            link(nc.vector.tensor_tensor(m[:, 4, :], m[:, 4, :], rows[:, 0:NS], ALU.mult))
            link(nc.vector.tensor_tensor(m[:, 5, 0:NV], m[:, 5, 0:NV], rows[:, 2 * NS:2 * NS + NV], ALU.mult))
            link(nc.vector.tensor_copy(m[:, 6, 0:12].rearrange("b (j c) -> b j c", c=3),
                                       m[:, 5, 0:NV].unsqueeze(2).to_broadcast([B, NV, 3])))
            link(nc.vector.tensor_tensor(val[:, :, 0:NS], val[:, :, 0:NS], bc(4), ALU.mult))
            link(nc.vector.tensor_tensor(val[:, :, 0:NS], val[:, :, 0:NS],
                                         rows[:, NS:2 * NS].unsqueeze(1).to_broadcast([B, L, NS]), ALU.add))
            link(nc.vector.tensor_tensor(val[:, :, NS:T0], val[:, :, NS:T0], bc(6, 12), ALU.mult))
            dve.engine_nop().then_inc(val_ready, 1)


def conv_pass(nc, sh, layer, w2, tab_d, sum_d):
    G, ps, iota_p = sh.G, sh.ps, sh.iota_p
    width = NS if layer == 0 else T0
    I, J = (NS, 20) if layer == 0 else (20, NS)
    F = F0 if layer == 0 else NS
    M = 4 + F0 if layer == 0 else NS
    scope = ExitStack()
    with scope:
        sbp, semp = sh.alloc(scope)
        tag = f"_c{layer}"
        recs = sbp("recs" + tag, [P, RING, GROUP, READ], F32)
        comp = sbp("comp" + tag, [P, RING, GROUP, CMP], F32)
        at = sbp("at" + tag, [P, RING, GROUP], I32)
        xs = sbp("xs" + tag, [P, RING, GROUP, width], F32)
        hid = sbp("hid" + tag, [2 * HID + 1, 2, GROUP, 2, P], BF16)
        w32 = sbp("w32" + tag, [2 * HID + 1, 320], F32)
        w_rest = sbp("w_rest" + tag, [2 * HID + 1, 2, 320], F32)
        w_part = sbp("w_part" + tag, [2 * HID + 1, 3, 320], BF16)
        prod = sbp("prod" + tag, [P, 2, 2, J, I], F32)
        vr = sbp("vr" + tag, [P, GROUP, NV, 3], F32)
        msg = sbp("msg" + tag, [P, 2, GROUP, M], F32)
        away = sbp("away" + tag, [P, 2, GROUP, P], F32)
        owns = sbp("owns" + tag, [P, 2, GROUP, P], F32)
        sums = sbp("sums" + tag, [P, RING, GU, F], F32)
        rec_in = [semp(f"rec_in{k}{tag}") for k in range(RING)]
        xs_in = [semp(f"xs_in{k}{tag}", True) for k in range(RING)]
        comp_out = [semp(f"comp_out{k}{tag}") for k in range(RING)]
        sums_out = [semp(f"sums_out{k}{tag}") for k in range(RING)]
        w_in, w_link, w_ready, ones_set = semp("w_in" + tag), semp("w_link" + tag), semp("w_ready" + tag), semp("ones_set" + tag)
        hid_on_pe, hid_ready = semp("hid_on_pe" + tag), semp("hid_ready" + tag)
        comp_ready, at_ready = semp("comp_ready" + tag), semp("at_ready" + tag)
        weights_ready, prod_ready, reduced = semp("weights_ready" + tag), semp("prod_ready" + tag), semp("reduced" + tag)
        away_ready, owns_ready, msg_ready = semp("away_ready" + tag), semp("owns_ready" + tag), semp("msg_ready" + tag)
        summed, sums_ready, vr_ready, xs_ready = semp("summed" + tag), semp("sums_ready" + tag), semp("vr_ready" + tag), semp("xs_ready" + tag)
        pool_turn, pe_turn = semp("pool_turn" + tag), semp("pe_turn" + tag)
        block = scope.enter_context(nc.Block())

        @block.sync
        def _(sp):
            sp.dma_start(w32[0:HID, :], w2[0:HID, :]).then_inc(w_in, 16)
            sp.dma_start(w32[HID:2 * HID + 1, :], w2).then_inc(w_in, 16)
            sp.wait_ge(w_link, 5)
            sp.dma_start(w_part[HID:2 * HID, 2, :], w_part[HID:2 * HID, 0, :]).then_inc(w_ready, 16)

            def step(n):
                if exists(n, 5, G):
                    slot = moved(n, 5)[1]
                    if exists(n, 1, G):
                        sp.wait_ge(hid_on_pe, count(n, 1))
                        sp.wait_ge(at_ready, count(n, 1))
                    of_group = sh.rec_d[bass.ds(index(n, 5), 1)].rearrange("o u p (j f) -> u p (o j) f", f=REC)
                    for u in range(GU):
                        sp.dma_start(recs[:, slot, u * UNIT:(u + 1) * UNIT, :],
                                     of_group[u, :, :, layer * SMALL:layer * SMALL + READ]).then_inc(rec_in[slot], 16)
                if layer == 0 and exists(n, 2, G):
                    slot = moved(n, 2)[1]
                    sp.wait_ge(comp_ready, count(n, 2))
                    sp.dma_start(sh.cmp_d[bass.ds(index(n, 2), 1)].rearrange("o p x -> p (o x)"),
                                 comp[:, slot].rearrange("p t f -> p (t f)")).then_inc(comp_out[slot], 16)
                if exists(n, -3, G):
                    slot = moved(n, -3)[1]
                    sp.wait_ge(sums_ready, count(n, -3))
                    sp.dma_start(sum_d[bass.ds(index(n, -3), 1)].rearrange("o p x -> p (o x)"),
                                 sums[:, slot].rearrange("p u f -> p (u f)")).then_inc(sums_out[slot], 16)
            walk(sp, step, G)
            for k in range(RING):
                if layer == 0:
                    sp.wait_ge(comp_out[k], 16 * (G // RING))
                sp.wait_ge(sums_out[k], 16 * (G // RING))

        @block.gpsimd
        def _(pool):
            def step(n):
                if exists(n, 3, G):
                    slot = moved(n, 3)[1]
                    pool.wait_ge(at_ready, count(n, 3))
                    if exists(n, -1, G):
                        pool.wait_ge(prod_ready, count(n, -1, 2))
                    pool.sem_inc(pool_turn, 1)
                    for t in range(GROUP):
                        nc.gpsimd.indirect_dma_start(
                            out=xs[:, slot, t, :], out_offset=None, in_=tab_d,
                            in_offset=bass.IndirectOffsetOnAxis(ap=at[:, slot, t:t + 1], axis=0))\
                          .then_inc(xs_in[slot], 16)
            walk(pool, step, G)

        @block.scalar
        def _(act):
            act.wait_ge(ones_set, 1)

            def step(n):
                if exists(n, 3, G):
                    slot = moved(n, 3)[1]
                    act.wait_ge(rec_in[slot], used(n, 3, 16 * GU))
                    if exists(n, -1, G):
                        act.wait_ge(msg_ready, count(n, -1))
                        if layer == 0:
                            act.wait_ge(comp_out[slot], used(n, -1))
                    fields = recs[:, slot, :, (1 - layer) * SMALL:(1 - layer) * SMALL + CMP]
                    nc.scalar.activation(comp[:, slot], fields, ACT.Copy).then_inc(comp_ready, 1)
                    if exists(n, -1, G):
                        act.wait_ge(xs_in[slot], used(n, -1, 16 * GROUP))
                    nc.scalar.activation(at[:, slot], fields[:, :, C_DST], ACT.Copy).then_inc(at_ready, 1)
                if exists(n, 1, G):
                    half = (n[1] + 1) % 2
                    act.wait_ge(hid_on_pe, count(n, 1))
                    if exists(n, -1, G):
                        act.wait_ge(weights_ready, count(n, -1, 2))
                    nc.scalar.activation(hid[0:2 * HID, half].rearrange("k t w e -> k (t w e)"),
                                         ps[0:2 * HID, half, :].bitcast(BF16), ACT.Copy).then_inc(hid_ready, 1)
                if exists(n, 0, G):
                    half = n[1] % 2
                    act.wait_ge(comp_ready, count(n))
                    for t in range(GROUP):
                        last = nc.scalar.activation(away[:, half, t, :], iota_p[:, :], ACT.Square,
                                                    bias=comp[:, n[1], t, C_NLO:C_NLO + 1])
                    last.then_inc(away_ready, 1)
                if exists(n, -2, G):
                    slot = moved(n, -2)[1]
                    act.wait_ge(summed, count(n, -2))
                    if exists(n, -6, G):
                        act.wait_ge(sums_out[slot], used(n, -6))
                    nc.scalar.activation(sums[:, slot], ps[:, 6 + slot % 2, 0:GU * F]
                                         .rearrange("p (u f) -> p u f", f=F), ACT.Copy).then_inc(sums_ready, 1)
                if exists(n, 0, G):
                    half = n[1] % 2
                    act.wait_ge(away_ready, count(n))
                    nc.scalar.activation(owns[:, half], away[:, half], ACT.Relu, bias=1.0, scale=-1.0)\
                      .then_inc(owns_ready, 1)
            walk(act, step, G)

        @block.tensor
        def _(pe):
            pe.wait_ge(w_link, 5)
            pe.wait_ge(w_ready, 16)

            def step(n):
                if exists(n, 1, G):
                    slot, half = moved(n, 1)[1], (n[1] + 1) % 2
                    pe.wait_ge(rec_in[slot], used(n, 1, 16 * GU))
                    if exists(n, -1, G):
                        pe.wait_ge(hid_ready, count(n, -1))
                    pe.sem_inc(pe_turn, 1)
                    for t in range(GROUP):
                        start = layer * 2 * CMP
                        for w in range(2):
                            last = nc.tensor.transpose(
                                ps[0:2 * HID, half, :].bitcast(BF16)[:, (2 * t + w) * P:(2 * t + w + 1) * P],
                                recs[:, slot, t, :].bitcast(BF16)[:, start + w * HID:start + (w + 2) * HID],
                                sh.ident_b[:, :])
                    last.then_inc(hid_on_pe, 1)
                if exists(n, 0, G):
                    pe.wait_ge(hid_ready, count(n))
                    for q in range(2):
                        if exists(n, -1, G):
                            pe.wait_ge(prod_ready, count(n, -1, 2) - 1 + q)
                        for t in (2 * q, 2 * q + 1):
                            for part in range(3):
                                last = nc.tensor.matmul(ps[:, 2 + t, 0:320], hid[:, n[1] % 2, t, part // 2, :],
                                                        w_part[:, part, :], start=(part == 0), stop=(part == 2))
                        last.then_inc(weights_ready, 1)
                if exists(n, -1, G):
                    half = (n[1] + 1) % 2
                    pe.wait_ge(msg_ready, count(n, -1))
                    pe.wait_ge(owns_ready, count(n, -1))
                    if exists(n, -3, G):
                        pe.wait_ge(sums_ready, count(n, -3))
                    for u in range(GU):
                        for j in range(UNIT):
                            t = u * UNIT + j
                            last = nc.tensor.matmul(ps[:, 6 + half, u * F:(u + 1) * F], owns[:, half, t, :],
                                                    msg[:, half, t, M - F:], start=(j == 0), stop=(j == UNIT - 1))
                    last.then_inc(summed, 1)
            walk(pe, step, G)

        @block.vector
        def _(dve):
            nc.vector.memset(hid[:, :, :, :, :], 1.0)
            nc.vector.memset(msg[:, :, :, :], 1.0).then_inc(ones_set, 1)
            link = Linker(dve, w_link)
            dve.wait_ge(w_in, 32)
            link(nc.vector.tensor_copy(w_part[:, 0, :], w32[:, :]))
            link(nc.vector.tensor_tensor(w_rest[:, 0, :], w32[:, :], w_part[:, 0, :], ALU.subtract))
            link(nc.vector.tensor_copy(w_part[:, 1, :], w_rest[:, 0, :]))
            link(nc.vector.tensor_tensor(w_rest[:, 1, :], w_rest[:, 0, :], w_part[:, 1, :], ALU.subtract))
            link(nc.vector.tensor_copy(w_part[:, 2, :], w_rest[:, 1, :]))

            def step(n):
                if not exists(n, 0, G):
                    return
                slot, half = n[1], n[1] % 2
                direction = comp[:, slot, :, C_RHAT:C_RHAT + 3].unsqueeze(2).to_broadcast([P, GROUP, NV, 3])
                dve.wait_ge(xs_in[slot], used(n, 0, 16 * GROUP))
                if layer == 1:
                    dve.wait_ge(comp_ready, count(n))
                    nc.vector.tensor_tensor(vr[:, :, :, :], xs[:, slot, :, NS:T0].rearrange("p t (i c) -> p t i c", c=3),
                                            direction, ALU.mult).then_inc(vr_ready, 1)
                    dve.wait_ge(vr_ready, count(n))
                    nc.vector.tensor_reduce(xs[:, slot, :, NS:NS + NV], vr[:, :, :, :], AX.X, ALU.add)\
                      .then_inc(xs_ready, 1)
                    dve.wait_ge(xs_ready, count(n))
                for q in range(2):
                    dve.wait_ge(weights_ready, count(n, 0, 2) - 1 + q)
                    nc.vector.tensor_tensor(
                        prod[:, q], ps[:, 2 + 2 * q:4 + 2 * q, 0:320].rearrange("p t (j i) -> p t j i", i=I),
                        xs[:, slot, 2 * q:2 * q + 2, 0:I].unsqueeze(2).to_broadcast([P, 2, J, I]),
                        ALU.mult).then_inc(prod_ready, 1)
                if exists(n, -2, G):
                    dve.wait_ge(summed, count(n, -2))
                for q in range(2):
                    dve.wait_ge(prod_ready, count(n, 0, 2) - 1 + q)
                    last = nc.vector.tensor_reduce(msg[:, half, 2 * q:2 * q + 2, 0:J], prod[:, q], AX.X, ALU.add)
                if layer == 1:
                    last.then_inc(msg_ready, 1)
                    return
                last.then_inc(reduced, 1)
                dve.wait_ge(reduced, count(n))
                dve.wait_ge(comp_ready, count(n))
                nc.vector.tensor_tensor(
                    msg[:, half, :, 20:32].rearrange("p t (j c) -> p t j c", c=3),
                    msg[:, half, :, 0:NV].unsqueeze(3).to_broadcast([P, GROUP, NV, 3]), direction,
                    ALU.mult).then_inc(msg_ready, 1)
            walk(dve, step, G)


def block_diagonal(sp, dst, src, blocks, width, done):
    for k in range(blocks):
        sp.dma_start(dst[k * NS:(k + 1) * NS, k * width:(k + 1) * width], src).then_inc(done, 16)


NB = 5


def nodes_1(nc, sh, sum_d, w_msg, tab_d):
    B, N, ps, ones, rows = sh.B, sh.N, sh.ps, sh.ones, sh.rows_sb
    L = LOCAL
    steps = L // NB
    scope = ExitStack()
    with scope:
        sbp, semp = sh.alloc(scope)
        tot = sbp("tot1", [B, P, NS], F32)
        val = sbp("val1", [B, L, NS], F32)
        sq = sbp("sq1", [B, L, NS], F32)
        m = sbp("m1", [B, 8, NS], F32)
        lnv = sbp("lnv1", [B, L], F32)
        wd = sbp("wd", [NB * NS, NB * P], F32)
        h_t = sbp("h_t", [NB * NS, 2, B], F32)
        tab = sbp("tab", [B, 4, NB * P], F32)
        sync, tensor, scalar, tot_ready = reduce_units(nc, sh, sum_d, NS, tot, 1, sbp, semp)
        link_s, asked, answered = semp("nlink1"), semp("asked1"), semp("answered1")
        root_asked, root_ready, h_ready = semp("root_asked1"), semp("root_ready1"), semp("h_ready1")
        wd_zero, wd_in, h_on_pe, h_t_ready = semp("wd_zero"), semp("wd_in"), semp("h_on_pe"), semp("h_t_ready")
        rows_on_pe, tab_ready = semp("rows_on_pe"), semp("tab_ready")
        tab_out = [semp(f"tab_out1{s}") for s in range(4)]
        block = scope.enter_context(nc.Block())

        @block.gpsimd
        def _(pool):
            nc.gpsimd.memset(wd[:, :], 0.0).then_inc(wd_zero, 1)

        @block.sync
        def _(sp):
            sync(sp)
            sp.wait_ge(wd_zero, 1)
            block_diagonal(sp, wd, w_msg, NB, P, wd_in)
            tab_v = tab_d.rearrange("(b l) f -> b l f", l=L)
            for k in range(steps):
                sp.wait_ge(tab_ready, k + 1)
                sp.dma_start(tab_v[:, k * NB:(k + 1) * NB, :].rearrange("b l f -> b (l f)"), tab[:, k % 4, :])\
                  .then_inc(tab_out[k % 4], 16)
            for s in range(4):
                sp.wait_ge(tab_out[s], 16 * len(range(s, steps, 4)))

        @block.tensor
        def _(pe):
            tensor(pe)
            for k in range(2):
                pe.wait_ge(asked, k + 1)
                nc.tensor.matmul(ps[0:B, 0, k * NS:(k + 1) * NS], ones[0:B, 0:B], m[:, k, :], start=True,
                                 stop=True).then_inc(answered, 1)
            pe.wait_ge(h_ready, 1)
            pe.wait_ge(wd_in, 16 * NB)

            def turn(k):
                if k >= 2:
                    pe.wait_ge(h_t_ready, k - 1)
                nc.tensor.transpose(ps[0:NB * NS, 1 + k % 2, 0:B],
                                    sh.h_sb[:, k * NB:(k + 1) * NB, :].rearrange("b l f -> b (l f)"),
                                    sh.ident[0:B, 0:B]).then_inc(h_on_pe, 1)
            turn(0)
            for k in range(steps):
                if k + 1 < steps:
                    turn(k + 1)
                pe.wait_ge(h_t_ready, k + 1)
                if k >= 2:
                    pe.wait_ge(tab_ready, k - 1)
                for s in range(2):
                    half = NB * P // 2
                    last = nc.tensor.matmul(ps[0:B, 4 + 2 * (k % 2) + s, 0:half], h_t[:, k % 2, :],
                                            wd[:, s * half:(s + 1) * half], start=True, stop=True)
                last.then_inc(rows_on_pe, 1)

        @block.scalar
        def _(act):
            scalar(act)
            act.wait_ge(root_asked, 1)
            nc.scalar.activation(m[:, 4, :], m[:, 4, :], ACT.Sqrt).then_inc(root_ready, 1)
            act.wait_ge(root_asked, 2)
            nc.scalar.activation(lnv[:, :], lnv[:, :], ACT.Sqrt).then_inc(root_ready, 1)
            for k in range(steps):
                act.wait_ge(rows_on_pe, k + 1)
                if k >= 4:
                    act.wait_ge(tab_out[k % 4], 16 * (k // 4))
                half = NB * P // 2
                nc.scalar.activation(tab[:, k % 4, :].rearrange("b (s x) -> b s x", s=2),
                                     ps[0:B, 4 + 2 * (k % 2):6 + 2 * (k % 2), 0:half], ACT.Copy).then_inc(tab_ready, 1)

        @block.vector
        def _(dve):
            link = Linker(dve, link_s)
            over_l = lambda a: a.rearrange("b l f -> b f l")
            bc = lambda row: m[:, row, :].unsqueeze(1).to_broadcast([B, L, NS])
            dve.wait_ge(tot_ready, 1)
            link(nc.vector.tensor_tensor(val[:, :, :], tot[:, 0:L, :],
                                         sh.rcount[:, :].unsqueeze(2).to_broadcast([B, L, NS]), ALU.mult))
            link(nc.vector.tensor_scalar(val[:, :, :], val[:, :, :], float(NS + NV) ** -0.5, None, ALU.mult))
            link(nc.vector.tensor_reduce(m[:, 0, :], over_l(val[:, :, :]), AX.X, ALU.add))
            dve.engine_nop().then_inc(asked, 1)
            dve.wait_ge(answered, 1)
            link(nc.vector.tensor_scalar(m[:, 3, :], ps[0:B, 0, 0:NS], 1.0 / N, None, ALU.mult))
            link(nc.vector.tensor_tensor(val[:, :, :], val[:, :, :], bc(3), ALU.subtract))
            link(nc.vector.tensor_tensor(sq[:, :, :], val[:, :, :], val[:, :, :], ALU.mult))
            link(nc.vector.tensor_reduce(m[:, 1, :], over_l(sq[:, :, :]), AX.X, ALU.add))
            dve.engine_nop().then_inc(asked, 1)
            dve.wait_ge(answered, 2)
            link(nc.vector.tensor_scalar(m[:, 4, :], ps[0:B, 0, NS:2 * NS], 1.0 / N, EPS, ALU.mult, ALU.add))
            dve.engine_nop().then_inc(root_asked, 1)
            dve.wait_ge(root_ready, 1)
            link(nc.vector.reciprocal(m[:, 4, :], m[:, 4, :]))
            g0 = 2 * NS + NV
            link(nc.vector.tensor_tensor(m[:, 4, :], m[:, 4, :], rows[:, g0:g0 + NS], ALU.mult))
            link(nc.vector.tensor_tensor(val[:, :, :], val[:, :, :], bc(4), ALU.mult))
            link(nc.vector.tensor_tensor(val[:, :, :], val[:, :, :],
                                         rows[:, g0 + NS:g0 + 2 * NS].unsqueeze(1).to_broadcast([B, L, NS]), ALU.add))
            link(nc.vector.tensor_tensor(sh.x_sb[:, :, :], sh.x_sb[:, :, :], val[:, :, :], ALU.add))
            sh.ln_before(link, sh.x_sb, sh.h_sb, lnv, sq, root_asked)
            dve.wait_ge(root_ready, 2)
            sh.ln_behind(link, sh.h_sb, lnv)
            dve.engine_nop().then_inc(h_ready, 1)
            for k in range(steps):
                dve.wait_ge(h_on_pe, k + 1)
                if k >= 2:
                    dve.wait_ge(rows_on_pe, k - 1)
                nc.vector.tensor_copy(h_t[:, k % 2, :], ps[0:NB * NS, 1 + k % 2, 0:B]).then_inc(h_t_ready, 1)


def pass_2(nc, sh, tab_d, sum_d):
    G, ps = sh.G, sh.ps
    scope = ExitStack()
    with scope:
        sbp, semp = sh.alloc(scope)
        comp = sbp("comp2", [P, RING, GROUP, CMP], F32)
        at = sbp("at2", [P, RING, GROUP], I32)
        ys = sbp("ys", [P, RING, GROUP, NS * 8], F32)
        prod = sbp("prod2", [P, 2, GROUP, NS, 8], F32)
        pre = sbp("pre2", [P, 2, GROUP, NS], F32)
        msg = sbp("msg2", [P, 2, GROUP, NS], F32)
        owns = sbp("owns2", [P, 2, GROUP, P], F32)
        sums = sbp("sums2_sb", [P, RING, GU, NS], F32)
        comp_in = [semp(f"comp_in2{k}") for k in range(RING)]
        ys_in = [semp(f"ys_in{k}", True) for k in range(RING)]
        sums_out = [semp(f"sums_out2{k}") for k in range(RING)]
        at_ready, prod_ready, pre_ready, msg_ready = semp("at_ready2"), semp("prod_ready2"), semp("pre_ready2"), semp("msg_ready2")
        owns_ready, summed, sums_ready, pool_turn = semp("owns_ready2"), semp("summed2"), semp("sums_ready2"), semp("pool_turn2")
        block = scope.enter_context(nc.Block())

        @block.sync
        def _(sp):
            def step(n):
                if exists(n, 5, G):
                    slot = moved(n, 5)[1]
                    if exists(n, 1, G):
                        sp.wait_ge(at_ready, count(n, 1))
                        sp.wait_ge(prod_ready, count(n, 1))
                        sp.wait_ge(owns_ready, count(n, 1))
                    sp.dma_start(comp[:, slot].rearrange("p t f -> p (t f)"),
                                 sh.cmp_d[bass.ds(index(n, 5), 1)].rearrange("o p x -> p (o x)"))\
                      .then_inc(comp_in[slot], 16)
                if exists(n, -1, G):
                    slot = moved(n, -1)[1]
                    sp.wait_ge(sums_ready, count(n, -1))
                    sp.dma_start(sum_d[bass.ds(index(n, -1), 1)].rearrange("o p x -> p (o x)"),
                                 sums[:, slot].rearrange("p u f -> p (u f)")).then_inc(sums_out[slot], 16)
            walk(sp, step, G)
            for k in range(RING):
                sp.wait_ge(sums_out[k], 16 * (G // RING))

        @block.gpsimd
        def _(pool):
            def step(n):
                if exists(n, 3, G):
                    slot = moved(n, 3)[1]
                    pool.wait_ge(at_ready, count(n, 3))
                    if exists(n, -1, G):
                        pool.wait_ge(prod_ready, count(n, -1))
                    pool.sem_inc(pool_turn, 1)
                    for t in range(GROUP):
                        nc.gpsimd.indirect_dma_start(
                            out=ys[:, slot, t, :], out_offset=None, in_=tab_d,
                            in_offset=bass.IndirectOffsetOnAxis(ap=at[:, slot, t:t + 1], axis=0))\
                          .then_inc(ys_in[slot], 16)
            walk(pool, step, G)

        @block.scalar
        def _(act):
            def step(n):
                if exists(n, 3, G):
                    slot = moved(n, 3)[1]
                    act.wait_ge(comp_in[slot], used(n, 3))
                    if exists(n, -1, G):
                        act.wait_ge(ys_in[slot], used(n, -1, 16 * GROUP))
                    nc.scalar.activation(at[:, slot], comp[:, slot, :, C_DST], ACT.Copy).then_inc(at_ready, 1)
                if exists(n, -1, G):
                    half = (n[1] + 1) % 2
                    act.wait_ge(pre_ready, count(n, -1))
                    if exists(n, -3, G):
                        act.wait_ge(summed, count(n, -3))
                    nc.scalar.activation(msg[:, half], pre[:, half], ACT.Silu, scale=float(NS * 8) ** -0.5)\
                      .then_inc(msg_ready, 1)
                if exists(n, -3, G):
                    slot = moved(n, -3)[1]
                    act.wait_ge(summed, count(n, -3))
                    if exists(n, -7, G):
                        act.wait_ge(sums_out[slot], used(n, -7))
                    nc.scalar.activation(sums[:, slot], ps[:, 6 + slot % 2, 0:GU * NS]
                                         .rearrange("p (u f) -> p u f", f=NS), ACT.Copy).then_inc(sums_ready, 1)
            walk(act, step, G)

        @block.tensor
        def _(pe):
            def step(n):
                if exists(n, -1, G):
                    half = (n[1] + 1) % 2
                    pe.wait_ge(msg_ready, count(n, -1))
                    pe.wait_ge(owns_ready, count(n, -1))
                    if exists(n, -3, G):
                        pe.wait_ge(sums_ready, count(n, -3))
                    for u in range(GU):
                        for j in range(UNIT):
                            t = u * UNIT + j
                            last = nc.tensor.matmul(ps[:, 6 + half, u * NS:(u + 1) * NS], owns[:, half, t, :],
                                                    msg[:, half, t, :], start=(j == 0), stop=(j == UNIT - 1))
                    last.then_inc(summed, 1)
            walk(pe, step, G)

        @block.vector
        def _(dve):
            def step(n):
                if not exists(n, 0, G):
                    return
                slot, half = n[1], n[1] % 2
                dve.wait_ge(ys_in[slot], used(n, 0, 16 * GROUP))
                dve.wait_ge(comp_in[slot], used(n))
                nc.vector.tensor_tensor(prod[:, half], ys[:, slot].rearrange("p t (h j) -> p t h j", j=8),
                                        comp[:, slot, :, C_EA8:C_EA8 + 8].unsqueeze(2).to_broadcast([P, GROUP, NS, 8]),
                                        ALU.mult).then_inc(prod_ready, 1)
                dve.wait_ge(prod_ready, count(n))
                if exists(n, -2, G):
                    dve.wait_ge(msg_ready, count(n, -2))
                nc.vector.tensor_reduce(pre[:, half], prod[:, half], AX.X, ALU.add).then_inc(pre_ready, 1)
                if exists(n, -2, G):
                    dve.wait_ge(summed, count(n, -2))
                for t in range(GROUP):
                    last = nc.vector.tensor_scalar(owns[:, half, t, :], sh.iota_n[:, :],
                                                   comp[:, slot, t, C_NLO:C_NLO + 1], None, ALU.is_equal)
                last.then_inc(owns_ready, 1)
            walk(dve, step, G)


def nodes_2(nc, sh, sum_d, w_lin_t, w_upd, w_out, out):
    B, ps = sh.B, sh.ps
    L = LOCAL
    steps = L // NB
    W = NB * NS
    scope = ExitStack()
    with scope:
        sbp, semp = sh.alloc(scope)
        tot = sbp("tot2", [B, P, NS], F32)
        lin_d = sbp("lin_d", [W, W], F32)
        upd_d = sbp("upd_d", [W, NB * 256], F32)
        both_d = sbp("both_d", [W, NB * 256], F32)
        out_d = sbp("out_d", [W, W], F32)
        a_t = sbp("a_t", [W, 2, B], F32)
        hv = sbp("hv", [B, 2, NB * 256], F32)
        u = sbp("u", [B, L, NS], F32)
        su = sbp("su", [B, L, NS], F32)
        sync, tensor, scalar, tot_ready = reduce_units(nc, sh, sum_d, NS, tot, 2, sbp, semp)
        zero, w_in, both_on_pe, both_ready = semp("zero2"), semp("w_in2"), semp("both_on_pe"), semp("both_ready")
        a_on_pe, a_t_ready, v_on_pe, hv_ready = semp("a_on_pe"), semp("a_t_ready"), semp("v_on_pe"), semp("hv_ready")
        u_ready, su_ready, s_on_pe, s_t_ready = semp("u_ready"), semp("su_ready"), semp("s_on_pe"), semp("s_t_ready")
        o_on_pe, x_ready, out_done, xh_ready = semp("o_on_pe"), semp("x_ready"), semp("out_done"), semp("xh_ready")
        block = scope.enter_context(nc.Block())
        v_cuts = [(0, 2), (2, 4), (4, 5)]

        @block.gpsimd
        def _(pool):
            for t in (lin_d, upd_d, out_d):
                nc.gpsimd.memset(t[:, :], 0.0).then_inc(zero, 1)

        @block.sync
        def _(sp):
            sync(sp)
            sp.wait_ge(zero, 3)
            block_diagonal(sp, lin_d, w_lin_t, NB, NS, w_in)
            block_diagonal(sp, upd_d, w_upd, NB, 256, w_in)
            block_diagonal(sp, out_d, w_out, NB, NS, w_in)
            sp.wait_ge(x_ready, steps)
            sp.dma_start(out.rearrange("(b l) f -> b l f", l=L), sh.x_sb[:, :, :]).then_inc(out_done, 16)
            sp.wait_ge(out_done, 16)

        @block.tensor
        def _(pe):
            tensor(pe)
            pe.wait_ge(w_in, 16 * 3 * NB)
            for c, (a, b) in enumerate(v_cuts):
                last = nc.tensor.matmul(ps[0:W, c, 0:(b - a) * 256], lin_d[:, :], upd_d[:, a * 256:b * 256],
                                        start=True, stop=True)
            last.then_inc(both_on_pe, 1)
            pe.wait_ge(both_ready, 1)
            for k in range(steps):
                l0 = slice(k * NB, (k + 1) * NB)
                if k >= 1:
                    pe.wait_ge(a_t_ready, k)
                nc.tensor.transpose(ps[0:W, 7, 0:B], tot[:, l0, :].rearrange("b l f -> b (l f)"),
                                    sh.ident[0:B, 0:B]).then_inc(a_on_pe, 1)
                pe.wait_ge(a_t_ready, k + 1)
                if k >= 2:
                    pe.wait_ge(hv_ready, k - 1)
                for c, (a, b) in enumerate(v_cuts):
                    last = nc.tensor.matmul(ps[0:B, 3 * (k % 2) + c, 0:(b - a) * 256], a_t[:, k % 2, :],
                                            both_d[:, a * 256:b * 256], start=True, stop=True)
                last.then_inc(v_on_pe, 1)
            pe.wait_ge(su_ready, 1)
            for k in range(steps):
                l0 = slice(k * NB, (k + 1) * NB)
                if k >= 2:
                    pe.wait_ge(s_t_ready, k - 1)
                nc.tensor.transpose(ps[0:W, k % 2, 0:B], su[:, l0, :].rearrange("b l f -> b (l f)"),
                                    sh.ident[0:B, 0:B]).then_inc(s_on_pe, 1)
                pe.wait_ge(s_t_ready, k + 1)
                if k >= 2:
                    pe.wait_ge(x_ready, k - 1)
                nc.tensor.matmul(ps[0:B, 2 + k % 2, 0:W], a_t[:, k % 2, :], out_d[:, :], start=True,
                                 stop=True).then_inc(o_on_pe, 1)

        @block.scalar
        def _(act):
            scalar(act)
            act.wait_ge(both_on_pe, 1)
            for c, (a, b) in enumerate(v_cuts):
                last = nc.scalar.activation(both_d[:, a * 256:b * 256], ps[0:W, c, 0:(b - a) * 256], ACT.Copy)
            last.then_inc(both_ready, 1)
            for k in range(steps):
                act.wait_ge(a_on_pe, k + 1)
                if k >= 2:
                    act.wait_ge(v_on_pe, k - 1)
                nc.scalar.activation(a_t[:, k % 2, :], ps[0:W, 7, 0:B], ACT.Copy).then_inc(a_t_ready, 1)
            act.wait_ge(u_ready, steps)
            nc.scalar.activation(su[:, :, :], u[:, :, :], ACT.Silu, scale=(NS * NS * NS) ** -0.5).then_inc(su_ready, 1)
            for k in range(steps):
                act.wait_ge(s_on_pe, k + 1)
                if k >= 2:
                    act.wait_ge(o_on_pe, k - 1)
                nc.scalar.activation(a_t[:, k % 2, :], ps[0:W, k % 2, 0:B], ACT.Copy).then_inc(s_t_ready, 1)

        @block.vector
        def _(dve):
            nc.vector.tensor_tensor(sh.x_sb[:, :, :], sh.x_sb[:, :, :], sh.h_sb[:, :, :], ALU.add).then_inc(xh_ready, 1)
            for k in range(steps):
                dve.wait_ge(v_on_pe, k + 1)
                for c, (a, b) in enumerate(v_cuts):
                    h_of = sh.h_sb[:, k * NB + a:k * NB + b, :].unsqueeze(2).to_broadcast([B, b - a, NS, NS])
                    last = nc.vector.tensor_tensor(
                        hv[:, k % 2, a * 256:b * 256].rearrange("b (l k i) -> b l k i", k=NS, i=NS),
                        ps[0:B, 3 * (k % 2) + c, 0:(b - a) * 256].rearrange("b (l k i) -> b l k i", k=NS, i=NS),
                        h_of, ALU.mult)
                last.then_inc(hv_ready, 1)
                dve.wait_ge(hv_ready, k + 1)
                nc.vector.tensor_reduce(u[:, k * NB:(k + 1) * NB, :], hv[:, k % 2, :]
                                        .rearrange("b (l k i) -> b l k i", k=NS, i=NS), AX.X, ALU.add).then_inc(u_ready, 1)
            dve.wait_ge(xh_ready, 1)
            for k in range(steps):
                dve.wait_ge(o_on_pe, k + 1)
                x_of = sh.x_sb[:, k * NB:(k + 1) * NB, :].rearrange("b l f -> b (l f)")
                nc.vector.scalar_tensor_tensor(out=x_of, in0=ps[0:B, 2 + k % 2, 0:W], scalar=float(NS) ** -0.5,
                                               in1=x_of, op0=ALU.mult, op1=ALU.add).then_inc(x_ready, 1)


_INS = ["x", "src", "dst", "ea3", "ea48", "ea8", "w1", "b1", "w2_0", "w2_1", "rows", "w_msg", "w_lin_t", "w_upd", "w_out"]


def lay_out(i):
    f = lambda n: np.ascontiguousarray(i[n])
    g = "L0_gnn_"

    def second(k):
        w, b = f(f"{g}fc{k}_w2"), f(f"{g}fc{k}_b2")
        w = np.concatenate([w, b[None, :]], 0)
        a, v = w[:, :NS * NS].reshape(-1, NS, NS), w[:, NS * NS:]
        if k == 0:
            v = v.reshape(-1, NS, NV)
            return np.ascontiguousarray(np.concatenate([v.transpose(0, 2, 1), a.transpose(0, 2, 1)], 1).reshape(-1, 320))
        v = v.reshape(-1, NV, NS)
        return np.ascontiguousarray(np.concatenate([a.transpose(0, 2, 1), v.transpose(0, 2, 1)], 2).reshape(-1, 320))

    rows = np.concatenate([f(g + n) for n in ("bn0_gs", "bn0_bs", "bn0_gv", "bn1_gs", "bn1_bs")])[None, :]
    return {
        "x": f("x"), "src": f("src"), "dst": f("dst"), "ea3": f("edge_attr_3"), "ea48": f("edge_attr_48"),
        "ea8": f("edge_attr_8"),
        "w1": np.stack([f(g + "fc0_w1"), f(g + "fc1_w1")]), "b1": np.stack([f(g + "fc0_b1"), f(g + "fc1_b1")])[:, None, :],
        "w2_0": second(0), "w2_1": second(1), "rows": np.ascontiguousarray(rows),
        "w_msg": np.ascontiguousarray(f("L1_gnn_W_msg_tp").transpose(0, 2, 1).reshape(NS, 128)),
        "w_lin_t": np.ascontiguousarray(f("L1_gnn_W_msg_lin").T),
        "w_upd": np.ascontiguousarray(f("L1_gnn_W_upd_tp").transpose(1, 2, 0).reshape(NS, 256)),
        "w_out": f("L1_gnn_W_upd_lin"),
    }


def kernel(**inputs):
    import numpy as _np
    import concourse.bacc as _bacc
    from concourse import mybir as _mybir
    from concourse.bass_utils import run_bass_kernel_spmd as _run

    nc = _bacc.Bacc("TRN2", target_bir_lowering=False, num_devices=1)
    given = lay_out({n: _np.asarray(a) for n, a in inputs.items()})
    arrays, args = {}, []
    for name in _INS:
        a = given[name]
        arrays[f"in_{name}"] = a
        args.append(nc.dram_tensor(f"in_{name}", a.shape, _mybir.dt.from_np(a.dtype), kind="ExternalInput").ap())
    out = nc.dram_tensor("out_0", given["x"].shape, _mybir.dt.float32, kind="ExternalOutput").ap()
    gnn(nc, *args, out)
    r = _run(nc, [arrays], core_ids=[0])
    return r.results[0]["out_0"]
```
